# Optimizing a Trainium2 kernel written in Bass

```python
import numpy as np
import jax
import jax.numpy as jnp

def _softmax(x, axis=-1):
    return jax.nn.softmax(x, axis=axis)

def _gelu(x):
    return jax.nn.gelu(x, approximate=True)

def _silu(x):
    return jax.nn.silu(x)

def _sigmoid(x):
    return jax.nn.sigmoid(x)

def _layernorm(x, axis=-1, eps=1e-05):
    m = jnp.mean(x, axis=axis, keepdims=True)
    v = jnp.var(x, axis=axis, keepdims=True)
    return (x - m) / jnp.sqrt(v + eps)

def _scatter_add(tgt, idx, src, axis=0):
    return tgt.at[idx].add(src)

def _segment_sum(src, seg, n):
    return jax.ops.segment_sum(src, seg, n)
kernel_name = 'mk_flamingo_gated_d2_seqx_r4_914268'

def setup_inputs(seed: int=0):
    np.random.seed(seed)
    _w = jnp.asarray

    def _rec_inputs():
        import jax
        import jax.numpy as jnp
        _rk = jax.random.key(seed)
        x = 0.0002417 + 0.9998 * jax.random.normal(jax.random.fold_in(_rk, 1), (8, 512, 256), jnp.float32)
        _lenS = 512 - jax.random.randint(jax.random.fold_in(_rk, 7), (8,), 0, max(1, 512 // 4) + 1, jnp.int32)
        _lenS2 = 1601 - jax.random.randint(jax.random.fold_in(_rk, 8), (8,), 0, max(1, 1601 // 4) + 1, jnp.int32)
        _ctx_1024P = jax.random.normal(jax.random.fold_in(_rk, 11), (8, 16, 256), jnp.float32)
        _ctx_1024c = jax.random.dirichlet(jax.random.fold_in(_rk, 511), 0.3 * jnp.ones((16,), jnp.float32), (8, 1601))
        _ctx_1024t = jnp.einsum('bsk,bkd->bsd', _ctx_1024c, _ctx_1024P)
        _ctx_1024t = _ctx_1024t * jax.lax.rsqrt(jnp.mean(jnp.square(_ctx_1024t)) + 1e-12) * 0.953939
        ctx_1024 = 7.22013e-05 + 1.00017 * (_ctx_1024t + 0.3 * jax.random.normal(jax.random.fold_in(_rk, 611), (8, 1601, 256), jnp.float32))
        _g = jax.random.normal(jax.random.fold_in(_rk, 9001), (2, 2), jnp.float32)
        _g = jnp.sign(_g) * jnp.maximum(jnp.abs(_g), 1.0) + (_g == 0) * 1.0
        g_xattn = _g[0]
        g_ffn = _g[1]
        return (x, ctx_1024, g_xattn, g_ffn)
    x, ctx_1024, g_xattn, g_ffn = _rec_inputs()

    def _L0_xattn_setup():
        import jax, jax.numpy as jnp
        import numpy as np
        EMBED_DIM = 256
        NUM_HEADS = 16
        HEAD_DIM = EMBED_DIM // NUM_HEADS
        key = jax.random.key(seed)
        ks = jax.random.split(key, 8)
        B, S, D = (4, 512, EMBED_DIM)
        scale = 1.0 / np.sqrt(D)
        return {'values': jax.random.normal(ks[0], (B, S, D), jnp.float32), 'keys': jax.random.normal(ks[1], (B, S, D), jnp.float32), 'query': jax.random.normal(ks[2], (B, S, D), jnp.float32), 'Wv': jax.random.normal(ks[3], (D, D), jnp.float32) * scale, 'Wk': jax.random.normal(ks[4], (D, D), jnp.float32) * scale, 'Wq': jax.random.normal(ks[5], (D, D), jnp.float32) * scale, 'Wo': jax.random.normal(ks[6], (D, D), jnp.float32) * scale, 'bo': jnp.zeros((D,), jnp.float32)}
    _L0_xattn_all = _L0_xattn_setup()
    _L0_xattn_in = {k: v for k, v in _L0_xattn_all.items() if k in ('Wv', 'Wk', 'Wq', 'Wo', 'bo')}
    del _L0_xattn_all

    def _L0_ffn_setup():
        import jax, jax.numpy as jnp
        import numpy as np
        NUM_EXPERTS = 4
        key = jax.random.key(seed)
        ks = jax.random.split(key, 8)
        B, L, H = (8, 512, 256)
        F = 4 * H
        s = 0.02
        x = jax.random.normal(ks[0], (B, L, H), dtype=jnp.float32)
        Wr = jax.random.normal(ks[1], (H, NUM_EXPERTS), dtype=jnp.float32) * s
        br = jnp.zeros((NUM_EXPERTS,), dtype=jnp.float32)
        We1 = jax.random.normal(ks[2], (NUM_EXPERTS, H, F), dtype=jnp.float32) * s
        be1 = jnp.zeros((NUM_EXPERTS, F), dtype=jnp.float32)
        We2 = jax.random.normal(ks[3], (NUM_EXPERTS, F, H), dtype=jnp.float32) * s
        be2 = jnp.zeros((NUM_EXPERTS, H), dtype=jnp.float32)
        return {'x': x, 'Wr': Wr, 'br': br, 'We1': We1, 'be1': be1, 'We2': We2, 'be2': be2}
    _L0_ffn_all = _L0_ffn_setup()
    _L0_ffn_in = {k: v for k, v in _L0_ffn_all.items() if k in ('Wr', 'br', 'We1', 'be1', 'We2', 'be2')}
    del _L0_ffn_all

    def _L1_xattn_setup():
        import jax, jax.numpy as jnp
        import numpy as np
        E = 256
        R = 16
        B = 4
        S = 512
        key = jax.random.key(seed)
        ks = jax.random.split(key, 12)
        inp = {'query': jax.random.normal(ks[0], (B, S, E), jnp.float32), 'key': jax.random.normal(ks[1], (B, S, E), jnp.float32), 'value': jax.random.normal(ks[2], (B, S, E), jnp.float32), 'Q_weight': jax.random.normal(ks[3], (E, E), jnp.float32) / np.sqrt(E), 'K_weight': jax.random.normal(ks[4], (E, E), jnp.float32) / np.sqrt(E), 'V_weight': jax.random.normal(ks[5], (E, E), jnp.float32) / np.sqrt(E), 'Q_A': 0.02 * jax.random.normal(ks[6], (R, E), jnp.float32), 'Q_B': 0.02 * jax.random.normal(ks[7], (E, R), jnp.float32), 'K_A': 0.02 * jax.random.normal(ks[8], (R, E), jnp.float32), 'K_B': 0.02 * jax.random.normal(ks[9], (E, R), jnp.float32), 'V_A': 0.02 * jax.random.normal(ks[10], (R, E), jnp.float32), 'V_B': 0.02 * jax.random.normal(ks[11], (E, R), jnp.float32), 'O_weight': jax.random.normal(jax.random.fold_in(key, 99), (E, E), jnp.float32) / np.sqrt(E)}
        return inp
    _L1_xattn_all = _L1_xattn_setup()
    _L1_xattn_in = {k: v for k, v in _L1_xattn_all.items() if k in ('Q_weight', 'K_weight', 'V_weight', 'Q_A', 'Q_B', 'K_A', 'K_B', 'V_A', 'V_B', 'O_weight')}
    del _L1_xattn_all

    def _L1_ffn_setup():
        import jax, jax.numpy as jnp
        import numpy as np
        TOPK = 8
        BN_EPS = 1e-05
        key = jax.random.key(seed)
        ks = jax.random.split(key, 5)
        b, n, d = (2, 256, 256)
        h, nk, kd = (8, 64, 128)
        ne = nk * nk
        scale = 0.02
        return {'inputs': jax.random.normal(ks[0], (b, n, d), jnp.float32), 'gamma': jnp.ones((d,), jnp.float32), 'beta': jnp.zeros((d,), jnp.float32), 'w_q': jax.random.normal(ks[1], (2 * h * kd, d), jnp.float32) * scale, 'keys': jax.random.normal(ks[2], (h, nk, 2, kd), jnp.float32) * scale, 'key_in': jax.random.normal(ks[3], (ne, d), jnp.float32) * scale, 'key_out': jax.random.normal(ks[4], (ne, d), jnp.float32) * scale}
    _L1_ffn_all = _L1_ffn_setup()
    _L1_ffn_in = {k: v for k, v in _L1_ffn_all.items() if k in ('gamma', 'beta', 'w_q', 'keys', 'key_in', 'key_out')}
    del _L1_ffn_all
    return {'x': x, 'ctx_1024': ctx_1024, 'g_xattn': g_xattn, 'g_ffn': g_ffn, 'L0_xattn_Wv': _L0_xattn_in['Wv'], 'L0_xattn_Wk': _L0_xattn_in['Wk'], 'L0_xattn_Wq': _L0_xattn_in['Wq'], 'L0_xattn_Wo': _L0_xattn_in['Wo'], 'L0_xattn_bo': _L0_xattn_in['bo'], 'L0_ffn_Wr': _L0_ffn_in['Wr'], 'L0_ffn_br': _L0_ffn_in['br'], 'L0_ffn_We1': _L0_ffn_in['We1'], 'L0_ffn_be1': _L0_ffn_in['be1'], 'L0_ffn_We2': _L0_ffn_in['We2'], 'L0_ffn_be2': _L0_ffn_in['be2'], 'L1_xattn_Q_weight': _L1_xattn_in['Q_weight'], 'L1_xattn_K_weight': _L1_xattn_in['K_weight'], 'L1_xattn_V_weight': _L1_xattn_in['V_weight'], 'L1_xattn_Q_A': _L1_xattn_in['Q_A'], 'L1_xattn_Q_B': _L1_xattn_in['Q_B'], 'L1_xattn_K_A': _L1_xattn_in['K_A'], 'L1_xattn_K_B': _L1_xattn_in['K_B'], 'L1_xattn_V_A': _L1_xattn_in['V_A'], 'L1_xattn_V_B': _L1_xattn_in['V_B'], 'L1_xattn_O_weight': _L1_xattn_in['O_weight'], 'L1_ffn_gamma': _L1_ffn_in['gamma'], 'L1_ffn_beta': _L1_ffn_in['beta'], 'L1_ffn_w_q': _L1_ffn_in['w_q'], 'L1_ffn_keys': _L1_ffn_in['keys'], 'L1_ffn_key_in': _L1_ffn_in['key_in'], 'L1_ffn_key_out': _L1_ffn_in['key_out']}

def reference(x, ctx_1024, g_xattn, g_ffn, L0_xattn_Wv, L0_xattn_Wk, L0_xattn_Wq, L0_xattn_Wo, L0_xattn_bo, L0_ffn_Wr, L0_ffn_br, L0_ffn_We1, L0_ffn_be1, L0_ffn_We2, L0_ffn_be2, L1_xattn_Q_weight, L1_xattn_K_weight, L1_xattn_V_weight, L1_xattn_Q_A, L1_xattn_Q_B, L1_xattn_K_A, L1_xattn_K_B, L1_xattn_V_A, L1_xattn_V_B, L1_xattn_O_weight, L1_ffn_gamma, L1_ffn_beta, L1_ffn_w_q, L1_ffn_keys, L1_ffn_key_in, L1_ffn_key_out):
    import jax
    import jax.numpy as jnp

    def _L0_xattn_ref(values, keys, query, Wv, Wk, Wq, Wo, bo):
        import jax, jax.numpy as jnp
        import numpy as np
        EMBED_DIM = 256
        NUM_HEADS = 16
        HEAD_DIM = EMBED_DIM // NUM_HEADS
        N = query.shape[0]
        H, Dh = (NUM_HEADS, HEAD_DIM)
        v = (values @ Wv.T).reshape(N, -1, H, Dh)
        k = (keys @ Wk.T).reshape(N, -1, H, Dh)
        q = (query @ Wq.T).reshape(N, -1, H, Dh)
        energy = jnp.einsum('nqhd,nkhd->nhqk', q, k)
        attn = jax.nn.softmax(energy / jnp.sqrt(jnp.float32(EMBED_DIM)), axis=3)
        out = jnp.einsum('nhql,nlhd->nqhd', attn, v).reshape(N, -1, H * Dh)
        return out @ Wo.T + bo

    def _L0_ffn_ref(x, Wr, br, We1, be1, We2, be2):
        import jax, jax.numpy as jnp
        import numpy as np
        NUM_EXPERTS = 4
        logits = jnp.einsum('blh,he->ble', x, Wr) + br
        top_expert = jnp.argmax(logits, axis=-1)
        mask = jax.nn.one_hot(top_expert, NUM_EXPERTS, dtype=x.dtype)
        out = jnp.zeros_like(x)
        for e in range(NUM_EXPERTS):
            h1 = jax.nn.relu(jnp.einsum('blh,hf->blf', x, We1[e]) + be1[e])
            oe = jnp.einsum('blf,fh->blh', h1, We2[e]) + be2[e]
            out = out + mask[..., e:e + 1] * oe
        return out

    def _L1_xattn_ref(query, key, value, Q_weight, K_weight, V_weight, Q_A, Q_B, K_A, K_B, V_A, V_B, O_weight):
        import jax, jax.numpy as jnp
        import numpy as np
        E = 256
        R = 16
        B = 4
        S = 512
        embed_dim = Q_weight.shape[0]
        Q = jnp.einsum('bse,fe->bsf', query, Q_weight) + jnp.einsum('bse,re->bsr', query, Q_A) @ Q_B.T
        K = jnp.einsum('bse,fe->bsf', key, K_weight) + jnp.einsum('bse,re->bsr', key, K_A) @ K_B.T
        V = jnp.einsum('bse,fe->bsf', value, V_weight) + jnp.einsum('bse,re->bsr', value, V_A) @ V_B.T
        scores = jnp.einsum('bqe,bke->bqk', Q, K) / jnp.sqrt(jnp.float32(embed_dim))
        attn = jax.nn.softmax(scores, axis=-1)
        out = jnp.einsum('bqk,bke->bqe', attn, V)
        return jnp.einsum('bse,fe->bsf', out, O_weight)

    def _L1_ffn_ref(inputs, gamma, beta, w_q, keys, key_in, key_out):
        import jax, jax.numpy as jnp
        import numpy as np
        TOPK = 8
        BN_EPS = 1e-05
        b, n, d = inputs.shape
        h, nk, _, kd = keys.shape
        k = TOPK
        x = inputs.reshape(b * n, d)
        mu = jnp.mean(x, axis=0)
        var = jnp.mean(jnp.square(x - mu), axis=0)
        xn = (x - mu) * jax.lax.rsqrt(var + BN_EPS) * gamma + beta
        q = (xn @ w_q.T).reshape(b, n, 2, h, kd).transpose(2, 0, 1, 3, 4)
        sim = jnp.einsum('pbnhd,hkpd->pbnhk', q, keys)
        s, i = jax.lax.top_k(sim, k)
        sx, sy = (s[0], s[1])
        ix, iy = (i[0], i[1])
        all_scores = (sx[..., :, None] + sy[..., None, :]).reshape(b, n, h, k * k)
        all_idx = (ix[..., :, None] * nk + iy[..., None, :]).reshape(b, n, h, k * k)
        scores, pk = jax.lax.top_k(all_scores, k)
        idx = jnp.take_along_axis(all_idx, pk, axis=-1)
        w_down = key_in[idx]
        w_up = key_out[idx]
        o = jnp.einsum('bnd,bnhkd->bnhk', inputs, w_down)
        o = jax.nn.gelu(o, approximate=False) * jax.nn.softmax(scores, axis=-1)
        return jnp.einsum('bnhk,bnhkd->bnd', o, w_up)
    x = x + jnp.tanh(g_xattn[0]) * _L0_xattn_ref(ctx_1024, ctx_1024, _layernorm(x, axis=-1), L0_xattn_Wv, L0_xattn_Wk, L0_xattn_Wq, L0_xattn_Wo, L0_xattn_bo)
    x = x + jnp.tanh(g_ffn[0]) * _L0_ffn_ref(_layernorm(x, axis=-1), L0_ffn_Wr, L0_ffn_br, L0_ffn_We1, L0_ffn_be1, L0_ffn_We2, L0_ffn_be2)
    x = x + jnp.tanh(g_xattn[1]) * _L1_xattn_ref(_layernorm(x, axis=-1), ctx_1024, ctx_1024, L1_xattn_Q_weight, L1_xattn_K_weight, L1_xattn_V_weight, L1_xattn_Q_A, L1_xattn_Q_B, L1_xattn_K_A, L1_xattn_K_B, L1_xattn_V_A, L1_xattn_V_B, L1_xattn_O_weight)
    x = x + jnp.tanh(g_ffn[1]) * _L1_ffn_ref(_layernorm(x, axis=-1), L1_ffn_gamma, L1_ffn_beta, L1_ffn_w_q, L1_ffn_keys, L1_ffn_key_in, L1_ffn_key_out)
    return x

_drawn_inputs = setup_inputs


def setup_inputs(seed=0):
    import zlib

    import numpy as np

    out = dict(_drawn_inputs(seed))
    spreads = {'g_ffn': (-1.0, 0.6),
     'L0_xattn_bo': (0.0, 0.1),
     'L0_ffn_br': (0.0, 0.1),
     'L0_ffn_be1': (0.0, 0.278),
     'L0_ffn_be2': (0.0, 0.1),
     'L1_ffn_gamma': (1.0, 0.6),
     'L1_ffn_beta': (0.0, 0.8)}
    factors = {'L1_xattn_Q_A': 8.0,
     'L1_xattn_Q_B': 8.0,
     'L1_xattn_K_A': 8.0,
     'L1_xattn_K_B': 8.0,
     'L1_xattn_V_A': 5.654,
     'L1_xattn_V_B': 5.213,
     'L1_ffn_w_q': 8.0,
     'L1_ffn_keys': 8.0,
     'L1_ffn_key_in': 8.0,
     'L1_ffn_key_out': 8.0}
    for name, (base, spread) in spreads.items():
        noise = np.random.default_rng([zlib.crc32(name.encode()), seed]).standard_normal(out[name].shape)
        drawn = base * np.exp(spread * noise) if base else spread * noise
        out[name] = jnp.asarray(drawn.astype(out[name].dtype))
    for name, factor in factors.items():
        out[name] = (out[name] * factor).astype(out[name].dtype)
    return out
```

```python
from contextlib import ExitStack

import concourse.bass as bass
from concourse import mybir

F32 = mybir.dt.float32
BF16 = mybir.dt.bfloat16
U32 = mybir.dt.uint32
ALU = mybir.AluOpType
ACT = mybir.ActivationFunctionType
AX = mybir.AxisListType

P = 128
B, S, D = 8, 512, 256
KEYS = 1601
KC = D // P
QT = S // P
NT = B * QT
KT = -(-KEYS // P)
H, DH = 16, 16
HG = 4
G = H // HG
LN_EPS = 1e-5


def key_rows(kt):
    return min(P, KEYS - kt * P)


def spans(total, width):
    return [(a, min(width, total - a)) for a in range(0, total, width)]


KEY_SPANS = spans(KEYS, 512)


class Own:

    def __init__(self, eng, sem, i=0, per=0):
        self.eng, self.sem, self.base, self.n = eng, sem, i * per, 0

    def then(self, ins):
        self.n += 1
        ins.then_inc(self.sem, 1)
        self.eng.wait_ge(self.sem, self.base + self.n)


def gate(eng, sem):
    eng.sem_inc(sem, 1)


class Stage:

    def __init__(self, nc, name):
        self.nc, self.name, self.ctx = nc, name, ExitStack()

    def __enter__(self):
        return self

    def __exit__(self, *exc):
        return self.ctx.__exit__(*exc)

    def sb(self, name, shape, dt=F32):
        return self.ctx.enter_context(self.nc.sbuf_tensor(f"{self.name}_{name}", shape, dt))

    def ps(self, name, shape, dt=F32):
        return self.ctx.enter_context(self.nc.psum_tensor(f"{self.name}_{name}", shape, dt))


def norm_tiles(nc, dve, own, x, out, stats, mv, ve, rstd, gates, var_ready, sd_ready, sd, done):
    gate(dve, gates)
    for q in range(QT):
        ins = nc.vector.bn_stats(stats[:, q, :], x(q))
    own.then(ins)
    gate(dve, gates)
    for q in range(QT):
        ins = nc.vector.bn_aggr(mv[:, q, :], stats[:, q, :])
    own.then(ins)
    nc.vector.tensor_scalar(ve[:, :], mv[:, :, 1], LN_EPS, None, ALU.add).then_inc(var_ready, 1)
    dve.wait_ge(*sd_ready)
    own.then(nc.vector.reciprocal(rstd[:, :], sd[:, :]))
    for q in range(QT):
        nc.vector.tensor_scalar(out(q), x(q), mv[:, q, 0:1], rstd[:, q:q + 1],
                                ALU.subtract, ALU.mult).then_inc(done, 1)


def project(nc, sem, t):
    PB = 2
    chunks = [("k", m, a, n) for m in range(KC) for a, n in KEY_SPANS] + [("q", m, 0, S) for m in range(KC)]
    NCH, RING = len(chunks), 4
    NKC = KC * len(KEY_SPANS)
    with Stage(nc, "pj") as st:
        ctx = st.sb("ctx", [P, PB, KC, KEYS])
        w = {n: st.sb(n, [P, KC, D]) for n in ("wq", "wk", "wv")}
        xn = st.sb("xn", [P, PB, QT, D])
        xnT = st.sb("xnT", [P, PB, KC, S])
        parts = {"k": st.sb("kp", [P, PB, 3, KC, KEYS], BF16), "q": st.sb("qp", [P, PB, 3, KC, S], BF16)}
        v = st.sb("v", [P, PB, G, KT, HG * DH])
        rest = st.sb("rest", [P, RING, 512])
        stats, mv = st.sb("stats", [P, QT, 6]), st.sb("mv", [P, QT, 2])
        ve, sd, rstd = st.sb("ve", [P, QT]), st.sb("sd", [P, QT]), st.sb("rstd", [P, QT])
        ps_t, ps_c, ps_v = st.ps("pst", [P, KC, 512]), st.ps("psc", [P, RING, 512]), st.ps("psv", [P, 2, 512])

        weights, ctx_in, ctx_used = sem("pj_weights"), [sem("pj_ctx0"), sem("pj_ctx1")], sem("pj_ctx_used")
        own, normed, var, sdr = sem("pj_dve_own"), sem("pj_normed"), sem("pj_var"), sem("pj_sd")
        turned, xnT_ready = sem("pj_turned"), sem("pj_xnT")
        mm, first, left, second, third = (sem(f"pj_{n}") for n in ("mm", "part1", "rest", "part2", "part3"))
        v_mm, v_out, stored = sem("pj_v_mm"), sem("pj_v_out"), [sem("pj_stored0"), sem("pj_stored1")]
        v_clear = sem("pj_v_clear")
        NSTORE = 3 + 3 + 1

        def out_of(parts_of, s, part, m, a, n):
            return parts[parts_of][:, s, part, m, a:a + n]

        with nc.Block() as block:
            @block.sync
            def _(sp):
                sp.dma_start(t["x"], t["x_in"]).then_inc(t["x_loaded"], 16)
                for n in ("wq", "wk", "wv"):
                    sp.dma_start(w[n][:, :, :], t[n + "_in"]).then_inc(weights, 16)
                for s in range(PB):
                    sp.sem_inc(stored[s], 1)
                    sp.dma_start(ctx[:, s, :, :], t["ctxT_in"][s]).then_inc(ctx_in[s], 16)

                def step(i, s, load):
                    b = i * PB + s
                    sp.wait_ge(third, (b + 1) * NCH)
                    sp.wait_ge(v_out, (b + 1) * KT + 2)
                    for part in range(3):
                        sp.dma_start(t["k_dram"][b, part].rearrange("(m p) n -> p m n", p=P),
                                     parts["k"][:, s, part, :, :]).then_inc(stored[s], 16)
                        sp.dma_start(t["q_dram"][b, part].rearrange("(m p) n -> p m n", p=P),
                                     parts["q"][:, s, part, :, :]).then_inc(stored[s], 16)
                    sp.dma_start(t["v_dram"][b].rearrange("g p n -> p g n"),
                                 v[:, s, :, :, :].rearrange("p g k c -> p g (k c)")).then_inc(stored[s], 16)
                    if load:
                        sp.wait_ge(ctx_used, b + 1)
                        sp.dma_start(ctx[:, s, :, :], t["ctxT_in"][b + PB]).then_inc(ctx_in[s], 16)

                with sp.Fori(0, B // PB - 1) as i:
                    for s in range(PB):
                        step(i, s, True)
                for s in range(PB):
                    step(B // PB - 1, s, False)
                for s in range(PB):
                    sp.wait_ge(stored[s], 1 + 16 * NSTORE * (B // PB))

            @block.tensor
            def _(pe):
                pe.wait_ge(weights, 48)
                pe.wait_ge(t["consts"], t["consts_n"])
                with pe.Fori(0, B // PB) as i:
                    for s in range(PB):
                        b = i * PB + s
                        pe.wait_ge(ctx_in[s], i * 16 + 16)
                        for c, (what, m, a, n) in enumerate(chunks[:NKC]):
                            pe.wait_ge(left, b * NCH + c + 1)
                            for k in range(KC):
                                ins = nc.tensor.matmul(ps_c[:, (NCH * s + c) % RING, 0:n], w["wk"][:, k, m * P:m * P + P],
                                                       ctx[:, s, k, a:a + n], start=k == 0, stop=k == KC - 1)
                            ins.then_inc(mm, 1)
                        for kt in range(KT):
                            r = key_rows(kt)
                            pe.wait_ge(v_out, b * KT + kt + 1)
                            for k in range(KC):
                                ins = nc.tensor.matmul(ps_v[0:r, (KT * s + kt) % 2, 0:D], ctx[:, s, k, kt * P:kt * P + r],
                                                       w["wv"][:, k, :], start=k == 0, stop=k == KC - 1)
                            ins.then_inc(v_mm, 1)
                        pe.wait_ge(v_mm, (b + 1) * KT)
                        pe.sem_inc(ctx_used, 1)
                        pe.wait_ge(normed, (b + 1) * QT)
                        pe.wait_ge(xnT_ready, b + 1)
                        for q in range(QT):
                            for k in range(KC):
                                ins = nc.tensor.transpose(ps_t[:, k, q * P:q * P + P],
                                                          xn[:, s, q, k * P:k * P + P], t["ident"][:, :])
                        ins.then_inc(turned, 1)
                        pe.wait_ge(xnT_ready, b + 2)
                        for c, (what, m, a, n) in list(enumerate(chunks))[NKC:]:
                            pe.wait_ge(left, b * NCH + c + 1)
                            for k in range(KC):
                                ins = nc.tensor.matmul(ps_c[:, (NCH * s + c) % RING, 0:n], w["wq"][:, k, m * P:m * P + P],
                                                       xnT[:, s, k, :], start=k == 0, stop=k == KC - 1)
                            ins.then_inc(mm, 1)

            @block.scalar
            def _(act):
                act.sem_inc(v_out, 2)
                act.wait_ge(v_clear, 1)
                with act.Fori(0, B // PB) as i:
                    for s in range(PB):
                        b = i * PB + s

                        def part1(c):
                            what, m, a, n = chunks[c]
                            act.wait_ge(mm, b * NCH + c + 1)
                            nc.scalar.activation(out_of(what, s, 0, m, a, n), ps_c[:, (NCH * s + c) % RING, 0:n],
                                                 ACT.Copy).then_inc(first, 1)

                        def part2(c):
                            what, m, a, n = chunks[c]
                            act.wait_ge(left, b * NCH + c + 1 + RING)
                            nc.scalar.activation(out_of(what, s, 1, m, a, n), rest[:, (NCH * s + c) % RING, 0:n],
                                                 ACT.Copy).then_inc(second, 1)

                        act.wait_ge(var, b + 1)
                        nc.scalar.activation(sd[:, :], ve[:, :], ACT.Sqrt).then_inc(sdr, 1)
                        act.wait_ge(stored[s], i * 16 * NSTORE + 1)
                        for c in range(NKC):
                            part1(c)
                            if c:
                                part2(c - 1)
                        part2(NKC - 1)
                        for kt in range(KT):
                            r = key_rows(kt)
                            act.wait_ge(v_mm, b * KT + kt + 1)
                            nc.scalar.activation(v[0:r, s, :, kt, :],
                                                 ps_v[0:r, (KT * s + kt) % 2, 0:D].rearrange("p (g c) -> p g c", g=G),
                                                 ACT.Copy).then_inc(v_out, 1)
                        for c in range(NKC, NCH):
                            part1(c)
                            if c > NKC:
                                part2(c - 1)
                        part2(NCH - 1)

            @block.vector
            def _(dve):
                nc.vector.memset(v[:, :, :, KT - 1, :], 0.0).then_inc(v_clear, 1)
                dve.sem_inc(left, RING)
                dve.sem_inc(xnT_ready, 1)
                dve.wait_ge(t["x_loaded"], 16)
                with dve.Fori(0, B // PB) as i:
                    for s in range(PB):
                        b = i * PB + s
                        me = Own(dve, own, b, 3)

                        def subtract1(c):
                            what, m, a, n = chunks[c]
                            dve.wait_ge(first, b * NCH + c + 1)
                            nc.vector.tensor_tensor(rest[:, (NCH * s + c) % RING, 0:n], ps_c[:, (NCH * s + c) % RING, 0:n],
                                                    out_of(what, s, 0, m, a, n), ALU.subtract).then_inc(left, 1)

                        def subtract2(c):
                            what, m, a, n = chunks[c]
                            dve.wait_ge(second, b * NCH + c + 1)
                            nc.vector.tensor_tensor(out_of(what, s, 2, m, a, n), rest[:, (NCH * s + c) % RING, 0:n],
                                                    out_of(what, s, 1, m, a, n), ALU.subtract).then_inc(third, 1)

                        norm_tiles(nc, dve, me, lambda q: t["x_tile"](b * QT + q), lambda q: xn[:, s, q, :],
                                   stats, mv, ve, rstd, t["dve_gate"], var, (sdr, b + 1), sd, normed)
                        for c in range(NKC):
                            subtract1(c)
                            if c:
                                subtract2(c - 1)
                        subtract2(NKC - 1)
                        dve.wait_ge(turned, b + 1)
                        nc.vector.tensor_copy(xnT[:, s, :, :], ps_t[:, :, :]).then_inc(xnT_ready, 1)
                        for c in range(NKC, NCH):
                            subtract1(c)
                            if c > NKC:
                                subtract2(c - 1)
                        subtract2(NCH - 1)


Q_PART = [0, 1, 0, 2, 0, 1]
K_PART = [0, 0, 1, 0, 2, 1]
TERMS = DH * len(Q_PART)
STACK = TERMS + 3


def attend_heads(nc, sem, t):
    SLOTS = G
    PRING, SBANKS, MBANKS = 8, 3, 2
    NST = KT * HG
    max_jobs = [(j, q, h) for j in range(HG) for q in range(QT) for h in range(2)]
    HALF = 1024
    SCALE = 1.0 / float(D) ** 0.5
    UNITS = B * G
    NLOAD = 2 * len(Q_PART) + 1
    with Stage(nc, "at") as st:
        ks, qs = st.sb("ks", [STACK, SLOTS, HG, KEYS], BF16), st.sb("qs", [STACK, SLOTS, HG, S], BF16)
        vd = st.sb("vd", [P, 2, KT * HG, DH])
        vw = st.sb("vw", [P, 2, KT * HG, 2 * DH])
        pr = st.sb("pr", [P, PRING, S])
        pmax, nmax = st.sb("pmax", [P, HG * QT, 2]), st.sb("nmax", [P, HG * QT])
        mrest, mpart = st.sb("mrest", [HG * QT, 2, P]), st.sb("mpart", [HG * QT, 3, P], BF16)
        acc, den, o = st.sb("acc", [P, S]), st.sb("den", [P, 2, S]), st.sb("o", [P, S])
        ps_s, ps_m, ps_o = st.ps("pss", [P, SBANKS, 512]), st.ps("psm", [P, MBANKS, HALF]), st.ps("pso", [P, 512])

        kq_in, v_in = [sem(f"at_kq{s}") for s in range(SLOTS)], [sem(f"at_v{s}") for s in range(2)]
        kq_used, v_used, v_wide = sem("at_kq_used"), sem("at_v_used"), sem("at_v_wide")
        v_dense_used, v_ones = sem("at_v_dense_used"), sem("at_v_ones")
        s_mm, expd, pv = sem("at_scores"), sem("at_exp"), sem("at_pv")
        m_mm, m_red, m_all, m_turned, m_parts, m_in = (sem(f"at_max_{n}") for n in ("mm", "red", "all", "turned", "parts", "in"))
        own, acc_out, o_ready, o_stored, ones = (sem(f"at_{n}") for n in ("own", "acc_out", "o_ready", "o_stored", "ones"))
        OWN = 6

        with nc.Block() as block:
            @block.sync
            def _(sp):
                def load(b, g):
                    u, v_slot = b * G + g, g % 2
                    sp.wait_ge(kq_used, u + 1)
                    for n, (kp, qp) in enumerate(zip(K_PART, Q_PART)):
                        rows = slice(g * HG * DH, (g + 1) * HG * DH)
                        sp.dma_start(ks[n * DH:(n + 1) * DH, g, :, :],
                                     t["k_dram"][b, kp, rows].rearrange("(j d) n -> d j n", d=DH)).then_inc(kq_in[g], 16)
                        sp.dma_start(qs[n * DH:(n + 1) * DH, g, :, :],
                                     t["q_dram"][b, qp, rows].rearrange("(j d) n -> d j n", d=DH)).then_inc(kq_in[g], 16)
                    sp.wait_ge(v_dense_used, u + 1)
                    sp.dma_start(vd[:, v_slot, :, :].rearrange("p a c -> p (a c)"), t["v_dram"][b, g]).then_inc(v_in[v_slot], 16)

                def rows_out(b, g):
                    u = b * G + g
                    sp.wait_ge(m_parts, u + 2)
                    for part in range(3):
                        sp.dma_start(qs[TERMS + part:TERMS + part + 1, g, :, :].rearrange("p j (q n) -> p (j q) n", n=P),
                                     mpart[:, part, :]).then_inc(m_in, 16)

                def heads_out(b, g):
                    sp.wait_ge(o_ready, b * G + g + 2)
                    for j in range(HG):
                        sp.dma_start(t["o_dram"][b, (g * HG + j) * DH:(g * HG + j + 1) * DH],
                                     o[j * 32:j * 32 + DH, :]).then_inc(o_stored, 16)

                def step(b, g, last):
                    if not last or g == 0:
                        load(*((b, 3) if g == 0 else (b + 1, g - 1)))
                    if not last or g + 1 < G:
                        rows_out(*((b, g + 1) if g + 1 < G else (b + 1, 0)))
                    heads_out(b, g)

                sp.sem_inc(m_in, 1)
                sp.sem_inc(o_stored, 1)
                for g in range(G - 1):
                    load(0, g)
                rows_out(0, 0)
                with sp.Fori(0, B - 1) as b:
                    for g in range(G):
                        step(b, g, False)
                for g in range(G):
                    step(B - 1, g, True)
                sp.wait_ge(o_stored, 1 + UNITS * HG * 16)

            @block.tensor
            def _(pe):
                pe.sem_inc(kq_used, SLOTS)
                pe.sem_inc(pv, PRING)
                pe.wait_ge(ones, 1)

                def max_product(b, g, u, n):
                    j, q, h = max_jobs[n]
                    if n == 0:
                        pe.wait_ge(kq_in[g], b * 16 * (NLOAD - 1) + 16 * (NLOAD - 1))
                        pe.wait_ge(m_parts, u + 1)
                    pe.wait_ge(m_red, u * len(max_jobs) + n + 1)
                    for a, w in spans(HALF if h == 0 else KEYS - HALF, 512):
                        ins = nc.tensor.matmul(ps_m[:, h, a:a + w], qs[0:TERMS, g, j, q * P:q * P + P],
                                               ks[0:TERMS, g, j, h * HALF + a:h * HALF + a + w], start=True, stop=True)
                    ins.then_inc(m_mm, 1)

                def turn_max(u):
                    pe.wait_ge(m_all, u + 1)
                    nc.tensor.transpose(ps_m[0:HG * QT, 0, 0:P], nmax[:, :], t["ident"][:, :]).then_inc(m_turned, 1)

                def scores(u, g, n):
                    kt, j = n // HG, n % HG
                    r = key_rows(kt)
                    pe.wait_ge(expd, u * NST + n + 1 + (SBANKS - 1 if g == n == 0 else 0))
                    nc.tensor.matmul(ps_s[0:r, (NST * g + n) % SBANKS, :], ks[:, g, j, kt * P:kt * P + r], qs[:, g, j, :],
                                     start=True, stop=True).then_inc(s_mm, 1)

                def values(u, g, n):
                    kt, j = n // HG, n % HG
                    r = key_rows(kt)
                    pe.wait_ge(expd, u * NST + n + 1 + SBANKS)
                    nc.tensor.matmul(ps_o[j * 32:(j + 1) * 32, :], vw[0:r, g % 2, kt * HG + j, :],
                                     pr[0:r, (NST * g + n) % PRING, :], start=kt == 0, stop=kt == KT - 1).then_inc(pv, 1)

                def unit(b, g, nxt):
                    u = b * G + g
                    pe.wait_ge(m_in, u * 48 + 49)
                    done = 0
                    for kt in range(KT + 1):
                        for j in range(HG):
                            if kt < KT:
                                scores(u, g, kt * HG + j)
                            if nxt is not None and j in (0, 2) or kt == KT:
                                todo = min(len(max_jobs), -(-len(max_jobs) * (2 * kt + j // 2 + 1) // (2 * KT - 3)))
                                while nxt is not None and done < todo:
                                    max_product(nxt[0], nxt[1], nxt[0] * G + nxt[1], done)
                                    done += 1
                        if nxt is not None and kt == KT - 1:
                            turn_max(nxt[0] * G + nxt[1])
                        if kt == 1:
                            pe.wait_ge(v_wide, u + 1)
                            pe.wait_ge(acc_out, u + 1)
                        if kt:
                            for j in range(HG):
                                values(u, g, (kt - 1) * HG + j)
                    pe.wait_ge(pv, (u + 1) * NST + PRING)
                    pe.sem_inc(kq_used, 1)
                    pe.sem_inc(v_used, 1)

                for n in range(len(max_jobs)):
                    max_product(0, 0, 0, n)
                turn_max(0)
                with pe.Fori(0, B - 1) as b:
                    for g in range(G):
                        unit(b, g, (b, g + 1) if g + 1 < G else (b + 1, 0))
                for g in range(G):
                    unit(B - 1, g, (B - 1, g + 1) if g + 1 < G else None)

            @block.scalar
            def _(act):
                act.sem_inc(expd, SBANKS)
                with act.Fori(0, B) as b:
                    for g in range(G):
                        for n in range(NST):
                            u, r = b * G + g, key_rows(n // HG)
                            act.wait_ge(pv, u * NST + n + 1)
                            act.wait_ge(s_mm, u * NST + n + 1)
                            nc.scalar.activation(pr[0:r, (NST * g + n) % PRING, :], ps_s[0:r, (NST * g + n) % SBANKS, :],
                                                 ACT.Exp, scale=SCALE).then_inc(expd, 1)

            @block.vector
            def _(dve):
                nc.vector.memset(ks[TERMS:STACK, :, :, :], 1.0).then_inc(ones, 1)
                dve.sem_inc(m_red, MBANKS)
                for credit in (acc_out, m_parts, o_ready):
                    dve.sem_inc(credit, 1)

                def maxima(u, me):
                    for n, (j, q, h) in enumerate(max_jobs):
                        w = HALF if h == 0 else KEYS - HALF
                        dve.wait_ge(m_mm, u * len(max_jobs) + n + 1)
                        nc.vector.tensor_reduce(pmax[:, j * QT + q, h:h + 1], ps_m[:, h, 0:w], AX.X, ALU.max).then_inc(m_red, 1)
                    dve.wait_ge(m_red, (u + 1) * len(max_jobs) + MBANKS)
                    nc.vector.tensor_reduce(nmax[:, :], pmax[:, :, :], AX.X, ALU.max, negate=True).then_inc(m_all, 1)
                    dve.wait_ge(m_turned, u + 1)
                    dve.wait_ge(m_in, u * 48 + 1)
                    me.then(nc.vector.tensor_copy(mpart[:, 0, :], ps_m[0:HG * QT, 0, 0:P]))
                    me.then(nc.vector.tensor_tensor(mrest[:, 0, :], ps_m[0:HG * QT, 0, 0:P], mpart[:, 0, :], ALU.subtract))
                    me.then(nc.vector.tensor_copy(mpart[:, 1, :], mrest[:, 0, :]))
                    nc.vector.tensor_tensor(mpart[:, 2, :], mrest[:, 0, :], mpart[:, 1, :], ALU.subtract).then_inc(m_parts, 1)

                def finish(u, me):
                    dve.wait_ge(o_ready, u + 1)
                    dve.wait_ge(pv, (u + 1) * NST + PRING)
                    nc.vector.tensor_copy(acc[:, :], ps_o[:, :]).then_inc(acc_out, 1)
                    dve.wait_ge(acc_out, u + 2)
                    gate(dve, t["dve_gate"])
                    me.then(nc.vector.stream_shuffle(den[:, 0, :], acc[:, :], [DH + r % DH for r in range(32)]))
                    me.then(nc.vector.reciprocal(den[:, 1, :], den[:, 0, :]))
                    dve.wait_ge(o_stored, u * 16 * HG + 1)
                    nc.vector.tensor_tensor(o[:, :], acc[:, :], den[:, 1, :], ALU.mult).then_inc(o_ready, 1)

                maxima(0, Own(dve, own))
                with dve.Fori(0, B - 1) as b:
                    for g in range(G):
                        u = b * G + g
                        me = Own(dve, own, u, 5)
                        me.n = 3
                        maxima(u + 1, me)
                        finish(u, me)
                for g in range(G):
                    u = (B - 1) * G + g
                    me = Own(dve, own, u, 5)
                    me.n = 3
                    if g + 1 < G:
                        maxima(u + 1, me)
                    finish(u, me)

            @block.gpsimd
            def _(pool):
                nc.gpsimd.memset(vw[:, :, :, :], 1.0).then_inc(v_ones, 1)
                pool.sem_inc(v_used, 2)
                pool.sem_inc(v_dense_used, 2)
                pool.wait_ge(v_ones, 1)

                def spread(b, g):
                    u = b * G + g
                    pool.wait_ge(v_in[g % 2], (b * 2 + g // 2 + 1) * 16)
                    pool.wait_ge(v_used, u + 1)
                    gate(pool, t["pool_gate"])
                    nc.gpsimd.tensor_copy(vw[:, g % 2, :, 0:DH], vd[:, g % 2, :, :]).then_inc(v_wide, 1)
                    pool.wait_ge(v_wide, u + 1)
                    pool.sem_inc(v_dense_used, 1)

                spread(0, 0)
                with pool.Fori(0, B - 1) as b:
                    for g in range(G):
                        spread(*((b, g + 1) if g + 1 < G else (b + 1, 0)))
                for g in range(1, G):
                    spread(B - 1, g)


E = 4
F = 4 * D
FC = F // P


def experts(nc, sem, t):
    USES = 1 + E
    with Stage(nc, "ex") as st:
        oT = st.sb("oT", [P, KC, S])
        wo, bo = st.sb("wo", [P, KC, D]), st.sb("bo", [P, D])
        wr, br, iota = st.sb("wr", [P, KC, E]), st.sb("br", [P, E]), st.sb("iota", [P, E])
        w1, b1 = st.sb("w1", [P, E, KC, F]), st.sb("b1", [P, E * FC])
        w2, b2 = st.sb("w2", [P, E, FC, D]), st.sb("b2", [P, E, D])
        xn, xnT = st.sb("xn", [P, QT, D]), st.sb("xnT", [P, KC, S])
        hid = st.sb("hid", [P, 2, FC, S])
        part = st.sb("part", [P, QT, D])
        stats, mv = st.sb("stats", [P, QT, 6]), st.sb("mv", [P, QT, 2])
        ve, sd, rstd = st.sb("ve", [P, QT]), st.sb("sd", [P, QT]), st.sb("rstd", [P, QT])
        logit, top, at = st.sb("logit", [P, QT, 8]), st.sb("top", [P, QT, 8]), st.sb("at", [P, QT, 8], U32)
        atf, share = st.sb("atf", [P, QT]), st.sb("share", [P, QT, E])
        ps_o, ps_h, ps_t = st.ps("pso", [P, 2, QT, D]), st.ps("psh", [P, 2, 512]), st.ps("pst", [P, KC, 512])

        w_in, o_in, o_used = sem("ex_w"), sem("ex_o"), sem("ex_o_used")
        filled, taken, up, relud = sem("ex_filled"), sem("ex_taken"), sem("ex_up"), sem("ex_relu")
        own, normed, var, sdr = sem("ex_own"), sem("ex_normed"), sem("ex_var"), sem("ex_sd")
        turned, xnT_ready, routed, logits_taken = sem("ex_turned"), sem("ex_xnT"), sem("ex_routed"), sem("ex_logits")
        added, padded = sem("ex_added"), sem("ex_padded")
        NW = 10

        with nc.Block() as block:
            @block.sync
            def _(sp):
                for dst, name in ((wo, "wo"), (bo, "bo"), (wr, "wr"), (br, "br"), (iota, "iota_e"),
                                  (w1, "w1"), (b1, "b1"), (w2, "w2"), (b2, "b2")):
                    sp.dma_start(dst.ap(), t[name + "_in"]).then_inc(w_in, 16)
                with sp.Fori(0, B) as b:
                    sp.wait_ge(o_used, b + 1)
                    sp.dma_start(oT[:, :, :], t["o_dram"][b].rearrange("(k p) n -> p k n", p=P)).then_inc(o_in, 16)

            @block.tensor
            def _(pe):
                pe.sem_inc(o_used, 1)
                pe.sem_inc(filled, 1)
                pe.wait_ge(w_in, 16 * (NW - 1))
                with pe.Fori(0, B) as b:
                    pe.wait_ge(o_in, b * 16 + 16)
                    pe.wait_ge(taken, b * USES + 1)
                    for q in range(QT):
                        for k in range(KC):
                            ins = nc.tensor.matmul(ps_o[:, 0, q, :], oT[:, k, q * P:q * P + P], wo[:, k, :],
                                                   start=k == 0, stop=k == KC - 1)
                    ins.then_inc(filled, 1)
                    pe.wait_ge(filled, b * USES + 2)
                    pe.sem_inc(o_used, 1)
                    pe.wait_ge(normed, (b + 1) * QT)
                    for q in range(QT):
                        for k in range(KC):
                            ins = nc.tensor.transpose(ps_t[:, k, q * P:q * P + P], xn[:, q, k * P:k * P + P],
                                                      t["ident"][:, :])
                    ins.then_inc(turned, 1)
                    pe.wait_ge(xnT_ready, b + 1)
                    for q in range(QT):
                        for k in range(KC):
                            ins = nc.tensor.matmul(ps_t[:, 0, q * E:q * E + E], xnT[:, k, q * P:q * P + P], wr[:, k, :],
                                                   start=k == 0, stop=k == KC - 1)
                    ins.then_inc(routed, 1)

                    def up_product(e):
                        for c in range(FC):
                            n = e * FC + c
                            pe.wait_ge(relud, b * E * FC + n + 1)
                            for k in range(KC):
                                ins = nc.tensor.matmul(ps_h[:, n % 2, :], w1[:, e, k, c * P:c * P + P], xnT[:, k, :],
                                                       start=k == 0, stop=k == KC - 1)
                            ins.then_inc(up, 1)

                    def down_product(e):
                        pe.wait_ge(relud, b * E * FC + (e + 1) * FC + 2)
                        if e:
                            pe.wait_ge(taken, b * USES + e + 1)
                        for q in range(QT):
                            for c in range(FC):
                                ins = nc.tensor.matmul(ps_o[:, (e + 1) % 2, q, :], hid[:, e % 2, c, q * P:q * P + P],
                                                       w2[:, e, c, :], start=c == 0, stop=c == FC - 1)
                        ins.then_inc(filled, 1)

                    up_product(0)
                    for e in range(E):
                        if e + 1 < E:
                            up_product(e + 1)
                        down_product(e)

            @block.scalar
            def _(act):
                act.sem_inc(relud, 2)
                act.wait_ge(w_in, 16 * (NW - 1))
                with act.Fori(0, B) as b:
                    act.wait_ge(var, b + 1)
                    nc.scalar.activation(sd[:, :], ve[:, :], ACT.Sqrt).then_inc(sdr, 1)
                    for e in range(E):
                        act.wait_ge(filled, b * USES + (e if e > 1 else 0) + 1)
                        for c in range(FC):
                            n = e * FC + c
                            act.wait_ge(up, b * E * FC + n + 1)
                            nc.scalar.activation(hid[:, e % 2, c, :], ps_h[:, n % 2, :], ACT.Relu,
                                                 bias=b1[:, n:n + 1]).then_inc(relud, 1)

            @block.vector
            def _(dve):
                nc.vector.memset(logit[:, :, :], -3.0e38).then_inc(padded, 1)
                dve.sem_inc(taken, 1)
                dve.wait_ge(padded, 1)
                dve.wait_ge(w_in, 16 * (NW - 1))
                with dve.Fori(0, B) as b:
                    me = Own(dve, own, b, 13)
                    tiles = t["x"][:, bass.ds(b * QT, QT), :]
                    dve.wait_ge(filled, b * USES + 2)
                    nc.vector.tensor_tensor(part[:, :, :], ps_o[:, 0, :, :],
                                            bo[:, :].unsqueeze(1).broadcast_to([P, QT, D]), ALU.add).then_inc(taken, 1)
                    dve.wait_ge(taken, b * USES + 2)
                    me.then(nc.vector.scalar_tensor_tensor(tiles, part[:, :, :], t["gate_x"](0), tiles,
                                                           ALU.mult, ALU.add))
                    norm_tiles(nc, dve, me, lambda q: t["x_tile"](b * QT + q), lambda q: xn[:, q, :],
                               stats, mv, ve, rstd, t["dve_gate"], var, (sdr, b + 1), sd, normed)
                    dve.wait_ge(turned, b + 1)
                    nc.vector.tensor_copy(xnT[:, :, :], ps_t[:, :, :]).then_inc(xnT_ready, 1)
                    dve.wait_ge(routed, b + 1)
                    me.then(nc.vector.tensor_tensor(logit[:, :, 0:E],
                                                    ps_t[:, 0, 0:QT * E].rearrange("p (q e) -> p q e", e=E),
                                                    br[:, :].unsqueeze(1).broadcast_to([P, QT, E]), ALU.add))
                    gate(dve, t["dve_gate"])
                    for q in range(QT):
                        ins = nc.vector.max(top[:, q, :], logit[:, q, :])
                    me.then(ins)
                    gate(dve, t["dve_gate"])
                    for q in range(QT):
                        ins = nc.vector.max_index(at[:, q, :], top[:, q, :], logit[:, q, :])
                    me.then(ins)
                    me.then(nc.vector.tensor_copy(atf[:, :], at[:, :, 0]))
                    for q in range(QT):
                        ins = nc.vector.tensor_scalar(share[:, q, :], iota[:, :], atf[:, q:q + 1], t["gate_f"](0),
                                                      ALU.is_equal, ALU.mult)
                    me.then(ins)
                    for e in range(E):
                        dve.wait_ge(filled, b * USES + e + 3)
                        nc.vector.tensor_tensor(part[:, :, :], ps_o[:, (e + 1) % 2, :, :],
                                                b2[:, e, :].unsqueeze(1).broadcast_to([P, QT, D]), ALU.add).then_inc(taken, 1)
                        dve.wait_ge(taken, b * USES + e + 3)
                        for q in range(QT):
                            ins = nc.vector.scalar_tensor_tensor(t["x_tile"](b * QT + q), part[:, q, :],
                                                                 share[:, q, e:e + 1], t["x_tile"](b * QT + q),
                                                                 ALU.mult, ALU.add)
                        me.then(ins)


def attend_wide(nc, sem, t):
    R = 16
    SCALE = 1.0 / float(D) ** 0.5
    NW = 12
    with Stage(nc, "aw") as st:
        ctxT, ctx = st.sb("ctxT", [P, KC, KEYS]), st.sb("ctx", [P, KT, D])
        wgt = {n: st.sb(n, [P, KC, D]) for n in ("q", "k", "v", "oT")}
        low = {n: (st.sb(n + "a", [R, D]), st.sb(n + "bT", [R, D])) for n in "qkv"}
        full = {n: st.sb(n + "f", [P, KC, D]) for n in "qkv"}
        amat, cmat = st.sb("amat", [P, KC, D]), st.sb("cmat", [P, KC, D])
        xn, xnT, gT = st.sb("xn", [P, QT, D]), st.sb("xnT", [P, KC, S]), st.sb("gT", [P, KC, S])
        prob, pT, uT = st.sb("prob", [P, 2, KEYS]), st.sb("pT", [P, KT, S]), st.sb("uT", [P, KC, S])
        peak, shift, den = st.sb("peak", [P, QT]), st.sb("shift", [P, QT]), st.sb("den", [P, QT])
        fac = st.sb("fac", [P, QT])
        stats, mv = st.sb("stats", [P, QT, 6]), st.sb("mv", [P, QT, 2])
        ve, sd, rstd = st.sb("ve", [P, QT]), st.sb("sd", [P, QT]), st.sb("rstd", [P, QT])
        ps_s, ps_p, ps_w = st.ps("pss", [P, 4, 512]), st.ps("psp", [P, 2, 4, P]), st.ps("psw", [P, 2, 512])

        w_in, c_in, c_used = sem("aw_w"), sem("aw_c"), sem("aw_c_used")
        mixed, mixed_out = sem("aw_mixed"), sem("aw_mixed_out")
        own, normed, var, sdr = sem("aw_own"), sem("aw_normed"), sem("aw_var"), sem("aw_sd")
        wide, wide_out = sem("aw_wide"), sem("aw_wide_out")
        s_mm, peaked, expd, p_turned, p_out = (sem(f"aw_{n}") for n in ("s_mm", "peaked", "exp", "p_turned", "p_out"))
        GR = [(a, min(4, KT - a)) for a in range(0, KT, 4)]
        WIDE = 4

        with nc.Block() as block:
            @block.sync
            def _(sp):
                for n in ("q", "k", "v", "oT"):
                    sp.dma_start(wgt[n][:, :, :], t["l1_" + n + "_in"]).then_inc(w_in, 16)
                for n in "qkv":
                    sp.dma_start(low[n][0][:, :], t["l1_" + n + "a_in"]).then_inc(w_in, 16)
                    sp.dma_start(low[n][1][:, :], t["l1_" + n + "bT_in"]).then_inc(w_in, 16)
                with sp.Fori(0, B) as b:
                    sp.wait_ge(c_used, b + 1)
                    sp.dma_start(ctxT[:, :, :], t["ctxT_in"][b]).then_inc(c_in, 16)
                    sp.dma_start(ctx[:, 0:KT - 1, :], t["ctx_in"][b, 0:(KT - 1) * P].rearrange("(k p) d -> p k d", p=P))\
                        .then_inc(c_in, 16)
                    sp.dma_start(ctx[0:key_rows(KT - 1), KT - 1, :], t["ctx_in"][b, (KT - 1) * P:KEYS]).then_inc(c_in, 16)

            @block.tensor
            def _(pe):
                pe.sem_inc(c_used, 1)
                pe.wait_ge(w_in, 160)
                for n, name in enumerate("qkv"):
                    pe.wait_ge(mixed_out, n)
                    for m in range(KC):
                        ins = nc.tensor.matmul(ps_w[:, m, 0:D], low[name][1][:, m * P:m * P + P], low[name][0][:, :],
                                               start=True, stop=True)
                    ins.then_inc(mixed, 1)
                for n, (left_, right) in enumerate(((full["q"], full["k"]), (full["v"], wgt["oT"]))):
                    pe.wait_ge(mixed_out, 3 + n)
                    for m in range(KC):
                        for k in range(KC):
                            ins = nc.tensor.matmul(ps_w[:, m, 0:D], left_[:, k, m * P:m * P + P], right[:, k, :],
                                                   start=k == 0, stop=k == KC - 1)
                    ins.then_inc(mixed, 1)
                pe.wait_ge(mixed_out, 5)
                with pe.Fori(0, B) as b:
                    pe.wait_ge(c_in, b * 48 + 48)
                    pe.wait_ge(normed, (b + 1) * QT)
                    pe.wait_ge(wide_out, b * WIDE + 1)
                    for q in range(QT):
                        for k in range(KC):
                            ins = nc.tensor.transpose(ps_w[:, k, q * P:q * P + P], xn[:, q, k * P:k * P + P],
                                                      t["ident"][:, :])
                    ins.then_inc(wide, 1)
                    pe.wait_ge(wide_out, b * WIDE + 2)
                    for m in range(KC):
                        for k in range(KC):
                            ins = nc.tensor.matmul(ps_w[:, m, :], amat[:, k, m * P:m * P + P], xnT[:, k, :],
                                                   start=k == 0, stop=k == KC - 1)
                    ins.then_inc(wide, 1)
                    pe.wait_ge(wide_out, b * WIDE + 3)

                    def score_rows(q):
                        pe.wait_ge(expd, b * QT + q + 1)
                        for n, (a, w) in enumerate(KEY_SPANS):
                            for k in range(KC):
                                ins = nc.tensor.matmul(ps_s[:, n, 0:w], gT[:, k, q * P:q * P + P], ctxT[:, k, a:a + w],
                                                       start=k == 0, stop=k == KC - 1)
                        ins.then_inc(s_mm, 1)

                    def turn_probs(q):
                        pe.wait_ge(expd, b * QT + q + 2)
                        for n, (a, m) in enumerate(GR):
                            u = (b * QT + q) * len(GR) + n
                            pe.wait_ge(p_out, u + 1)
                            for kt in range(a, a + m):
                                r = key_rows(kt)
                                ins = nc.tensor.transpose(ps_p[0:r, n % 2, kt - a, :], prob[:, q % 2, kt * P:kt * P + r],
                                                          t["ident"][:, :])
                            ins.then_inc(p_turned, 1)

                    score_rows(0)
                    for q in range(QT):
                        if q + 1 < QT:
                            score_rows(q + 1)
                        turn_probs(q)
                    pe.wait_ge(p_out, (b + 1) * QT * len(GR) + 2)
                    for m in range(KC):
                        for kt in range(KT):
                            r = key_rows(kt)
                            ins = nc.tensor.matmul(ps_w[:, m, :], ctx[0:r, kt, m * P:m * P + P], pT[0:r, kt, :],
                                                   start=kt == 0, stop=kt == KT - 1)
                    ins.then_inc(wide, 1)
                    pe.wait_ge(wide_out, b * WIDE + 4)
                    pe.sem_inc(c_used, 1)
                    for q in range(QT):
                        for k in range(KC):
                            ins = nc.tensor.matmul(ps_w[:, q // 2, (q % 2) * D:(q % 2) * D + D], uT[:, k, q * P:q * P + P],
                                                   cmat[:, k, :], start=k == 0, stop=k == KC - 1)
                    ins.then_inc(wide, 1)

            @block.scalar
            def _(act):
                act.sem_inc(expd, 1)
                with act.Fori(0, B) as b:
                    act.wait_ge(var, b + 1)
                    nc.scalar.activation(sd[:, :], ve[:, :], ACT.Sqrt).then_inc(sdr, 1)
                    for q in range(QT):
                        if q > 1:
                            act.wait_ge(p_turned, (b * QT + q - 1) * len(GR))
                        act.wait_ge(peaked, b * QT + q + 1)
                        nc.scalar.activation(prob[:, q % 2, :], ps_s[:, :, :].rearrange("p a n -> p (a n)")[:, 0:KEYS],
                                             ACT.Exp, bias=shift[:, q:q + 1], scale=SCALE,
                                             accum_out=den[:, q:q + 1]).then_inc(expd, 1)

            @block.vector
            def _(dve):
                dve.sem_inc(p_out, 2)
                dve.sem_inc(wide_out, 1)
                dve.wait_ge(w_in, 160)
                for n, name in enumerate("qkv"):
                    dve.wait_ge(mixed, n + 1)
                    nc.vector.tensor_tensor(full[name][:, :, :], ps_w[:, :, 0:D], wgt[name][:, :, :],
                                            ALU.add).then_inc(mixed_out, 1)
                for n, dst in enumerate((amat, cmat)):
                    dve.wait_ge(mixed, n + 4)
                    nc.vector.tensor_copy(dst[:, :, :], ps_w[:, :, 0:D]).then_inc(mixed_out, 1)
                with dve.Fori(0, B) as b:
                    me = Own(dve, own, b, 3 + QT + 2)
                    norm_tiles(nc, dve, me, lambda q: t["x_tile"](b * QT + q), lambda q: xn[:, q, :],
                               stats, mv, ve, rstd, t["dve_gate"], var, (sdr, b + 1), sd, normed)
                    dve.wait_ge(wide, b * WIDE + 1)
                    nc.vector.tensor_copy(xnT[:, :, :], ps_w[:, :, :]).then_inc(wide_out, 1)
                    dve.wait_ge(wide, b * WIDE + 2)
                    nc.vector.tensor_copy(gT[:, :, :], ps_w[:, :, :]).then_inc(wide_out, 1)

                    def find_peak(q):
                        dve.wait_ge(s_mm, b * QT + q + 1)
                        me.then(nc.vector.tensor_reduce(peak[:, q:q + 1],
                                                        ps_s[:, :, :].rearrange("p a n -> p (a n)")[:, 0:KEYS],
                                                        AX.X, ALU.max))
                        nc.vector.tensor_scalar(shift[:, q:q + 1], peak[:, q:q + 1], -SCALE, None,
                                                ALU.mult).then_inc(peaked, 1)

                    def probs_out(q):
                        for n, (a, m) in enumerate(GR):
                            u = (b * QT + q) * len(GR) + n
                            r = key_rows(a + m - 1)
                            dve.wait_ge(p_turned, u + 1)
                            nc.vector.tensor_copy(pT[0:r, a:a + m, q * P:q * P + P], ps_p[0:r, n % 2, 0:m, :]).then_inc(p_out, 1)

                    find_peak(0)
                    for q in range(QT):
                        if q + 1 < QT:
                            find_peak(q + 1)
                        probs_out(q)
                    dve.wait_ge(wide, b * WIDE + 3)
                    nc.vector.tensor_copy(uT[:, :, :], ps_w[:, :, :]).then_inc(wide_out, 1)
                    dve.wait_ge(expd, (b + 1) * QT + 1)
                    me.then(nc.vector.reciprocal(fac[:, :], den[:, :]))
                    me.then(nc.vector.tensor_scalar(fac[:, :], fac[:, :], t["gate_x"](1), None, ALU.mult))
                    dve.wait_ge(wide, b * WIDE + 4)
                    for q in range(QT):
                        ins = nc.vector.scalar_tensor_tensor(t["x_tile"](b * QT + q),
                                                             ps_w[:, q // 2, (q % 2) * D:(q % 2) * D + D],
                                                             fac[:, q:q + 1], t["x_tile"](b * QT + q), ALU.mult, ALU.add)
                    ins.then_inc(wide_out, 1)


MH, NK, KD = 8, 64, 128
TOP = 8
SEL = MH * TOP
YH = NK // 2
HT = P // 2


def memory(nc, sem, t, out):
    memory_keys(nc, sem, t, *t["memory"])
    t["release_x"]()
    memory_tiles(nc, sem, t, out, *t["memory"])


def memory_keys(nc, sem, t, mk, scale, offset):
    PH = 2 * MH
    with Stage(nc, "mk") as st:
        wq, keys = st.sb("wq", [P, PH, D]), st.sb("keys", [P, PH, NK])
        gamma, beta = st.sb("gamma", [P, KC]), st.sb("beta", [P, KC])
        xn, xnT = st.sb("xn", [P, 2, QT, D]), st.sb("xnT", [P, 2, KC, S])
        stats, mv = st.sb("stats", [P, QT, 6]), st.sb("mv", [P, QT, 2])
        ve, sd, rstd = st.sb("ve", [P, QT]), st.sb("sd", [P, QT]), st.sb("rstd", [P, QT])
        bstats, bmv = st.sb("bstats", [P, KC, B, 6]), st.sb("bmv", [P, KC, 2])
        ps_t, ps_k = st.ps("pst", [P, 2, KC, S]), st.ps("psk", [P, 2, 512])
        w_in, own, normed, var, sdr = sem("mk_w"), sem("mk_own"), sem("mk_normed"), sem("mk_var"), sem("mk_sd")
        turned, copied, stored = sem("mk_turned"), sem("mk_copied"), [sem("mk_stored0"), sem("mk_stored1")]
        counted = sem("mk_counted")
        k_mm, k_out, x_stored = sem("mk_k_mm"), sem("mk_k_out"), sem("mk_x_stored")
        HALVES = [(m, c) for m in range(KC) for c in range(2)]

        with nc.Block() as block:
            @block.sync
            def _(sp):
                for s in range(2):
                    sp.sem_inc(stored[s], 1)
                sp.dma_start(t["x_dram"].rearrange("n p d -> p n d"), t["x"]).then_inc(x_stored, 16)
                for dst, name in ((wq, "m_wq"), (keys, "m_keys"), (gamma, "m_gamma"), (beta, "m_beta")):
                    sp.dma_start(dst.ap(), t[name + "_in"]).then_inc(w_in, 16)
                with sp.Fori(0, B // 2) as i:
                    for s in range(2):
                        b = 2 * i + s
                        sp.wait_ge(copied, b + 1)
                        for k in range(KC):
                            sp.dma_start(t["xT_dram"][bass.ds(b * QT, QT), :, k, :].rearrange("q p n -> p q n"),
                                         xnT[:, s, k, :].rearrange("p (q n) -> p q n", n=P)).then_inc(stored[s], 16)
                for s in range(2):
                    sp.wait_ge(stored[s], 16 * KC * (B // 2) + 1)
                sp.wait_ge(x_stored, 16)

            @block.tensor
            def _(pe):
                pe.wait_ge(w_in, 64)
                for n, (m, c) in enumerate(HALVES):
                    if n > 1:
                        pe.wait_ge(k_out, n - 1)
                    for ph in range(MH):
                        ins = nc.tensor.matmul(ps_k[:, n % 2, ph * NK:(ph + 1) * NK], wq[:, c * MH + ph, m * P:m * P + P],
                                               keys[:, c * MH + ph, :], start=True, stop=True)
                    ins.then_inc(k_mm, 1)
                with pe.Fori(0, B // 2) as i:
                    for s in range(2):
                        b = 2 * i + s
                        pe.wait_ge(normed, (b + 1) * QT)
                        for q in range(QT):
                            for k in range(KC):
                                ins = nc.tensor.transpose(ps_t[:, s, k, q * P:q * P + P], xn[:, s, q, k * P:k * P + P],
                                                          t["ident"][:, :])
                        ins.then_inc(turned, 1)

            @block.scalar
            def _(act):
                for n, (m, c) in enumerate(HALVES):
                    act.wait_ge(k_mm, n + 1)
                    nc.scalar.activation(mk[:, m, c * 512:c * 512 + 512], ps_k[:, n % 2, :], ACT.Copy).then_inc(k_out, 1)
                with act.Fori(0, B // 2) as i:
                    for s in range(2):
                        b = 2 * i + s
                        act.wait_ge(var, b + 1)
                        nc.scalar.activation(sd[:, :], ve[:, :], ACT.Sqrt).then_inc(sdr, 1)
                        act.wait_ge(turned, b + 1)
                        act.wait_ge(stored[s], i * 16 * KC + 1)
                        nc.scalar.activation(xnT[:, s, :, :], ps_t[:, s, :, :], ACT.Copy).then_inc(copied, 1)
                act.wait_ge(var, B + 1)
                nc.scalar.activation(sd[:, 0:KC], ve[:, 0:KC], ACT.Sqrt).then_inc(sdr, 1)

            @block.vector
            def _(dve):
                with dve.Fori(0, B // 2) as i:
                    for s in range(2):
                        b = 2 * i + s
                        me = Own(dve, own, b, 3)
                        norm_tiles(nc, dve, me, lambda q: t["x_tile"](b * QT + q), lambda q: xn[:, s, q, :],
                                   stats, mv, ve, rstd, t["dve_gate"], var, (sdr, b + 1), sd, normed)
                        dve.wait_ge(copied, b + 1)
                        gate(dve, t["dve_gate"])
                        for k in range(KC):
                            ins = nc.vector.bn_stats(bstats[:, k, bass.ds(b, 1), :].rearrange("p a c -> p (a c)"),
                                                     xnT[:, s, k, :])
                        ins.then_inc(counted, 1)
                me = Own(dve, own, B, 3)
                dve.wait_ge(counted, B)
                for k in range(KC):
                    ins = nc.vector.bn_aggr(bmv[:, k, :], bstats[:, k, :, :].rearrange("p b c -> p (b c)"))
                me.then(ins)
                nc.vector.tensor_scalar(ve[:, 0:KC], bmv[:, :, 1], LN_EPS, None, ALU.add).then_inc(var, 1)
                dve.wait_ge(sdr, B + 1)
                dve.wait_ge(w_in, 64)
                me.then(nc.vector.reciprocal(rstd[:, 0:KC], sd[:, 0:KC]))
                me.then(nc.vector.tensor_tensor(scale[:, :], rstd[:, 0:KC], gamma[:, :], ALU.mult))
                me.then(nc.vector.tensor_tensor(offset[:, :], bmv[:, :, 0], scale[:, :], ALU.mult))
                me.then(nc.vector.tensor_tensor(offset[:, :], beta[:, :], offset[:, :], ALU.subtract))


def memory_tiles(nc, sem, t, out, mk, scale, offset):
    TB = 16
    NB = HT // TB * 2
    YB = 4
    ND = YH // YB
    QN = 5
    with Stage(nc, "mt") as st:
        key_in, key_out = st.sb("key_in", [P, KC, YH, P]), st.sb("key_out", [P, YH, D])
        iota_m, iota8 = st.sb("iota_m", [P, P, TB], BF16), st.sb("iota8", [P, TOP])
        identb = st.sb("identb", [P, P], BF16)
        iota_f = st.sb("iota_f", [P, P])
        xl, xb = st.sb("xl", [P, 2, KC, P]), st.sb("xb", [P, 2, KC, P])
        xr, o = st.sb("xr", [P, 2, D]), st.sb("o", [P, 2, D])
        sims = st.sb("sims", [P, 2 * MH, NK])
        s8, i8, i8f = st.sb("s8", [P, 2 * MH, TOP]), st.sb("i8", [P, 2 * MH, TOP], U32), st.sb("i8f", [P, 2 * MH, TOP])
        pairs = st.sb("pairs", [P, MH, TOP, TOP])
        best, rank = st.sb("best", [P, MH, TOP]), st.sb("rank", [P, MH, TOP], U32)
        ab, abf = st.sb("ab", [P, 2, SEL], U32), st.sb("abf", [P, 2, SEL])
        match = st.sb("match", [P, 2 * MH, TOP, TOP])
        xy, ge = st.sb("xy", [P, 2, SEL]), st.sb("ge", [P, SEL])
        diff, ew, den, w, wr = (st.sb("diff", [P, MH, TOP]), st.sb("ew", [P, MH, TOP]), st.sb("den", [P, 2, MH]),
                                st.sb("w", [P, MH, TOP]), st.sb("wrest", [P, SEL]))
        picks, picksT = st.sb("picks", [P, 2, QN, SEL], BF16), st.sb("picksT", [P, QN, HT], BF16)
        hot_m, hot_y = st.sb("hot_m", [P, 2, P, HT], BF16), st.sb("hot_y", [P, YH, HT], BF16)
        hot_w = st.sb("hot_w", [P, 2, 3, YH, HT], BF16)
        g = st.sb("g", [P, 2, YH, P])
        ps_c, ps_d = st.ps("psc", [P, 2, 2, 512]), st.ps("psd", [P, 2, 512])
        ps_u, ps_x = st.ps("psu", [P, 512]), st.ps("psx", [P, 1024], BF16)
        ps_sim = ps_x[:, :].bitcast(F32)

        w_in, ready, xl_in, xr_in = sem("mt_w"), sem("mt_ready"), [sem("mt_xl0"), sem("mt_xl1")], [sem("mt_xr0"), sem("mt_xr1")]
        xb_ready, sim_mm, sim_out, picked = sem("mt_xb"), sem("mt_sim_mm"), sem("mt_sim_out"), sem("mt_picked")
        diff_ready, weighed, sel_ready = sem("mt_diff"), sem("mt_weighed"), sem("mt_sel")
        turned, turned_out, hot = sem("mt_turned"), sem("mt_turned_out"), sem("mt_hot")
        c_mm, w_out, d_mm, g_out = sem("mt_c_mm"), sem("mt_w_out"), sem("mt_d_mm"), sem("mt_g_out")
        u_mm, final, o_stored = sem("mt_u_mm"), sem("mt_final"), [sem("mt_o0"), sem("mt_o1")]
        own_s, own_h = sem("mt_own_select"), sem("mt_own_hot")
        NSEL, NHOT = 17, 2

        def steps(eng, first, step):
            first()
            with eng.Fori(0, NT // 2 - 1) as i:
                for off in range(2):
                    step(i, off, 2)
            for off in range(2):
                step(NT // 2 - 1, off, 1 - off)

        with nc.Block() as block:
            @block.sync
            def _(sp):
                for dst, name in ((iota_f, "m_iota"), (key_in, "m_in"), (key_out, "m_out"), (iota8, "m_iota8")):
                    sp.dma_start(dst.ap(), t[name + "_in"]).then_inc(w_in, 16)

                for s in range(2):
                    sp.sem_inc(o_stored[s], 1)

                def load(i, off):
                    n = 2 * i + off
                    sp.dma_start(xr[:, off % 2, :], t["x_dram"][n]).then_inc(xr_in[off % 2], 16)

                def first():
                    load(0, 0)
                    load(0, 1)

                def step(i, off, ahead):
                    n = 2 * i + off
                    sp.wait_ge(final, n + 2)
                    sp.dma_start(t["out_tiles"][n], o[:, off, :]).then_inc(o_stored[off], 16)
                    if ahead == 2:
                        load(i, off + 2)

                steps(sp, first, step)
                for s in range(2):
                    sp.wait_ge(o_stored[s], 16 * (NT // 2) + 1)

            @block.gpsimd
            def _(pool):
                def token_rows(i, off):
                    n, s = 2 * i + off, off % 2
                    if off > 1:
                        pool.wait_ge(d_mm, (n - 1) * ND)
                        gate(pool, t["pool_gate"])
                    pool.dma_start(xl[:, s, :, :], t["xT_dram"][n]).then_inc(xl_in[s], 16)
                    if off > 1:
                        pool.wait_ge(sim_mm, (n - 1) * 2)
                    pool.wait_ge(xl_in[s], 16 * (i + off // 2) + 16)
                    gate(pool, t["pool_gate"])
                    for k in range(KC):
                        ins = nc.gpsimd.tensor_scalar(xb[:, s, k, :], xl[:, s, k, :], scale[:, k:k + 1], offset[:, k:k + 1],
                                                      ALU.mult, ALU.add)
                    ins.then_inc(xb_ready, 1)

                token_rows(0, 0)
                token_rows(0, 1)
                with pool.Fori(0, NT // 2 - 1) as i:
                    for off in range(2):
                        token_rows(i, off + 2)

            @block.tensor
            def _(pe):
                pe.sem_inc(u_mm, 1)
                pe.wait_ge(ready, 1)

                def half_scores(i, off, c):
                    n = 2 * i + off
                    if c == 0:
                        pe.wait_ge(xb_ready, n + 1)
                        if off > 1:
                            pe.wait_ge(turned_out, n - 1)
                    if off or c:
                        pe.wait_ge(sim_out, 2 * n + c)
                    for k in range(KC):
                        ins = nc.tensor.matmul(ps_sim, xb[:, off % 2, k, :], mk[:, k, c * 512:c * 512 + 512],
                                               start=k == 0, stop=k == KC - 1)
                    ins.then_inc(sim_mm, 1)

                def turn_picks(i, off, ahead):
                    n = 2 * i + off
                    pe.wait_ge(sel_ready, n + 1)
                    pe.wait_ge(sim_out, 2 * (n + 1 + ahead))
                    gate(pe, t["pe_gate"])
                    for h in range(2):
                        rows = slice(h * HT, h * HT + HT)
                        for v in range(QN):
                            ins = nc.tensor.transpose(ps_x[rows, v * HT:v * HT + HT], picks[rows, off % 2, v, :],
                                                      identb[rows, rows])
                    ins.then_inc(turned, 1)

                def dense_in(i, off):
                    n, s = 2 * i + off, off % 2
                    pe.wait_ge(xl_in[s], 16 * (i + off // 2) + 16)
                    for j in range(ND):
                        pe.wait_ge(g_out, n * ND + j + 1)
                        for y in range(YB):
                            for k in range(KC):
                                ins = nc.tensor.matmul(ps_d[:, j % 2, y * P:y * P + P], key_in[:, k, j * YB + y, :],
                                                       xl[:, s, k, :], start=k == 0, stop=k == KC - 1)
                        ins.then_inc(d_mm, 1)

                def scatter(i, off, part):
                    n = 2 * i + off
                    if part == 0:
                        pe.wait_ge(hot, n + 1)
                    for tb in range(2 * part, 2 * part + 2):
                        pe.wait_ge(w_out, n * NB + 2 * tb + 2)
                        for tok in range(TB):
                            for v in range(3):
                                for h in range(2):
                                    rows = slice(h * HT, h * HT + HT)
                                    ins = nc.tensor.matmul(ps_c[:, h, tb % 2, tok * YH:(tok + 1) * YH],
                                                           hot_m[rows, off % 2, :, tb * TB + tok],
                                                           hot_w[rows, off % 2, v, :, tb * TB + tok],
                                                           start=v == 0, stop=v == 2)
                                    if tok == TB - 1 and v == 2:
                                        ins.then_inc(c_mm, 1)

                def dense_out(i, off):
                    n = 2 * i + off
                    pe.wait_ge(w_out, (n + 1) * NB + 4)
                    pe.wait_ge(final, n + 1)
                    for y in range(YH):
                        ins = nc.tensor.matmul(ps_u[:, 0:D], g[:, off % 2, y, :], key_out[:, y, :],
                                               start=y == 0, stop=y == YH - 1)
                    ins.then_inc(u_mm, 1)

                def first():
                    for off in range(2):
                        for c in range(2):
                            half_scores(0, off, c)
                    turn_picks(0, 0, 1)
                    pe.wait_ge(w_in, 64)
                    dense_in(0, 0)

                def step(i, off, ahead):
                    for c in range(2):
                        if ahead == 2:
                            half_scores(i, off + 2, c)
                        scatter(i, off, c)
                    if ahead:
                        turn_picks(i, off + 1, min(ahead - 1, 1))
                        dense_in(i, off + 1)
                    dense_out(i, off)

                steps(pe, first, step)

            @block.scalar
            def _(act):
                act.sem_inc(g_out, 2)

                def scores_out(i, off):
                    n = 2 * i + off
                    for c in range(2):
                        act.wait_ge(sim_mm, 2 * n + c + 1)
                        if off:
                            act.wait_ge(picked, n)
                        nc.scalar.activation(sims[:, c * MH:(c + 1) * MH, :].rearrange("p h k -> p (h k)"), ps_sim,
                                             ACT.Copy).then_inc(sim_out, 1)

                def exps(i, off):
                    act.wait_ge(diff_ready, 2 * i + off + 1)
                    nc.scalar.activation(ew[:, :, :], diff[:, :, :], ACT.Exp).then_inc(weighed, 1)

                def gelus(i, off):
                    n = 2 * i + off
                    if off:
                        act.wait_ge(u_mm, n)
                    for j in range(ND):
                        act.wait_ge(d_mm, n * ND + j + 1)
                        nc.scalar.activation(g[:, off % 2, j * YB:(j + 1) * YB, :],
                                             ps_d[:, j % 2, :].rearrange("p (y n) -> p y n", n=P), ACT.Gelu).then_inc(g_out, 1)

                def first():
                    scores_out(0, 0)
                    exps(0, 0)
                    scores_out(0, 1)
                    gelus(0, 0)
                    exps(0, 1)

                def step(i, off, ahead):
                    if ahead == 2:
                        scores_out(i, off + 2)
                    if ahead:
                        gelus(i, off + 1)
                    if ahead == 2:
                        exps(i, off + 2)

                steps(act, first, step)

            @block.vector
            def _(dve):
                dve.sem_inc(w_out, 4)
                dve.sem_inc(final, 1)
                dve.wait_ge(w_in, 64)
                nc.vector.tensor_copy(identb[:, :], t["ident"][:, :])
                nc.vector.tensor_copy(iota_m[:, :, :], iota_f[:, :].unsqueeze(2).broadcast_to([P, P, TB])).then_inc(ready, 1)
                dve.wait_ge(ready, 1)

                def select(i, off):
                    n, s = 2 * i + off, off % 2
                    me = Own(dve, own_s, n, NSEL)
                    dve.wait_ge(sim_out, 2 * n + 2)
                    gate(dve, t["dve_gate"])
                    for h in range(2 * MH):
                        ins = nc.vector.max(s8[:, h, :], sims[:, h, :])
                    me.then(ins)
                    gate(dve, t["dve_gate"])
                    for h in range(2 * MH):
                        ins = nc.vector.max_index(i8[:, h, :], s8[:, h, :], sims[:, h, :])
                    ins.then_inc(picked, 1)
                    dve.wait_ge(picked, n + 1)
                    nc.vector.tensor_copy(i8f[:, :, :], i8[:, :, :])
                    me.then(nc.vector.tensor_tensor(pairs[:, :, :, :],
                                                    s8[:, 0:MH, :].unsqueeze(3).broadcast_to([P, MH, TOP, TOP]),
                                                    s8[:, MH:, :].unsqueeze(2).broadcast_to([P, MH, TOP, TOP]), ALU.add))
                    gate(dve, t["dve_gate"])
                    for h in range(MH):
                        ins = nc.vector.max(best[:, h, :], pairs[:, h, :, :].rearrange("p a b -> p (a b)"))
                    me.then(ins)
                    nc.vector.tensor_tensor(diff[:, :, :], best[:, :, :], best[:, :, 0:1].broadcast_to([P, MH, TOP]),
                                            ALU.subtract).then_inc(diff_ready, 1)
                    for h in range(MH):
                        ins = nc.vector.max_index(rank[:, h, :], best[:, h, :], pairs[:, h, :, :].rearrange("p a b -> p (a b)"))
                    me.then(ins)
                    flat = rank[:, :, :].rearrange("p h k -> p (h k)")
                    nc.vector.tensor_scalar(ab[:, 0, :], flat, 3, None, ALU.logical_shift_right)
                    me.then(nc.vector.tensor_scalar(ab[:, 1, :], flat, TOP - 1, None, ALU.bitwise_and))
                    me.then(nc.vector.tensor_copy(abf[:, :, :], ab[:, :, :]))
                    me.then(nc.vector.tensor_tensor(match[:, :, :, :].rearrange("p h k a -> p (h k) a"),
                                                    abf[:, :, :].rearrange("p c n -> p (c n)").unsqueeze(2).broadcast_to([P, 2 * SEL, TOP]),
                                                    iota8[:, :].unsqueeze(1).broadcast_to([P, 2 * SEL, TOP]), ALU.is_equal))
                    me.then(nc.vector.tensor_tensor(match[:, :, :, :], match[:, :, :, :],
                                                    i8f[:, :, :].unsqueeze(2).broadcast_to([P, 2 * MH, TOP, TOP]), ALU.mult))
                    me.then(nc.vector.tensor_reduce(xy[:, :, :], match[:, :, :, :].rearrange("p (c h) k a -> p c (h k) a", c=2),
                                                    AX.X, ALU.add))
                    me.then(nc.vector.tensor_scalar(ge[:, :], xy[:, 1, :], float(YH), None, ALU.is_ge))
                    nc.vector.scalar_tensor_tensor(picks[:, s, 0, :], ge[:, :], float(NK), xy[:, 0, :], ALU.mult, ALU.add)
                    nc.vector.scalar_tensor_tensor(picks[:, s, 1, :], ge[:, :], -float(YH), xy[:, 1, :], ALU.mult, ALU.add)
                    dve.wait_ge(weighed, n + 1)
                    me.then(nc.vector.tensor_reduce(den[:, 0, :], ew[:, :, :], AX.X, ALU.add))
                    me.then(nc.vector.reciprocal(den[:, 1, :], den[:, 0, :]))
                    me.then(nc.vector.tensor_tensor(w[:, :, :], ew[:, :, :], den[:, 1, :].unsqueeze(2).broadcast_to([P, MH, TOP]),
                                                    ALU.mult))
                    wf = w[:, :, :].rearrange("p h k -> p (h k)")
                    me.then(nc.vector.tensor_copy(picks[:, s, 2, :], wf))
                    me.then(nc.vector.tensor_tensor(wr[:, :], wf, picks[:, s, 2, :], ALU.subtract))
                    me.then(nc.vector.tensor_copy(picks[:, s, 3, :], wr[:, :]))
                    me.then(nc.vector.tensor_tensor(picks[:, s, 4, :], wr[:, :], picks[:, s, 3, :], ALU.subtract))
                    dve.sem_inc(sel_ready, 1)
                    assert me.n == NSEL, me.n

                def one_hots(i, off):
                    n, s = 2 * i + off, off % 2
                    me = Own(dve, own_h, n, NHOT)
                    dve.wait_ge(turned, n + 1)
                    nc.vector.tensor_copy(picksT[:, :, :].rearrange("p v n -> p (v n)"), ps_x[:, 0:QN * HT]).then_inc(turned_out, 1)
                    dve.wait_ge(turned_out, n + 1)

                    def is_at(dst, rows, v):
                        return nc.vector.tensor_tensor(
                            dst.rearrange("p m (b n) -> p m b n", n=TB),
                            iota_m[:, 0:rows, :].unsqueeze(2).broadcast_to([P, rows, HT // TB, TB]),
                            picksT[:, v, :].rearrange("p (b n) -> p b n", n=TB).unsqueeze(1).broadcast_to([P, rows, HT // TB, TB]),
                            ALU.is_equal)

                    me.then(is_at(hot_y[:, :, :], YH, 1))
                    is_at(hot_m[:, s, :, :], P, 0)
                    me.then(nc.vector.tensor_tensor(hot_w[:, s, :, :, :], hot_y[:, :, :].unsqueeze(1).broadcast_to([P, 3, YH, HT]),
                                                    picksT[:, 2:QN, :].unsqueeze(2).broadcast_to([P, 3, YH, HT]), ALU.mult))
                    dve.sem_inc(hot, 1)
                    assert me.n == NHOT, me.n

                def weigh(i, off):
                    n = 2 * i + off
                    dve.wait_ge(g_out, (n + 1) * ND + 2)
                    for tb in range(HT // TB):
                        for h in range(2):
                            dve.wait_ge(c_mm, n * NB + 2 * tb + h + 1)
                            a = h * HT + tb * TB
                            gv = g[:, off % 2, :, a:a + TB].rearrange("p y n -> p n y")
                            nc.vector.tensor_tensor(gv, ps_c[:, h, tb % 2, :].rearrange("p (n y) -> p n y", y=YH), gv,
                                                    ALU.mult).then_inc(w_out, 1)

                def finish(i, off):
                    n = 2 * i + off
                    dve.wait_ge(u_mm, n + 2)
                    dve.wait_ge(xr_in[off], 16 * i + 16)
                    dve.wait_ge(o_stored[off], 16 * i + 1)
                    nc.vector.scalar_tensor_tensor(o[:, off, :], ps_u[:, 0:D], t["gate_f"](1), xr[:, off, :],
                                                   ALU.mult, ALU.add).then_inc(final, 1)

                def first():
                    select(0, 0)
                    one_hots(0, 0)
                    select(0, 1)

                def step(i, off, ahead):
                    weigh(i, off)
                    if ahead:
                        one_hots(i, off + 1)
                    if ahead == 2:
                        select(i, off + 2)
                    finish(i, off)

                steps(dve, first, step)


def build(nc, ins, out, debug=None):
    with ExitStack() as ctx:
        def sem(name):
            return ctx.enter_context(nc.semaphore(name))

        memory_of = [ctx.enter_context(nc.sbuf_tensor(n, shape, F32)) for n, shape in (
            ("mk_sb", [P, KC, 2 * MH * NK]), ("scale_sb", [P, KC]), ("offset_sb", [P, KC]))]
        x_life = ctx.enter_context(ExitStack())
        ident = ctx.enter_context(nc.sbuf_tensor("ident_sb", [P, P], F32))
        gates = ctx.enter_context(nc.sbuf_tensor("gates_sb", [P, 4], F32))
        opened = ctx.enter_context(nc.sbuf_tensor("opened_sb", [P, 4], F32))
        x = x_life.enter_context(nc.sbuf_tensor("x_rows", [P, NT, D], F32))
        t = {
            "x": x[:, :, :], "x_in": ins["x"].rearrange("b (q p) d -> p (b q) d", p=P),
            "x_tile": lambda n: x[:, bass.ds(n, 1), :].rearrange("p a d -> p (a d)"),
            "ident": ident, "release_x": x_life.close, "memory": memory_of,
            "x_dram": nc.dram_tensor("x_dram", (NT, P, D), F32, kind="Internal").ap(),
            "xT_dram": nc.dram_tensor("xT_dram", (NT, P, KC, P), F32, kind="Internal").ap(),
            "out_tiles": out.rearrange("b (q p) d -> (b q) p d", p=P),
            "gate_x": lambda layer: opened[:, layer:layer + 1],
            "gate_f": lambda layer: opened[:, 2 + layer:3 + layer],
            "ctx_in": ins["ctx"],
            "ctxT_in": ins["ctxT"].rearrange("b (k p) n -> b p k n", p=P),
            "x_loaded": sem("x_loaded"), "consts": sem("consts"), "consts_n": 32,
            "dve_gate": sem("dve_gate"), "pool_gate": sem("pool_gate"),
            "pe_gate": sem("pe_gate"),
            "k_dram": nc.dram_tensor("k_dram", (B, 3, D, KEYS), BF16, kind="Internal").ap(),
            "q_dram": nc.dram_tensor("q_dram", (B, 3, D, S), BF16, kind="Internal").ap(),
            "v_dram": nc.dram_tensor("v_dram", (B, G, P, KT * HG * DH), F32, kind="Internal").ap(),
            "o_dram": nc.dram_tensor("o_dram", (B, D, S), F32, kind="Internal").ap(),
        }
        for n in ("wq", "wk", "wv", "wo", "wr", "l1_q", "l1_k", "l1_v", "l1_oT"):
            t[n + "_in"] = ins[n].rearrange("(k p) n -> p k n", p=P)
        for n in ("bo", "br", "iota_e", "b1", "b2") + tuple(f"l1_{a}{b}" for a in "qkv" for b in ("a", "bT")):
            t[n + "_in"] = ins[n]
        for n in ("m_wq", "m_keys", "m_gamma", "m_beta", "m_iota", "m_out", "m_iota8"):
            t[n + "_in"] = ins[n]
        t["m_in_in"] = ins["m_in"].rearrange("(k p) y m -> p k y m", p=P)
        t["w1_in"] = ins["w1"].rearrange("e (k p) f -> p e k f", p=P)
        t["w2_in"] = ins["w2"].rearrange("e (c p) d -> p e c d", p=P)
        gates_opened = sem("gates_opened")
        with nc.Block() as block:
            @block.sync
            def _(sp):
                sp.dma_start(ident[:, :], ins["ident"]).then_inc(t["consts"], 16)
                sp.dma_start(gates[:, :], ins["gates"]).then_inc(t["consts"], 16)

            @block.scalar
            def _(act):
                act.wait_ge(t["consts"], 32)
                nc.scalar.activation(opened[:, :], gates[:, :], ACT.Tanh).then_inc(gates_opened, 1)
        project(nc, sem, t)
        attend_heads(nc, sem, t)
        experts(nc, sem, t)
        if debug != 2:
            attend_wide(nc, sem, t)
        if debug is None or debug > 3:
            memory(nc, sem, t, out)
            return
        written = sem("written")
        with nc.Block() as block:
            @block.sync
            def _(sp):
                sp.dma_start(out.rearrange("b (q p) d -> p (b q) d", p=P), x[:, :, :]).then_inc(written, 16)
                sp.wait_ge(written, 16)


def laid_out(inputs):
    import numpy as np
    c = np.ascontiguousarray
    a = {k: np.asarray(v) for k, v in inputs.items()}

    def rows(v):
        return c(np.broadcast_to(v.reshape(1, -1), (P, v.size)))

    r = {
        "x": a["x"],
        "ctx": a["ctx_1024"],
        "ctxT": c(a["ctx_1024"].transpose(0, 2, 1)),
        "wq": c(a["L0_xattn_Wq"].T), "wk": c(a["L0_xattn_Wk"].T), "wv": c(a["L0_xattn_Wv"].T),
        "wo": c(a["L0_xattn_Wo"].T), "bo": rows(a["L0_xattn_bo"]),
        "wr": a["L0_ffn_Wr"], "br": rows(a["L0_ffn_br"]),
        "w1": a["L0_ffn_We1"], "b1": c(a["L0_ffn_be1"].reshape(E * FC, P).T),
        "w2": a["L0_ffn_We2"], "b2": rows(a["L0_ffn_be2"]).reshape(P, E, D),
        "l1_q": a["L1_xattn_Q_weight"], "l1_k": a["L1_xattn_K_weight"], "l1_v": a["L1_xattn_V_weight"],
        "l1_oT": c(a["L1_xattn_O_weight"].T),
        "gates": rows(np.concatenate([a["g_xattn"], a["g_ffn"]])),
        "ident": np.eye(P, dtype=np.float32),
        "iota_e": c(np.broadcast_to(np.arange(E, dtype=np.float32), (P, E))),
    }
    r |= {
        "m_wq": c(a["L1_ffn_w_q"].reshape(2 * MH, KD, D).transpose(1, 0, 2)),
        "m_keys": c(a["L1_ffn_keys"].transpose(3, 2, 0, 1).reshape(KD, 2 * MH, NK)),
        "m_gamma": c(a["L1_ffn_gamma"].reshape(KC, P).T), "m_beta": c(a["L1_ffn_beta"].reshape(KC, P).T),
        "m_in": c(a["L1_ffn_key_in"].reshape(NK, 2, YH, D).transpose(3, 2, 1, 0).reshape(D, YH, P)),
        "m_out": c(a["L1_ffn_key_out"].reshape(NK, 2, YH, D).transpose(1, 0, 2, 3).reshape(P, YH, D)),
        "m_iota": c(np.broadcast_to(np.arange(P, dtype=np.float32), (P, P))),
        "m_iota8": c(np.broadcast_to(np.arange(TOP, dtype=np.float32), (P, TOP))),
    }
    for n in "qkv":
        r[f"l1_{n}a"] = a[f"L1_xattn_{n.upper()}_A"]
        r[f"l1_{n}bT"] = c(a[f"L1_xattn_{n.upper()}_B"].T)
    return r


def kernel(**inputs):
    import concourse.bacc as bacc
    import numpy as np
    from concourse.bass_utils import run_bass_kernel_spmd

    nc = bacc.Bacc("TRN2", target_bir_lowering=False, num_devices=1)
    arrays = laid_out(inputs)
    ins = {n: nc.dram_tensor(n, a.shape, mybir.dt.from_np(a.dtype), kind="ExternalInput").ap() for n, a in arrays.items()}
    out = nc.dram_tensor("out", (B, S, D), F32, kind="ExternalOutput").ap()
    build(nc, ins, out)
    r = run_bass_kernel_spmd(nc, [arrays], core_ids=[0])
    return np.asarray(r.results[0]["out"])
```

```python
from contextlib import ExitStack

import concourse.bass as bass
from concourse import mybir

F32 = mybir.dt.float32
BF16 = mybir.dt.bfloat16
U32 = mybir.dt.uint32
I32 = mybir.dt.int32
ALU = mybir.AluOpType
ACT = mybir.ActivationFunctionType
AX = mybir.AxisListType

P = 128
B, S, D = 8, 512, 256
KEYS = 1601
KC = D // P
QT = S // P
NT = B * QT
KT = -(-KEYS // P)
H, DH = 16, 16
HG = 4
G = H // HG
LN_EPS = 1e-5


def key_rows(kt):
    return min(P, KEYS - kt * P)


def spans(total, width):
    return [(a, min(width, total - a)) for a in range(0, total, width)]


KEY_SPANS = spans(KEYS, 512)


class Own:

    def __init__(self, eng, sem, i=0, per=0):
        self.eng, self.sem, self.base, self.n = eng, sem, i * per, 0

    def then(self, ins):
        self.n += 1
        ins.then_inc(self.sem, 1)
        self.eng.wait_ge(self.sem, self.base + self.n)


def gate(eng, sem):
    eng.sem_inc(sem, 1)


class Stage:

    def __init__(self, nc, name):
        self.nc, self.name, self.ctx = nc, name, ExitStack()

    def __enter__(self):
        return self

    def __exit__(self, *exc):
        return self.ctx.__exit__(*exc)

    def sb(self, name, shape, dt=F32):
        return self.ctx.enter_context(self.nc.sbuf_tensor(f"{self.name}_{name}", shape, dt))

    def ps(self, name, shape, dt=F32):
        return self.ctx.enter_context(self.nc.psum_tensor(f"{self.name}_{name}", shape, dt))


def norm_tiles(nc, dve, own, x, out, stats, mv, ve, rstd, gates, var_ready, sd_ready, sd, done):
    gate(dve, gates)
    for q in range(QT):
        ins = nc.vector.bn_stats(stats[:, q, :], x(q))
    own.then(ins)
    gate(dve, gates)
    for q in range(QT):
        ins = nc.vector.bn_aggr(mv[:, q, :], stats[:, q, :])
    own.then(ins)
    nc.vector.tensor_scalar(ve[:, :], mv[:, :, 1], LN_EPS, None, ALU.add).then_inc(var_ready, 1)
    dve.wait_ge(*sd_ready)
    own.then(nc.vector.reciprocal(rstd[:, :], sd[:, :]))
    for q in range(QT):
        nc.vector.tensor_scalar(out(q), x(q), mv[:, q, 0:1], rstd[:, q:q + 1],
                                ALU.subtract, ALU.mult).then_inc(done, 1)


def project(nc, sem, t):
    PB = 2
    chunks = [("k", m, a, n) for m in range(KC) for a, n in KEY_SPANS] + [("q", m, 0, S) for m in range(KC)]
    NCH, RING = len(chunks), 4
    NKC = KC * len(KEY_SPANS)
    with Stage(nc, "pj") as st:
        ctx = st.sb("ctx", [P, PB, KC, KEYS])
        w = {n: st.sb(n, [P, KC, D]) for n in ("wq", "wk", "wv")}
        xn = st.sb("xn", [P, PB, QT, D])
        xnT = st.sb("xnT", [P, PB, KC, S])
        parts = {"k": st.sb("kp", [P, PB, 3, KC, KEYS], BF16), "q": st.sb("qp", [P, PB, 3, KC, S], BF16)}
        v = st.sb("v", [P, PB, G, KT, HG * DH])
        rest = st.sb("rest", [P, RING, 512])
        stats, mv = st.sb("stats", [P, QT, 6]), st.sb("mv", [P, QT, 2])
        ve, sd, rstd = st.sb("ve", [P, QT]), st.sb("sd", [P, QT]), st.sb("rstd", [P, QT])
        ps_t, ps_c, ps_v = st.ps("pst", [P, KC, 512]), st.ps("psc", [P, RING, 512]), st.ps("psv", [P, 2, 512])

        weights, ctx_in, ctx_used = sem("pj_weights"), [sem("pj_ctx0"), sem("pj_ctx1")], sem("pj_ctx_used")
        own, normed, var, sdr = sem("pj_dve_own"), sem("pj_normed"), sem("pj_var"), sem("pj_sd")
        turned, xnT_ready = sem("pj_turned"), sem("pj_xnT")
        mm, first, left, second, third = (sem(f"pj_{n}") for n in ("mm", "part1", "rest", "part2", "part3"))
        v_mm, v_out, stored = sem("pj_v_mm"), sem("pj_v_out"), [sem("pj_stored0"), sem("pj_stored1")]
        v_clear = sem("pj_v_clear")
        NSTORE = 3 + 3 + 1

        def out_of(parts_of, s, part, m, a, n):
            return parts[parts_of][:, s, part, m, a:a + n]

        with nc.Block() as block:
            @block.sync
            def _(sp):
                sp.dma_start(t["x"], t["x_in"]).then_inc(t["x_loaded"], 16)
                for n in ("wq", "wk", "wv"):
                    sp.dma_start(w[n][:, :, :], t[n + "_in"]).then_inc(weights, 16)
                for s in range(PB):
                    sp.sem_inc(stored[s], 1)
                    sp.dma_start(ctx[:, s, :, :], t["ctxT_in"][s]).then_inc(ctx_in[s], 16)

                def step(i, s, load):
                    b = i * PB + s
                    sp.wait_ge(third, (b + 1) * NCH)
                    sp.wait_ge(v_out, (b + 1) * KT + 2)
                    for part in range(3):
                        sp.dma_start(t["k_dram"][b, part].rearrange("(m p) n -> p m n", p=P),
                                     parts["k"][:, s, part, :, :]).then_inc(stored[s], 16)
                        sp.dma_start(t["q_dram"][b, part].rearrange("(m p) n -> p m n", p=P),
                                     parts["q"][:, s, part, :, :]).then_inc(stored[s], 16)
                    sp.dma_start(t["v_dram"][b].rearrange("g p n -> p g n"),
                                 v[:, s, :, :, :].rearrange("p g k c -> p g (k c)")).then_inc(stored[s], 16)
                    if load:
                        sp.wait_ge(ctx_used, b + 1)
                        sp.dma_start(ctx[:, s, :, :], t["ctxT_in"][b + PB]).then_inc(ctx_in[s], 16)

                with sp.Fori(0, B // PB - 1) as i:
                    for s in range(PB):
                        step(i, s, True)
                for s in range(PB):
                    step(B // PB - 1, s, False)
                for s in range(PB):
                    sp.wait_ge(stored[s], 1 + 16 * NSTORE * (B // PB))

            @block.tensor
            def _(pe):
                pe.wait_ge(weights, 48)
                pe.wait_ge(t["consts"], t["consts_n"])
                with pe.Fori(0, B // PB) as i:
                    for s in range(PB):
                        b = i * PB + s
                        pe.wait_ge(ctx_in[s], i * 16 + 16)
                        for c, (what, m, a, n) in enumerate(chunks[:NKC]):
                            pe.wait_ge(left, b * NCH + c + 1)
                            for k in range(KC):
                                ins = nc.tensor.matmul(ps_c[:, (NCH * s + c) % RING, 0:n], w["wk"][:, k, m * P:m * P + P],
                                                       ctx[:, s, k, a:a + n], start=k == 0, stop=k == KC - 1)
                            ins.then_inc(mm, 1)
                        for kt in range(KT):
                            r = key_rows(kt)
                            pe.wait_ge(v_out, b * KT + kt + 1)
                            for k in range(KC):
                                ins = nc.tensor.matmul(ps_v[0:r, (KT * s + kt) % 2, 0:D], ctx[:, s, k, kt * P:kt * P + r],
                                                       w["wv"][:, k, :], start=k == 0, stop=k == KC - 1)
                            ins.then_inc(v_mm, 1)
                        pe.wait_ge(v_mm, (b + 1) * KT)
                        pe.sem_inc(ctx_used, 1)
                        pe.wait_ge(normed, (b + 1) * QT)
                        pe.wait_ge(xnT_ready, b + 1)
                        for q in range(QT):
                            for k in range(KC):
                                ins = nc.tensor.transpose(ps_t[:, k, q * P:q * P + P],
                                                          xn[:, s, q, k * P:k * P + P], t["ident"][:, :])
                        ins.then_inc(turned, 1)
                        pe.wait_ge(xnT_ready, b + 2)
                        for c, (what, m, a, n) in list(enumerate(chunks))[NKC:]:
                            pe.wait_ge(left, b * NCH + c + 1)
                            for k in range(KC):
                                ins = nc.tensor.matmul(ps_c[:, (NCH * s + c) % RING, 0:n], w["wq"][:, k, m * P:m * P + P],
                                                       xnT[:, s, k, :], start=k == 0, stop=k == KC - 1)
                            ins.then_inc(mm, 1)

            @block.scalar
            def _(act):
                act.sem_inc(v_out, 2)
                act.wait_ge(v_clear, 1)
                with act.Fori(0, B // PB) as i:
                    for s in range(PB):
                        b = i * PB + s

                        def part1(c):
                            what, m, a, n = chunks[c]
                            act.wait_ge(mm, b * NCH + c + 1)
                            nc.scalar.activation(out_of(what, s, 0, m, a, n), ps_c[:, (NCH * s + c) % RING, 0:n],
                                                 ACT.Copy).then_inc(first, 1)

                        def part2(c):
                            what, m, a, n = chunks[c]
                            act.wait_ge(left, b * NCH + c + 1 + RING)
                            nc.scalar.activation(out_of(what, s, 1, m, a, n), rest[:, (NCH * s + c) % RING, 0:n],
                                                 ACT.Copy).then_inc(second, 1)

                        act.wait_ge(var, b + 1)
                        nc.scalar.activation(sd[:, :], ve[:, :], ACT.Sqrt).then_inc(sdr, 1)
                        act.wait_ge(stored[s], i * 16 * NSTORE + 1)
                        for c in range(NKC):
                            part1(c)
                            if c:
                                part2(c - 1)
                        part2(NKC - 1)
                        for kt in range(KT):
                            r = key_rows(kt)
                            act.wait_ge(v_mm, b * KT + kt + 1)
                            nc.scalar.activation(v[0:r, s, :, kt, :],
                                                 ps_v[0:r, (KT * s + kt) % 2, 0:D].rearrange("p (g c) -> p g c", g=G),
                                                 ACT.Copy).then_inc(v_out, 1)
                        for c in range(NKC, NCH):
                            part1(c)
                            if c > NKC:
                                part2(c - 1)
                        part2(NCH - 1)

            @block.vector
            def _(dve):
                nc.vector.memset(v[:, :, :, KT - 1, :], 0.0).then_inc(v_clear, 1)
                dve.sem_inc(left, RING)
                dve.sem_inc(xnT_ready, 1)
                dve.wait_ge(t["x_loaded"], 16)
                with dve.Fori(0, B // PB) as i:
                    for s in range(PB):
                        b = i * PB + s
                        me = Own(dve, own, b, 3)

                        def subtract1(c):
                            what, m, a, n = chunks[c]
                            dve.wait_ge(first, b * NCH + c + 1)
                            nc.vector.tensor_tensor(rest[:, (NCH * s + c) % RING, 0:n], ps_c[:, (NCH * s + c) % RING, 0:n],
                                                    out_of(what, s, 0, m, a, n), ALU.subtract).then_inc(left, 1)

                        def subtract2(c):
                            what, m, a, n = chunks[c]
                            dve.wait_ge(second, b * NCH + c + 1)
                            nc.vector.tensor_tensor(out_of(what, s, 2, m, a, n), rest[:, (NCH * s + c) % RING, 0:n],
                                                    out_of(what, s, 1, m, a, n), ALU.subtract).then_inc(third, 1)

                        norm_tiles(nc, dve, me, lambda q: t["x_tile"](b * QT + q), lambda q: xn[:, s, q, :],
                                   stats, mv, ve, rstd, t["dve_gate"], var, (sdr, b + 1), sd, normed)
                        for c in range(NKC):
                            subtract1(c)
                            if c:
                                subtract2(c - 1)
                        subtract2(NKC - 1)
                        dve.wait_ge(turned, b + 1)
                        nc.vector.tensor_copy(xnT[:, s, :, :], ps_t[:, :, :]).then_inc(xnT_ready, 1)
                        for c in range(NKC, NCH):
                            subtract1(c)
                            if c > NKC:
                                subtract2(c - 1)
                        subtract2(NCH - 1)


Q_PART = [0, 1, 0, 2, 0, 1]
K_PART = [0, 0, 1, 0, 2, 1]
TERMS = DH * len(Q_PART)
STACK = TERMS + 3


def attend_heads(nc, sem, t):
    SLOTS = G
    PRING, SBANKS, MBANKS = 8, 3, 2
    NST = KT * HG
    max_jobs = [(j, q, h) for j in range(HG) for q in range(QT) for h in range(2)]
    HALF = 1024
    SCALE = 1.0 / float(D) ** 0.5
    UNITS = B * G
    NLOAD = 2 * len(Q_PART) + 1
    with Stage(nc, "at") as st:
        ks, qs = st.sb("ks", [STACK, SLOTS, HG, KEYS], BF16), st.sb("qs", [STACK, SLOTS, HG, S], BF16)
        vd = st.sb("vd", [P, 2, KT * HG, DH])
        vw = st.sb("vw", [P, 2, KT * HG, 2 * DH])
        pr = st.sb("pr", [P, PRING, S])
        pmax, nmax = st.sb("pmax", [P, HG * QT, 2]), st.sb("nmax", [P, HG * QT])
        mrest, mpart = st.sb("mrest", [HG * QT, 2, P]), st.sb("mpart", [HG * QT, 3, P], BF16)
        acc, den, o = st.sb("acc", [P, S]), st.sb("den", [P, 2, S]), st.sb("o", [P, S])
        ps_s, ps_m, ps_o = st.ps("pss", [P, SBANKS, 512]), st.ps("psm", [P, MBANKS, HALF]), st.ps("pso", [P, 512])

        kq_in, v_in = [sem(f"at_kq{s}") for s in range(SLOTS)], [sem(f"at_v{s}") for s in range(2)]
        kq_used, v_used, v_wide = sem("at_kq_used"), sem("at_v_used"), sem("at_v_wide")
        v_dense_used, v_ones = sem("at_v_dense_used"), sem("at_v_ones")
        s_mm, expd, pv = sem("at_scores"), sem("at_exp"), sem("at_pv")
        m_mm, m_red, m_all, m_turned, m_parts, m_in = (sem(f"at_max_{n}") for n in ("mm", "red", "all", "turned", "parts", "in"))
        own, acc_out, o_ready, o_stored, ones = (sem(f"at_{n}") for n in ("own", "acc_out", "o_ready", "o_stored", "ones"))
        OWN = 6

        with nc.Block() as block:
            @block.sync
            def _(sp):
                def load(b, g):
                    u, v_slot = b * G + g, g % 2
                    sp.wait_ge(kq_used, u + 1)
                    for n, (kp, qp) in enumerate(zip(K_PART, Q_PART)):
                        rows = slice(g * HG * DH, (g + 1) * HG * DH)
                        sp.dma_start(ks[n * DH:(n + 1) * DH, g, :, :],
                                     t["k_dram"][b, kp, rows].rearrange("(j d) n -> d j n", d=DH)).then_inc(kq_in[g], 16)
                        sp.dma_start(qs[n * DH:(n + 1) * DH, g, :, :],
                                     t["q_dram"][b, qp, rows].rearrange("(j d) n -> d j n", d=DH)).then_inc(kq_in[g], 16)
                    sp.wait_ge(v_dense_used, u + 1)
                    sp.dma_start(vd[:, v_slot, :, :].rearrange("p a c -> p (a c)"), t["v_dram"][b, g]).then_inc(v_in[v_slot], 16)

                def rows_out(b, g):
                    u = b * G + g
                    sp.wait_ge(m_parts, u + 2)
                    for part in range(3):
                        sp.dma_start(qs[TERMS + part:TERMS + part + 1, g, :, :].rearrange("p j (q n) -> p (j q) n", n=P),
                                     mpart[:, part, :]).then_inc(m_in, 16)

                def heads_out(b, g):
                    sp.wait_ge(o_ready, b * G + g + 2)
                    for j in range(HG):
                        sp.dma_start(t["o_dram"][b, (g * HG + j) * DH:(g * HG + j + 1) * DH],
                                     o[j * 32:j * 32 + DH, :]).then_inc(o_stored, 16)

                def step(b, g, last):
                    if not last or g == 0:
                        load(*((b, 3) if g == 0 else (b + 1, g - 1)))
                    if not last or g + 1 < G:
                        rows_out(*((b, g + 1) if g + 1 < G else (b + 1, 0)))
                    heads_out(b, g)

                sp.sem_inc(m_in, 1)
                sp.sem_inc(o_stored, 1)
                for g in range(G - 1):
                    load(0, g)
                rows_out(0, 0)
                with sp.Fori(0, B - 1) as b:
                    for g in range(G):
                        step(b, g, False)
                for g in range(G):
                    step(B - 1, g, True)
                sp.wait_ge(o_stored, 1 + UNITS * HG * 16)

            @block.tensor
            def _(pe):
                pe.sem_inc(kq_used, SLOTS)
                pe.sem_inc(pv, PRING)
                pe.wait_ge(ones, 1)

                def max_product(b, g, u, n):
                    j, q, h = max_jobs[n]
                    if n == 0:
                        pe.wait_ge(kq_in[g], b * 16 * (NLOAD - 1) + 16 * (NLOAD - 1))
                        pe.wait_ge(m_parts, u + 1)
                    pe.wait_ge(m_red, u * len(max_jobs) + n + 1)
                    for a, w in spans(HALF if h == 0 else KEYS - HALF, 512):
                        ins = nc.tensor.matmul(ps_m[:, h, a:a + w], qs[0:TERMS, g, j, q * P:q * P + P],
                                               ks[0:TERMS, g, j, h * HALF + a:h * HALF + a + w], start=True, stop=True)
                    ins.then_inc(m_mm, 1)

                def turn_max(u):
                    pe.wait_ge(m_all, u + 1)
                    nc.tensor.transpose(ps_m[0:HG * QT, 0, 0:P], nmax[:, :], t["ident"][:, :]).then_inc(m_turned, 1)

                def scores(u, g, n):
                    kt, j = n // HG, n % HG
                    r = key_rows(kt)
                    pe.wait_ge(expd, u * NST + n + 1 + (SBANKS - 1 if g == n == 0 else 0))
                    nc.tensor.matmul(ps_s[0:r, (NST * g + n) % SBANKS, :], ks[:, g, j, kt * P:kt * P + r], qs[:, g, j, :],
                                     start=True, stop=True).then_inc(s_mm, 1)

                def values(u, g, n):
                    kt, j = n // HG, n % HG
                    r = key_rows(kt)
                    pe.wait_ge(expd, u * NST + n + 1 + SBANKS)
                    nc.tensor.matmul(ps_o[j * 32:(j + 1) * 32, :], vw[0:r, g % 2, kt * HG + j, :],
                                     pr[0:r, (NST * g + n) % PRING, :], start=kt == 0, stop=kt == KT - 1).then_inc(pv, 1)

                def unit(b, g, nxt):
                    u = b * G + g
                    pe.wait_ge(m_in, u * 48 + 49)
                    done = 0
                    for kt in range(KT + 1):
                        for j in range(HG):
                            if kt < KT:
                                scores(u, g, kt * HG + j)
                            if nxt is not None and j in (0, 2) or kt == KT:
                                todo = min(len(max_jobs), -(-len(max_jobs) * (2 * kt + j // 2 + 1) // (2 * KT - 3)))
                                while nxt is not None and done < todo:
                                    max_product(nxt[0], nxt[1], nxt[0] * G + nxt[1], done)
                                    done += 1
                        if nxt is not None and kt == KT - 1:
                            turn_max(nxt[0] * G + nxt[1])
                        if kt == 1:
                            pe.wait_ge(v_wide, u + 1)
                            pe.wait_ge(acc_out, u + 1)
                        if kt:
                            for j in range(HG):
                                values(u, g, (kt - 1) * HG + j)
                    pe.wait_ge(pv, (u + 1) * NST + PRING)
                    pe.sem_inc(kq_used, 1)
                    pe.sem_inc(v_used, 1)

                for n in range(len(max_jobs)):
                    max_product(0, 0, 0, n)
                turn_max(0)
                with pe.Fori(0, B - 1) as b:
                    for g in range(G):
                        unit(b, g, (b, g + 1) if g + 1 < G else (b + 1, 0))
                for g in range(G):
                    unit(B - 1, g, (B - 1, g + 1) if g + 1 < G else None)

            @block.scalar
            def _(act):
                act.sem_inc(expd, SBANKS)
                with act.Fori(0, B) as b:
                    for g in range(G):
                        for n in range(NST):
                            u, r = b * G + g, key_rows(n // HG)
                            act.wait_ge(pv, u * NST + n + 1)
                            act.wait_ge(s_mm, u * NST + n + 1)
                            nc.scalar.activation(pr[0:r, (NST * g + n) % PRING, :], ps_s[0:r, (NST * g + n) % SBANKS, :],
                                                 ACT.Exp, scale=SCALE).then_inc(expd, 1)

            @block.vector
            def _(dve):
                nc.vector.memset(ks[TERMS:STACK, :, :, :], 1.0).then_inc(ones, 1)
                dve.sem_inc(m_red, MBANKS)
                for credit in (acc_out, m_parts, o_ready):
                    dve.sem_inc(credit, 1)

                def maxima(u, me):
                    for n, (j, q, h) in enumerate(max_jobs):
                        w = HALF if h == 0 else KEYS - HALF
                        dve.wait_ge(m_mm, u * len(max_jobs) + n + 1)
                        nc.vector.tensor_reduce(pmax[:, j * QT + q, h:h + 1], ps_m[:, h, 0:w], AX.X, ALU.max).then_inc(m_red, 1)
                    dve.wait_ge(m_red, (u + 1) * len(max_jobs) + MBANKS)
                    nc.vector.tensor_reduce(nmax[:, :], pmax[:, :, :], AX.X, ALU.max, negate=True).then_inc(m_all, 1)
                    dve.wait_ge(m_turned, u + 1)
                    dve.wait_ge(m_in, u * 48 + 1)
                    me.then(nc.vector.tensor_copy(mpart[:, 0, :], ps_m[0:HG * QT, 0, 0:P]))
                    me.then(nc.vector.tensor_tensor(mrest[:, 0, :], ps_m[0:HG * QT, 0, 0:P], mpart[:, 0, :], ALU.subtract))
                    me.then(nc.vector.tensor_copy(mpart[:, 1, :], mrest[:, 0, :]))
                    nc.vector.tensor_tensor(mpart[:, 2, :], mrest[:, 0, :], mpart[:, 1, :], ALU.subtract).then_inc(m_parts, 1)

                def finish(u, me):
                    dve.wait_ge(o_ready, u + 1)
                    dve.wait_ge(pv, (u + 1) * NST + PRING)
                    nc.vector.tensor_copy(acc[:, :], ps_o[:, :]).then_inc(acc_out, 1)
                    dve.wait_ge(acc_out, u + 2)
                    gate(dve, t["dve_gate"])
                    me.then(nc.vector.stream_shuffle(den[:, 0, :], acc[:, :], [DH + r % DH for r in range(32)]))
                    me.then(nc.vector.reciprocal(den[:, 1, :], den[:, 0, :]))
                    dve.wait_ge(o_stored, u * 16 * HG + 1)
                    nc.vector.tensor_tensor(o[:, :], acc[:, :], den[:, 1, :], ALU.mult).then_inc(o_ready, 1)

                maxima(0, Own(dve, own))
                with dve.Fori(0, B - 1) as b:
                    for g in range(G):
                        u = b * G + g
                        me = Own(dve, own, u, 5)
                        me.n = 3
                        maxima(u + 1, me)
                        finish(u, me)
                for g in range(G):
                    u = (B - 1) * G + g
                    me = Own(dve, own, u, 5)
                    me.n = 3
                    if g + 1 < G:
                        maxima(u + 1, me)
                    finish(u, me)

            @block.gpsimd
            def _(pool):
                nc.gpsimd.memset(vw[:, :, :, :], 1.0).then_inc(v_ones, 1)
                pool.sem_inc(v_used, 2)
                pool.sem_inc(v_dense_used, 2)
                pool.wait_ge(v_ones, 1)

                def spread(b, g):
                    u = b * G + g
                    pool.wait_ge(v_in[g % 2], (b * 2 + g // 2 + 1) * 16)
                    pool.wait_ge(v_used, u + 1)
                    gate(pool, t["pool_gate"])
                    nc.gpsimd.tensor_copy(vw[:, g % 2, :, 0:DH], vd[:, g % 2, :, :]).then_inc(v_wide, 1)
                    pool.wait_ge(v_wide, u + 1)
                    pool.sem_inc(v_dense_used, 1)

                spread(0, 0)
                with pool.Fori(0, B - 1) as b:
                    for g in range(G):
                        spread(*((b, g + 1) if g + 1 < G else (b + 1, 0)))
                for g in range(1, G):
                    spread(B - 1, g)


E = 4
F = 4 * D
FC = F // P
TOK = 256
TQ = TOK // P
FULL_BLOCKS = B * S // TOK
MAX_BLOCKS = FULL_BLOCKS + E - 1
REGION = B * S + TOK


def route(nc, sem, t, st):
    NW = 6
    NOWN = 9
    with Stage(nc, "rt") as st_r:
        sb, ps = st_r.sb, st_r.ps
        oT = sb("oT", [P, 2, KC, S])
        wo, bo, one_row = sb("wo", [P, KC, D]), sb("bo", [1, D]), sb("one_row", [1, P])
        wr, br, iota = sb("wr", [P, KC, E]), sb("br", [P, E]), sb("iota", [P, E])
        base0, before_f = sb("base0", [P, E]), sb("before_f", [P, P])
        before, ones = sb("before", [P, P], BF16), sb("ones", [P, P], BF16)
        xn, xnT = sb("xn", [P, 2, QT, D]), sb("xnT", [P, KC, S])
        stats, mv = sb("stats", [P, QT, 6]), sb("mv", [P, QT, 2])
        ve, sd, rstd = sb("ve", [P, QT]), sb("sd", [P, QT]), sb("rstd", [P, QT])
        logit, top, at = sb("logit", [P, QT, 8]), sb("top", [P, QT, 8]), sb("at", [P, QT, 8], U32)
        atf, hot = sb("atf", [P, QT]), sb("hot", [P, QT + 1, E], BF16)
        place, slotf, slot = sb("place", [P, QT, E]), sb("slotf", [P, QT]), sb("slot", [P, 2, QT], U32)
        base, zeros = sb("base", [P, E]), sb("zeros", [P, TQ, D])
        rows, back = sb("rows", [P, 2, NT]), sb("back", [P, 2, NT])
        moved, step_ = sb("moved", [P, E]), sb("step", [P, E])
        count, blocks, blocks_u = sb("count", [P, E]), sb("blocks", [P, 1 + E]), sb("blocks_u", [P, E], U32)
        ps_o, ps_t = ps("pso", [P, 2, QT, D]), ps("pst", [P, KC, 512])
        ps_l, ps_r = ps("psl", [P, 512]), ps("psr", [P, 512])

        w_in, made, o_in = sem("rt_w"), sem("rt_made"), [sem("rt_o0"), sem("rt_o1")]
        projected, taken = sem("rt_projected"), sem("rt_taken")
        own_a, own_b, normed, var, sdr = sem("rt_own_a"), sem("rt_own_b"), sem("rt_normed"), sem("rt_var"), sem("rt_sd")
        turned, xnT_ready, routed, hot_ready = sem("rt_turned"), sem("rt_xnT"), sem("rt_routed"), sem("rt_hot")
        ranked, placed, scattered, xn_free = sem("rt_ranked"), sem("rt_placed"), sem("rt_scattered"), sem("rt_xn_free")
        counted, tailed = sem("rt_counted"), sem("rt_tailed")

        def steps(eng, first, step):
            first()
            with eng.Fori(0, B // 2 - 1) as i:
                for s in range(2):
                    step(i * 2 + s, s, True)
            step(B - 2, 0, True)
            step(B - 1, 1, False)

        with nc.Block() as block:
            @block.sync
            def _(sp):
                for dst, name in ((wo, "wo"), (bo, "bo"), (wr, "wr"), (br, "br"), (iota, "iota_e"), (base0, "base0"),
                                  (before_f, "before")):
                    sp.dma_start(dst.ap(), t[name + "_in"]).then_inc(w_in, 16)
                sp.wait_ge(counted, 1)
                for n in range(FULL_BLOCKS, MAX_BLOCKS):
                    sp.dma_start(t["ys_dram"][n].rearrange("(k p) d -> p k d", p=P), zeros[:, :, :]).then_inc(tailed, 16)

                def heads_in(b, s):
                    sp.dma_start(oT[:, s, :, :], t["o_dram"][b].rearrange("(k p) n -> p k n", p=P)).then_inc(o_in[s], 16)

                heads_in(0, 0)
                heads_in(1, 1)
                for e in range(E):
                    sp.dma_start(st["w1"][:, e, :, :], t["w1_in"][:, e]).then_inc(st["w_in"], 16)
                    sp.dma_start(st["w2"][:, e, :, :], t["w2_in"][:, e]).then_inc(st["w_in"], 16)
                sp.dma_start(st["b1"][:, :], t["b1_in"]).then_inc(st["w_in"], 16)
                sp.dma_start(st["b2"][:, :, :], t["b2_in"]).then_inc(st["w_in"], 16)
                with sp.Fori(1, B // 2) as i:
                    for s in range(2):
                        sp.wait_ge(projected, i * 2 + s - 1)
                        heads_in(i * 2 + s, s)
                sp.wait_ge(counted, 2)
                for e in range(E):
                    n = sp.value_load(st["table"][0:1, 1 + E + e:2 + E + e], min_val=0, max_val=B * S)
                    sp.dma_start(t["xs_dram"][e, bass.ds(n, TOK)].rearrange("(k p) d -> p k d", p=P),
                                 zeros[:, :, :]).then_inc(tailed, 16)
                sp.wait_ge(tailed, 16 * (E + MAX_BLOCKS - FULL_BLOCKS))

            @block.tensor
            def _(pe):
                pe.wait_ge(w_in, 16 * (NW + 1))
                pe.wait_ge(made, 3)

                def project_heads(b, s):
                    pe.wait_ge(o_in[s], (b - s) * 8 + 16)
                    pe.wait_ge(taken, b + 1)
                    for q in range(QT):
                        for k in range(KC):
                            nc.tensor.matmul(ps_o[:, s, q, :], oT[:, s, k, q * P:q * P + P], wo[:, k, :],
                                             start=k == 0, stop=False)
                        ins = nc.tensor.matmul(ps_o[:, s, q, :], one_row[:, :], bo[:, :], start=False, stop=True)
                    ins.then_inc(projected, 1)

                def step(b, s, ahead):
                    if ahead:
                        project_heads(b + 1, 1 - s)
                    pe.wait_ge(normed, (b + 1) * QT)
                    pe.wait_ge(xnT_ready, b + 1)
                    for q in range(QT):
                        for k in range(KC):
                            ins = nc.tensor.transpose(ps_t[:, k, q * P:q * P + P], xn[:, s, q, k * P:k * P + P],
                                                      t["ident"][:, :])
                    ins.then_inc(turned, 1)
                    pe.wait_ge(xnT_ready, b + 2)
                    for q in range(QT):
                        for k in range(KC):
                            ins = nc.tensor.matmul(ps_l[:, q * E:q * E + E], xnT[:, k, q * P:q * P + P], wr[:, k, :],
                                                   start=k == 0, stop=k == KC - 1)
                    ins.then_inc(routed, 1)
                    pe.wait_ge(hot_ready, b + 2)
                    pe.wait_ge(placed, b + 1)
                    nc.tensor.matmul(ps_r[:, 0:(QT + 1) * E], before[:, :], hot[:, :, :].rearrange("p q e -> p (q e)"),
                                     start=True, stop=False)
                    for q in range(QT):
                        ins = nc.tensor.matmul(ps_r[:, (q + 1) * E:(QT + 1) * E].rearrange("p (q e) -> p q e", e=E),
                                               ones[:, :], hot[:, q:q + 1, :].broadcast_to([P, QT - q, E]),
                                               start=False, stop=q == QT - 1)
                    ins.then_inc(ranked, 1)

                steps(pe, lambda: project_heads(0, 0), step)

            @block.scalar
            def _(act):
                def root(b):
                    act.wait_ge(var, b + 1)
                    nc.scalar.activation(sd[:, :], ve[:, :], ACT.Sqrt).then_inc(sdr, 1)

                def step(b, s, ahead):
                    act.wait_ge(turned, b + 1)
                    act.wait_ge(routed, b + 1)
                    nc.scalar.activation(xnT[:, :, :], ps_t[:, :, :], ACT.Copy).then_inc(xnT_ready, 1)
                    if ahead:
                        root(b + 1)

                act.sem_inc(xnT_ready, 1)
                act.sem_inc(routed, 1)
                steps(act, lambda: root(0), step)

            @block.vector
            def _(dve):
                nc.vector.memset(logit[:, :, :], -3.0e38)
                nc.vector.memset(back[:, :, :], 0.0)
                nc.vector.memset(hot[:, :, :], 0.0).then_inc(hot_ready, 1)
                nc.vector.memset(one_row[:, :], 1.0).then_inc(made, 1)
                nc.vector.memset(ones[:, :], 1.0).then_inc(made, 1)
                dve.wait_ge(hot_ready, 1)
                dve.wait_ge(w_in, 16 * (NW + 1))
                nc.vector.tensor_copy(base[:, :], base0[:, :])
                nc.vector.tensor_copy(before[:, :], before_f[:, :]).then_inc(made, 1)
                dve.wait_ge(made, 3)
                dve.sem_inc(taken, 2)
                dve.sem_inc(placed, 1)

                def residual(b, s):
                    me = Own(dve, own_a, b, 4)
                    tiles = t["x"][:, bass.ds(b * QT, QT), :]
                    dve.wait_ge(projected, b + 1)
                    me.then(nc.vector.scalar_tensor_tensor(tiles, ps_o[:, s, :, :], t["gate_x"](0), tiles,
                                                           ALU.mult, ALU.add))
                    dve.sem_inc(taken, 1)
                    dve.wait_ge(xn_free, b + 1)
                    norm_tiles(nc, dve, me, lambda q: t["x_tile"](b * QT + q), lambda q: xn[:, s, q, :],
                               stats, mv, ve, rstd, t["dve_gate"], var, (sdr, b + 1), sd, normed)
                    assert me.n == 4, me.n

                def step(b, s, ahead):
                    if ahead:
                        residual(b + 1, 1 - s)
                    me = Own(dve, own_b, b, NOWN)
                    dve.wait_ge(routed, b + 2)
                    me.then(nc.vector.tensor_tensor(logit[:, :, 0:E], ps_l[:, 0:QT * E].rearrange("p (q e) -> p q e", e=E),
                                                    br[:, :].unsqueeze(1).broadcast_to([P, QT, E]), ALU.add))
                    gate(dve, t["dve_gate"])
                    for q in range(QT):
                        ins = nc.vector.max(top[:, q, :], logit[:, q, :])
                    me.then(ins)
                    gate(dve, t["dve_gate"])
                    for q in range(QT):
                        ins = nc.vector.max_index(at[:, q, :], top[:, q, :], logit[:, q, :])
                    me.then(ins)
                    me.then(nc.vector.tensor_copy(atf[:, :], at[:, :, 0]))
                    nc.vector.tensor_tensor(hot[:, 0:QT, :], iota[:, :].unsqueeze(1).broadcast_to([P, QT, E]),
                                            atf[:, :].unsqueeze(2).broadcast_to([P, QT, E]), ALU.is_equal).then_inc(hot_ready, 1)
                    dve.wait_ge(ranked, b + 1)
                    me.then(nc.vector.tensor_tensor(place[:, :, :], ps_r[:, 0:QT * E].rearrange("p (q e) -> p q e", e=E),
                                                    base[:, :].unsqueeze(1).broadcast_to([P, QT, E]), ALU.add))
                    me.then(nc.vector.tensor_tensor(place[:, :, :], place[:, :, :], hot[:, 0:QT, :], ALU.mult))
                    me.then(nc.vector.tensor_tensor(base[:, :], base[:, :], ps_r[:, QT * E:(QT + 1) * E], ALU.add))
                    me.then(nc.vector.tensor_reduce(slotf[:, :], place[:, :, :], AX.X, ALU.add))
                    nc.vector.tensor_copy(slot[:, s, :], slotf[:, :])
                    me.then(nc.vector.tensor_copy(rows[:, 0, bass.ds(b * QT, QT)], slotf[:, :]))
                    dve.sem_inc(placed, 1)

                steps(dve, lambda: residual(0, 0), step)
                me = Own(dve, own_b, B, NOWN)
                me.then(nc.vector.tensor_tensor(count[:, :], base[:, :], base0[:, :], ALU.subtract))
                me.then(nc.vector.tensor_scalar(blocks_u[:, :], count[:, :], float(TOK - 1), None, ALU.add))
                me.then(nc.vector.tensor_scalar(blocks_u[:, :], blocks_u[:, :], TOK.bit_length() - 1, None,
                                                ALU.logical_shift_right))
                me.then(nc.vector.memset(blocks[:, 0:1], 0.0))
                me.then(nc.vector.tensor_copy(blocks[:, 1:1 + E], blocks_u[:, :]))
                me.then(nc.vector.tensor_scalar(blocks[:, 1:1 + E], blocks[:, 1:1 + E], 1.0, None, ALU.max))
                for e in range(1, E):
                    me.then(nc.vector.tensor_tensor(blocks[:, 1 + e:2 + e], blocks[:, 1 + e:2 + e], blocks[:, e:e + 1], ALU.add))
                nc.vector.tensor_copy(st["table"][:, 0:1 + E], blocks[:, :])
                me.then(nc.vector.scalar_tensor_tensor(moved[:, :], blocks[:, 0:E], -float(TOK), base0[:, :], ALU.mult, ALU.add))
                me.then(nc.vector.tensor_tensor(step_[:, 1:E], moved[:, 1:E], moved[:, 0:E - 1], ALU.subtract))
                for e in range(1, E):
                    me.then(nc.vector.tensor_scalar(rows[:, 1, :], rows[:, 0, :], float(e * REGION), step_[:, e:e + 1],
                                                    ALU.is_ge, ALU.mult))
                    me.then(nc.vector.tensor_tensor(back[:, e % 2, :], rows[:, 1, :], back[:, 1 - e % 2, :], ALU.add))
                nc.vector.tensor_tensor(t["slots"][:, :], rows[:, 0, :], back[:, (E - 1) % 2, :], ALU.subtract)
                nc.vector.tensor_copy(st["table"][:, 1 + E:1 + 2 * E], count[:, :]).then_inc(counted, 1)

            @block.gpsimd
            def _(pool):
                nc.gpsimd.memset(zeros[:, :, :], 0.0).then_inc(counted, 1)
                pool.sem_inc(xn_free, 2)

                def step(b, s, ahead):
                    pool.wait_ge(placed, b + 2)
                    gate(pool, t["pool_gate"])
                    for q in range(QT):
                        nc.gpsimd.indirect_dma_start(
                            out=t["xs_rows"], out_offset=bass.IndirectOffsetOnAxis(ap=slot[:, s, q:q + 1], axis=0),
                            in_=xn[:, s, q, :], in_offset=None).then_inc(scattered, 16)
                    pool.wait_ge(scattered, b * 16 * QT + 16 * QT)
                    pool.sem_inc(xn_free, 1)

                steps(pool, lambda: None, step)


def experts(nc, sem, t):
    with Stage(nc, "ex") as stage:
        w1, b1 = stage.sb("w1", [P, E, KC, F]), stage.sb("b1", [P, E * FC])
        w2, b2 = stage.sb("w2", [P, E, FC, D]), stage.sb("b2", [P, E, D])
        table = stage.sb("table", [P, 1 + 2 * E], I32)
        w_in = sem("ex_w")
        route(nc, sem, t, {"w1": w1, "b1": b1, "w2": w2, "b2": b2, "table": table, "w_in": w_in})

        xs, xsT = stage.sb("xs", [P, TQ, D]), stage.sb("xsT", [P, KC, TOK])
        hid, y = stage.sb("hid", [P, FC, TOK]), stage.sb("y", [P, TQ, D])
        HB = 4
        ps_h, ps_o, ps_t = stage.ps("psh", [P, HB, 512]), stage.ps("pso", [P, TQ, 512]), stage.ps("pst", [P, KC, TOK])
        xs_in, turned, xsT_ready = sem("ex_xs"), sem("ex_turned"), sem("ex_xsT")
        up, relud, down, y_ready, y_stored = sem("ex_up"), sem("ex_relu"), sem("ex_down"), sem("ex_y"), sem("ex_stored")

        def starts(eng):
            return [eng.value_load(table[0:1, e:e + 1], min_val=0 if e == 0 else e, max_val=MAX_BLOCKS)
                    for e in range(E + 1)]

        def rows_of(dram, e, n, first):
            row = nc.s_assert_within((n - first) * TOK, 0, REGION - TOK, skip_runtime_bounds_check_because=
                                     "an expert has at most B * S tokens, so n - first <= B * S / TOK")
            return dram[e, bass.ds(row, TOK)].rearrange("(k p) d -> p k d", p=P)

        with nc.Block() as block:
            @block.sync
            def _(sp):
                sp.sem_inc(turned, 1)
                first = starts(sp)
                for e in range(E):
                    with sp.Fori(first[e], first[e + 1]) as n:
                        sp.wait_ge(turned, n + 1)
                        sp.dma_start(xs[:, :, :], rows_of(t["xs_dram"], e, n, first[e])).then_inc(xs_in, 16)
                sp.wait_ge(turned, first[E] + 1)
                sp.dma_start(xs[:, :, :], t["xs_dram"][0, 0:TOK].rearrange("(k p) d -> p k d", p=P)).then_inc(xs_in, 16)

            @block.tensor
            def _(pe):
                pe.wait_ge(w_in, 16 * (2 * E + 2))
                first = starts(pe)

                def turn(n):
                    pe.wait_ge(xs_in, n * 16 + 16)
                    pe.wait_ge(xsT_ready, n + 1)
                    for q in range(TQ):
                        for k in range(KC):
                            ins = nc.tensor.transpose(ps_t[:, k, q * P:q * P + P], xs[:, q, k * P:k * P + P],
                                                      t["ident"][:, :])
                    ins.then_inc(turned, 1)

                turn(0)
                for e in range(E):
                    with pe.Fori(first[e], first[e + 1]) as n:
                        def up_product(c):
                            pe.wait_ge(relud, n * FC + c + 1)
                            for k in range(KC):
                                ins = nc.tensor.matmul(ps_h[:, c % HB, 0:TOK], w1[:, e, k, c * P:c * P + P], xsT[:, k, :],
                                                       start=k == 0, stop=k == KC - 1)
                            ins.then_inc(up, 1)

                        def down_product(c):
                            pe.wait_ge(relud, n * FC + c + 1 + HB)
                            for q in range(TQ):
                                ins = nc.tensor.matmul(ps_o[:, q, 0:D], hid[:, c, q * P:q * P + P], w2[:, e, c, :],
                                                       start=c == 0, stop=c == FC - 1)
                            ins.then_inc(down, 1)

                        pe.wait_ge(xsT_ready, n + 2)
                        for c in range(FC + 2):
                            if c < FC:
                                up_product(c)
                            if c == FC // 2:
                                turn(n + 1)
                            if c == 2:
                                pe.wait_ge(y_ready, n + 1)
                            if c >= 2:
                                down_product(c - 2)

            @block.scalar
            def _(act):
                act.sem_inc(relud, HB)
                act.sem_inc(down, 1)
                act.wait_ge(w_in, 16 * (2 * E + 2))
                first = starts(act)
                for e in range(E):
                    with act.Fori(first[e], first[e + 1]) as n:
                        act.wait_ge(down, n * FC + 1)
                        for c in range(FC):
                            act.wait_ge(up, n * FC + c + 1)
                            nc.scalar.activation(hid[:, c, :], ps_h[:, c % HB, 0:TOK], ACT.Relu,
                                                 bias=b1[:, e * FC + c:e * FC + c + 1]).then_inc(relud, 1)
                        act.wait_ge(y_ready, n + 2)
                        act.dma_start(t["ys_dram"][bass.ds(n, 1)].rearrange("a (k p) d -> p (a k) d", p=P),
                                      y[:, :, :]).then_inc(y_stored, 16)
                act.wait_ge(y_stored, first[E] * 16 + 1)
                gate(act, t["act_gate"])

            @block.vector
            def _(dve):
                dve.sem_inc(xsT_ready, 1)
                dve.sem_inc(y_ready, 1)
                dve.sem_inc(y_stored, 1)
                dve.wait_ge(w_in, 16 * (2 * E + 2))
                first = starts(dve)
                dve.wait_ge(turned, 2)
                nc.vector.tensor_copy(xsT[:, :, :], ps_t[:, :, :]).then_inc(xsT_ready, 1)
                for e in range(E):
                    with dve.Fori(first[e], first[e + 1]) as n:
                        dve.wait_ge(turned, n + 3)
                        dve.wait_ge(up, n * FC + FC)
                        nc.vector.tensor_copy(xsT[:, :, :], ps_t[:, :, :]).then_inc(xsT_ready, 1)
                        dve.wait_ge(down, n * FC + FC + 1)
                        dve.wait_ge(y_stored, n * 16 + 1)
                        nc.vector.tensor_tensor(y[:, :, :], ps_o[:, :, 0:D],
                                                b2[:, e, :].unsqueeze(1).broadcast_to([P, TQ, D]), ALU.add).then_inc(y_ready, 1)


def attend_wide(nc, sem, t):
    R = 16
    SCALE = 1.0 / float(D) ** 0.5
    NW = 12
    with Stage(nc, "aw") as st:
        ctxT, ctx = st.sb("ctxT", [P, KC, KEYS]), st.sb("ctx", [P, KT, D])
        wgt = {n: st.sb(n, [P, KC, D]) for n in ("q", "k", "v", "oT")}
        low = {n: (st.sb(n + "a", [R, D]), st.sb(n + "bT", [R, D])) for n in "qkv"}
        full = {n: st.sb(n + "f", [P, KC, D]) for n in "qkv"}
        amat, cmat = st.sb("amat", [P, KC, D]), st.sb("cmat", [P, KC, D])
        xn, xnT, gT = st.sb("xn", [P, QT, D]), st.sb("xnT", [P, KC, S]), st.sb("gT", [P, KC, S])
        prob, pT, uT = st.sb("prob", [P, 2, KEYS]), st.sb("pT", [P, KT, S]), st.sb("uT", [P, KC, S])
        peak, shift, den = st.sb("peak", [P, QT]), st.sb("shift", [P, QT]), st.sb("den", [P, QT])
        fac = st.sb("fac", [P, QT])
        stats, mv = st.sb("stats", [P, QT, 6]), st.sb("mv", [P, QT, 2])
        ve, sd, rstd = st.sb("ve", [P, QT]), st.sb("sd", [P, QT]), st.sb("rstd", [P, QT])
        y, slot = st.sb("y", [P, QT, D]), st.sb("slot", [P, QT], U32)
        ps_s, ps_p, ps_w = st.ps("pss", [P, 4, 512]), st.ps("psp", [P, 2, 4, P]), st.ps("psw", [P, 2, 512])

        y_in, y_used, slot_ready = sem("aw_y"), sem("aw_y_used"), sem("aw_slot")
        w_in, c_in, c_used = sem("aw_w"), sem("aw_c"), sem("aw_c_used")
        mixed, mixed_out = sem("aw_mixed"), sem("aw_mixed_out")
        own, normed, var, sdr = sem("aw_own"), sem("aw_normed"), sem("aw_var"), sem("aw_sd")
        wide, wide_out = sem("aw_wide"), sem("aw_wide_out")
        s_mm, peaked, expd, p_turned, p_out = (sem(f"aw_{n}") for n in ("s_mm", "peaked", "exp", "p_turned", "p_out"))
        GR = [(a, min(4, KT - a)) for a in range(0, KT, 4)]
        WIDE = 4

        with nc.Block() as block:
            @block.sync
            def _(sp):
                for n in ("q", "k", "v", "oT"):
                    sp.dma_start(wgt[n][:, :, :], t["l1_" + n + "_in"]).then_inc(w_in, 16)
                for n in "qkv":
                    sp.dma_start(low[n][0][:, :], t["l1_" + n + "a_in"]).then_inc(w_in, 16)
                    sp.dma_start(low[n][1][:, :], t["l1_" + n + "bT_in"]).then_inc(w_in, 16)
                with sp.Fori(0, B) as b:
                    sp.wait_ge(c_used, b + 1)
                    sp.dma_start(ctxT[:, :, :], t["ctxT_in"][b]).then_inc(c_in, 16)
                    sp.dma_start(ctx[:, 0:KT - 1, :], t["ctx_in"][b, 0:(KT - 1) * P].rearrange("(k p) d -> p k d", p=P))\
                        .then_inc(c_in, 16)
                    sp.dma_start(ctx[0:key_rows(KT - 1), KT - 1, :], t["ctx_in"][b, (KT - 1) * P:KEYS]).then_inc(c_in, 16)

            @block.tensor
            def _(pe):
                pe.sem_inc(c_used, 1)
                pe.wait_ge(w_in, 160)
                for n, name in enumerate("qkv"):
                    pe.wait_ge(mixed_out, n)
                    for m in range(KC):
                        ins = nc.tensor.matmul(ps_w[:, m, 0:D], low[name][1][:, m * P:m * P + P], low[name][0][:, :],
                                               start=True, stop=True)
                    ins.then_inc(mixed, 1)
                for n, (left_, right) in enumerate(((full["q"], full["k"]), (full["v"], wgt["oT"]))):
                    pe.wait_ge(mixed_out, 3 + n)
                    for m in range(KC):
                        for k in range(KC):
                            ins = nc.tensor.matmul(ps_w[:, m, 0:D], left_[:, k, m * P:m * P + P], right[:, k, :],
                                                   start=k == 0, stop=k == KC - 1)
                    ins.then_inc(mixed, 1)
                pe.wait_ge(mixed_out, 5)
                with pe.Fori(0, B) as b:
                    pe.wait_ge(c_in, b * 48 + 48)
                    pe.wait_ge(normed, (b + 1) * QT)
                    pe.wait_ge(wide_out, b * WIDE + 1)
                    for q in range(QT):
                        for k in range(KC):
                            ins = nc.tensor.transpose(ps_w[:, k, q * P:q * P + P], xn[:, q, k * P:k * P + P],
                                                      t["ident"][:, :])
                    ins.then_inc(wide, 1)
                    pe.wait_ge(wide_out, b * WIDE + 2)
                    for m in range(KC):
                        for k in range(KC):
                            ins = nc.tensor.matmul(ps_w[:, m, :], amat[:, k, m * P:m * P + P], xnT[:, k, :],
                                                   start=k == 0, stop=k == KC - 1)
                    ins.then_inc(wide, 1)
                    pe.wait_ge(wide_out, b * WIDE + 3)

                    def score_rows(q):
                        pe.wait_ge(expd, b * QT + q + 1)
                        for n, (a, w) in enumerate(KEY_SPANS):
                            for k in range(KC):
                                ins = nc.tensor.matmul(ps_s[:, n, 0:w], gT[:, k, q * P:q * P + P], ctxT[:, k, a:a + w],
                                                       start=k == 0, stop=k == KC - 1)
                        ins.then_inc(s_mm, 1)

                    def turn_probs(q):
                        pe.wait_ge(expd, b * QT + q + 2)
                        for n, (a, m) in enumerate(GR):
                            u = (b * QT + q) * len(GR) + n
                            pe.wait_ge(p_out, u + 1)
                            for kt in range(a, a + m):
                                r = key_rows(kt)
                                ins = nc.tensor.transpose(ps_p[0:r, n % 2, kt - a, :], prob[:, q % 2, kt * P:kt * P + r],
                                                          t["ident"][:, :])
                            ins.then_inc(p_turned, 1)

                    score_rows(0)
                    for q in range(QT):
                        if q + 1 < QT:
                            score_rows(q + 1)
                        turn_probs(q)
                    pe.wait_ge(p_out, (b + 1) * QT * len(GR) + 2)
                    for m in range(KC):
                        for kt in range(KT):
                            r = key_rows(kt)
                            ins = nc.tensor.matmul(ps_w[:, m, :], ctx[0:r, kt, m * P:m * P + P], pT[0:r, kt, :],
                                                   start=kt == 0, stop=kt == KT - 1)
                    ins.then_inc(wide, 1)
                    pe.wait_ge(wide_out, b * WIDE + 4)
                    pe.sem_inc(c_used, 1)
                    for q in range(QT):
                        for k in range(KC):
                            ins = nc.tensor.matmul(ps_w[:, q // 2, (q % 2) * D:(q % 2) * D + D], uT[:, k, q * P:q * P + P],
                                                   cmat[:, k, :], start=k == 0, stop=k == KC - 1)
                    ins.then_inc(wide, 1)

            @block.scalar
            def _(act):
                act.sem_inc(expd, 1)
                with act.Fori(0, B) as b:
                    act.wait_ge(var, b + 1)
                    nc.scalar.activation(sd[:, :], ve[:, :], ACT.Sqrt).then_inc(sdr, 1)
                    for q in range(QT):
                        if q > 1:
                            act.wait_ge(p_turned, (b * QT + q - 1) * len(GR))
                        act.wait_ge(peaked, b * QT + q + 1)
                        nc.scalar.activation(prob[:, q % 2, :], ps_s[:, :, :].rearrange("p a n -> p (a n)")[:, 0:KEYS],
                                             ACT.Exp, bias=shift[:, q:q + 1], scale=SCALE,
                                             accum_out=den[:, q:q + 1]).then_inc(expd, 1)

            @block.vector
            def _(dve):
                dve.sem_inc(p_out, 2)
                dve.sem_inc(wide_out, 1)
                dve.wait_ge(w_in, 160)
                for n, name in enumerate("qkv"):
                    dve.wait_ge(mixed, n + 1)
                    nc.vector.tensor_tensor(full[name][:, :, :], ps_w[:, :, 0:D], wgt[name][:, :, :],
                                            ALU.add).then_inc(mixed_out, 1)
                for n, dst in enumerate((amat, cmat)):
                    dve.wait_ge(mixed, n + 4)
                    nc.vector.tensor_copy(dst[:, :, :], ps_w[:, :, 0:D]).then_inc(mixed_out, 1)
                dve.sem_inc(y_used, 1)
                with dve.Fori(0, B) as b:
                    me = Own(dve, own, b, 4 + QT + 2)
                    dve.wait_ge(y_in, b * 16 * QT + 16 * QT)
                    tiles = t["x"][:, bass.ds(b * QT, QT), :]
                    me.then(nc.vector.scalar_tensor_tensor(tiles, y[:, :, :], t["gate_f"](0), tiles, ALU.mult, ALU.add))
                    dve.sem_inc(y_used, 1)
                    norm_tiles(nc, dve, me, lambda q: t["x_tile"](b * QT + q), lambda q: xn[:, q, :],
                               stats, mv, ve, rstd, t["dve_gate"], var, (sdr, b + 1), sd, normed)
                    dve.wait_ge(wide, b * WIDE + 1)
                    nc.vector.tensor_copy(xnT[:, :, :], ps_w[:, :, :]).then_inc(wide_out, 1)
                    dve.wait_ge(wide, b * WIDE + 2)
                    nc.vector.tensor_copy(gT[:, :, :], ps_w[:, :, :]).then_inc(wide_out, 1)

                    def find_peak(q):
                        dve.wait_ge(s_mm, b * QT + q + 1)
                        me.then(nc.vector.tensor_reduce(peak[:, q:q + 1],
                                                        ps_s[:, :, :].rearrange("p a n -> p (a n)")[:, 0:KEYS],
                                                        AX.X, ALU.max))
                        nc.vector.tensor_scalar(shift[:, q:q + 1], peak[:, q:q + 1], -SCALE, None,
                                                ALU.mult).then_inc(peaked, 1)

                    def probs_out(q):
                        for n, (a, m) in enumerate(GR):
                            u = (b * QT + q) * len(GR) + n
                            r = key_rows(a + m - 1)
                            dve.wait_ge(p_turned, u + 1)
                            nc.vector.tensor_copy(pT[0:r, a:a + m, q * P:q * P + P], ps_p[0:r, n % 2, 0:m, :]).then_inc(p_out, 1)

                    find_peak(0)
                    for q in range(QT):
                        if q + 1 < QT:
                            find_peak(q + 1)
                        probs_out(q)
                    dve.wait_ge(wide, b * WIDE + 3)
                    nc.vector.tensor_copy(uT[:, :, :], ps_w[:, :, :]).then_inc(wide_out, 1)
                    dve.wait_ge(expd, (b + 1) * QT + 1)
                    me.then(nc.vector.reciprocal(fac[:, :], den[:, :]))
                    me.then(nc.vector.tensor_scalar(fac[:, :], fac[:, :], t["gate_x"](1), None, ALU.mult))
                    dve.wait_ge(wide, b * WIDE + 4)
                    for q in range(QT):
                        ins = nc.vector.scalar_tensor_tensor(t["x_tile"](b * QT + q),
                                                             ps_w[:, q // 2, (q % 2) * D:(q % 2) * D + D],
                                                             fac[:, q:q + 1], t["x_tile"](b * QT + q), ALU.mult, ALU.add)
                    ins.then_inc(wide_out, 1)


            @block.gpsimd
            def _(pool):
                with pool.Fori(0, B) as b:
                    pool.wait_ge(y_used, b + 1)
                    gate(pool, t["pool_gate"])
                    nc.gpsimd.tensor_copy(slot[:, :], t["slots"][:, bass.ds(b * QT, QT)]).then_inc(slot_ready, 1)
                    pool.wait_ge(slot_ready, b + 1)
                    gate(pool, t["pool_gate"])
                    for q in range(QT):
                        nc.gpsimd.indirect_dma_start(
                            out=y[:, q, :], out_offset=None, in_=t["ys_rows"],
                            in_offset=bass.IndirectOffsetOnAxis(ap=slot[:, q:q + 1], axis=0)).then_inc(y_in, 16)


MH, NK, KD = 8, 64, 128
TOP = 8
SEL = MH * TOP
YH = NK // 2
HT = P // 2


def memory(nc, sem, t, out):
    memory_keys(nc, sem, t, *t["memory"])
    t["release_x"]()
    memory_tiles(nc, sem, t, out, *t["memory"])


def memory_keys(nc, sem, t, mk, scale, offset):
    PH = 2 * MH
    with Stage(nc, "mk") as st:
        wq, keys = st.sb("wq", [P, PH, D]), st.sb("keys", [P, PH, NK])
        gamma, beta = st.sb("gamma", [P, KC]), st.sb("beta", [P, KC])
        xn, xnT = st.sb("xn", [P, 2, QT, D]), st.sb("xnT", [P, 2, KC, S])
        stats, mv = st.sb("stats", [P, QT, 6]), st.sb("mv", [P, QT, 2])
        ve, sd, rstd = st.sb("ve", [P, QT]), st.sb("sd", [P, QT]), st.sb("rstd", [P, QT])
        bstats, bmv = st.sb("bstats", [P, KC, B, 6]), st.sb("bmv", [P, KC, 2])
        ps_t, ps_k = st.ps("pst", [P, 2, KC, S]), st.ps("psk", [P, 2, 512])
        w_in, own, normed, var, sdr = sem("mk_w"), sem("mk_own"), sem("mk_normed"), sem("mk_var"), sem("mk_sd")
        turned, copied, stored = sem("mk_turned"), sem("mk_copied"), [sem("mk_stored0"), sem("mk_stored1")]
        counted = sem("mk_counted")
        k_mm, k_out, x_stored = sem("mk_k_mm"), sem("mk_k_out"), sem("mk_x_stored")
        HALVES = [(m, c) for m in range(KC) for c in range(2)]

        with nc.Block() as block:
            @block.sync
            def _(sp):
                for s in range(2):
                    sp.sem_inc(stored[s], 1)
                sp.dma_start(t["x_dram"].rearrange("n p d -> p n d"), t["x"]).then_inc(x_stored, 16)
                for dst, name in ((wq, "m_wq"), (keys, "m_keys"), (gamma, "m_gamma"), (beta, "m_beta")):
                    sp.dma_start(dst.ap(), t[name + "_in"]).then_inc(w_in, 16)
                with sp.Fori(0, B // 2) as i:
                    for s in range(2):
                        b = 2 * i + s
                        sp.wait_ge(copied, b + 1)
                        for k in range(KC):
                            sp.dma_start(t["xT_dram"][bass.ds(b * QT, QT), :, k, :].rearrange("q p n -> p q n"),
                                         xnT[:, s, k, :].rearrange("p (q n) -> p q n", n=P)).then_inc(stored[s], 16)
                for s in range(2):
                    sp.wait_ge(stored[s], 16 * KC * (B // 2) + 1)
                sp.wait_ge(x_stored, 16)

            @block.tensor
            def _(pe):
                pe.wait_ge(w_in, 64)
                for n, (m, c) in enumerate(HALVES):
                    if n > 1:
                        pe.wait_ge(k_out, n - 1)
                    for ph in range(MH):
                        ins = nc.tensor.matmul(ps_k[:, n % 2, ph * NK:(ph + 1) * NK], wq[:, c * MH + ph, m * P:m * P + P],
                                               keys[:, c * MH + ph, :], start=True, stop=True)
                    ins.then_inc(k_mm, 1)
                with pe.Fori(0, B // 2) as i:
                    for s in range(2):
                        b = 2 * i + s
                        pe.wait_ge(normed, (b + 1) * QT)
                        for q in range(QT):
                            for k in range(KC):
                                ins = nc.tensor.transpose(ps_t[:, s, k, q * P:q * P + P], xn[:, s, q, k * P:k * P + P],
                                                          t["ident"][:, :])
                        ins.then_inc(turned, 1)

            @block.scalar
            def _(act):
                for n, (m, c) in enumerate(HALVES):
                    act.wait_ge(k_mm, n + 1)
                    nc.scalar.activation(mk[:, m, c * 512:c * 512 + 512], ps_k[:, n % 2, :], ACT.Copy).then_inc(k_out, 1)
                with act.Fori(0, B // 2) as i:
                    for s in range(2):
                        b = 2 * i + s
                        act.wait_ge(var, b + 1)
                        nc.scalar.activation(sd[:, :], ve[:, :], ACT.Sqrt).then_inc(sdr, 1)
                        act.wait_ge(turned, b + 1)
                        act.wait_ge(stored[s], i * 16 * KC + 1)
                        nc.scalar.activation(xnT[:, s, :, :], ps_t[:, s, :, :], ACT.Copy).then_inc(copied, 1)
                act.wait_ge(var, B + 1)
                nc.scalar.activation(sd[:, 0:KC], ve[:, 0:KC], ACT.Sqrt).then_inc(sdr, 1)

            @block.vector
            def _(dve):
                with dve.Fori(0, B // 2) as i:
                    for s in range(2):
                        b = 2 * i + s
                        me = Own(dve, own, b, 3)
                        norm_tiles(nc, dve, me, lambda q: t["x_tile"](b * QT + q), lambda q: xn[:, s, q, :],
                                   stats, mv, ve, rstd, t["dve_gate"], var, (sdr, b + 1), sd, normed)
                        dve.wait_ge(copied, b + 1)
                        gate(dve, t["dve_gate"])
                        for k in range(KC):
                            ins = nc.vector.bn_stats(bstats[:, k, bass.ds(b, 1), :].rearrange("p a c -> p (a c)"),
                                                     xnT[:, s, k, :])
                        ins.then_inc(counted, 1)
                me = Own(dve, own, B, 3)
                dve.wait_ge(counted, B)
                for k in range(KC):
                    ins = nc.vector.bn_aggr(bmv[:, k, :], bstats[:, k, :, :].rearrange("p b c -> p (b c)"))
                me.then(ins)
                nc.vector.tensor_scalar(ve[:, 0:KC], bmv[:, :, 1], LN_EPS, None, ALU.add).then_inc(var, 1)
                dve.wait_ge(sdr, B + 1)
                dve.wait_ge(w_in, 64)
                me.then(nc.vector.reciprocal(rstd[:, 0:KC], sd[:, 0:KC]))
                me.then(nc.vector.tensor_tensor(scale[:, :], rstd[:, 0:KC], gamma[:, :], ALU.mult))
                me.then(nc.vector.tensor_tensor(offset[:, :], bmv[:, :, 0], scale[:, :], ALU.mult))
                me.then(nc.vector.tensor_tensor(offset[:, :], beta[:, :], offset[:, :], ALU.subtract))


def memory_tiles(nc, sem, t, out, mk, scale, offset):
    TB = 16
    NB = HT // TB * 2
    YB = 4
    ND = YH // YB
    QN = 5
    with Stage(nc, "mt") as st:
        key_in, key_out = st.sb("key_in", [P, KC, YH, P]), st.sb("key_out", [P, YH, D])
        iota_m, iota8 = st.sb("iota_m", [P, P, TB], BF16), st.sb("iota8", [P, TOP])
        identb = st.sb("identb", [P, P], BF16)
        iota_f = st.sb("iota_f", [P, P])
        xl, xb = st.sb("xl", [P, 2, KC, P]), st.sb("xb", [P, 2, KC, P])
        xr, o = st.sb("xr", [P, 2, D]), st.sb("o", [P, 2, D])
        sims = st.sb("sims", [P, 2 * MH, NK])
        s8, i8, i8f = st.sb("s8", [P, 2 * MH, TOP]), st.sb("i8", [P, 2 * MH, TOP], U32), st.sb("i8f", [P, 2 * MH, TOP])
        pairs = st.sb("pairs", [P, MH, TOP, TOP])
        best, rank = st.sb("best", [P, MH, TOP]), st.sb("rank", [P, MH, TOP], U32)
        ab, abf = st.sb("ab", [P, 2, SEL], U32), st.sb("abf", [P, 2, SEL])
        match = st.sb("match", [P, 2 * MH, TOP, TOP])
        xy, ge = st.sb("xy", [P, 2, SEL]), st.sb("ge", [P, SEL])
        diff, ew, den, w, wr = (st.sb("diff", [P, MH, TOP]), st.sb("ew", [P, MH, TOP]), st.sb("den", [P, 2, MH]),
                                st.sb("w", [P, MH, TOP]), st.sb("wrest", [P, SEL]))
        picks, picksT = st.sb("picks", [P, 2, QN, SEL], BF16), st.sb("picksT", [P, QN, HT], BF16)
        hot_m, hot_y = st.sb("hot_m", [P, 2, P, HT], BF16), st.sb("hot_y", [P, YH, HT], BF16)
        hot_w = st.sb("hot_w", [P, 2, 3, YH, HT], BF16)
        g = st.sb("g", [P, 2, YH, P])
        ps_c, ps_d = st.ps("psc", [P, 2, 2, 512]), st.ps("psd", [P, 2, 512])
        ps_u, ps_x = st.ps("psu", [P, 512]), st.ps("psx", [P, 1024], BF16)
        ps_sim = ps_x[:, :].bitcast(F32)

        w_in, ready, xl_in, xr_in = sem("mt_w"), sem("mt_ready"), [sem("mt_xl0"), sem("mt_xl1")], [sem("mt_xr0"), sem("mt_xr1")]
        xb_ready, sim_mm, sim_out, picked = sem("mt_xb"), sem("mt_sim_mm"), sem("mt_sim_out"), sem("mt_picked")
        diff_ready, weighed, sel_ready = sem("mt_diff"), sem("mt_weighed"), sem("mt_sel")
        turned, turned_out, hot = sem("mt_turned"), sem("mt_turned_out"), sem("mt_hot")
        c_mm, w_out, d_mm, g_out = sem("mt_c_mm"), sem("mt_w_out"), sem("mt_d_mm"), sem("mt_g_out")
        u_mm, final, o_stored = sem("mt_u_mm"), sem("mt_final"), [sem("mt_o0"), sem("mt_o1")]
        own_s, own_h = sem("mt_own_select"), sem("mt_own_hot")
        NSEL, NHOT = 17, 2

        def steps(eng, first, step):
            first()
            with eng.Fori(0, NT // 2 - 1) as i:
                for off in range(2):
                    step(i, off, 2)
            for off in range(2):
                step(NT // 2 - 1, off, 1 - off)

        with nc.Block() as block:
            @block.sync
            def _(sp):
                for dst, name in ((iota_f, "m_iota"), (key_in, "m_in"), (key_out, "m_out"), (iota8, "m_iota8")):
                    sp.dma_start(dst.ap(), t[name + "_in"]).then_inc(w_in, 16)

                for s in range(2):
                    sp.sem_inc(o_stored[s], 1)

                def load(i, off):
                    n = 2 * i + off
                    sp.dma_start(xr[:, off % 2, :], t["x_dram"][n]).then_inc(xr_in[off % 2], 16)

                def first():
                    load(0, 0)
                    load(0, 1)

                def step(i, off, ahead):
                    n = 2 * i + off
                    sp.wait_ge(final, n + 2)
                    sp.dma_start(t["out_tiles"][n], o[:, off, :]).then_inc(o_stored[off], 16)
                    if ahead == 2:
                        load(i, off + 2)

                steps(sp, first, step)
                for s in range(2):
                    sp.wait_ge(o_stored[s], 16 * (NT // 2) + 1)

            @block.gpsimd
            def _(pool):
                def token_rows(i, off):
                    n, s = 2 * i + off, off % 2
                    if off > 1:
                        pool.wait_ge(d_mm, (n - 1) * ND)
                        gate(pool, t["pool_gate"])
                    pool.dma_start(xl[:, s, :, :], t["xT_dram"][n]).then_inc(xl_in[s], 16)
                    if off > 1:
                        pool.wait_ge(sim_mm, (n - 1) * 2)
                    pool.wait_ge(xl_in[s], 16 * (i + off // 2) + 16)
                    gate(pool, t["pool_gate"])
                    for k in range(KC):
                        ins = nc.gpsimd.tensor_scalar(xb[:, s, k, :], xl[:, s, k, :], scale[:, k:k + 1], offset[:, k:k + 1],
                                                      ALU.mult, ALU.add)
                    ins.then_inc(xb_ready, 1)

                token_rows(0, 0)
                token_rows(0, 1)
                with pool.Fori(0, NT // 2 - 1) as i:
                    for off in range(2):
                        token_rows(i, off + 2)

            @block.tensor
            def _(pe):
                pe.sem_inc(u_mm, 1)
                pe.wait_ge(ready, 1)

                def half_scores(i, off, c):
                    n = 2 * i + off
                    if c == 0:
                        pe.wait_ge(xb_ready, n + 1)
                        if off > 1:
                            pe.wait_ge(turned_out, n - 1)
                    if off or c:
                        pe.wait_ge(sim_out, 2 * n + c)
                    for k in range(KC):
                        ins = nc.tensor.matmul(ps_sim, xb[:, off % 2, k, :], mk[:, k, c * 512:c * 512 + 512],
                                               start=k == 0, stop=k == KC - 1)
                    ins.then_inc(sim_mm, 1)

                def turn_picks(i, off, ahead):
                    n = 2 * i + off
                    pe.wait_ge(sel_ready, n + 1)
                    pe.wait_ge(sim_out, 2 * (n + 1 + ahead))
                    gate(pe, t["pe_gate"])
                    for h in range(2):
                        rows = slice(h * HT, h * HT + HT)
                        for v in range(QN):
                            ins = nc.tensor.transpose(ps_x[rows, v * HT:v * HT + HT], picks[rows, off % 2, v, :],
                                                      identb[rows, rows])
                    ins.then_inc(turned, 1)

                def dense_in(i, off):
                    n, s = 2 * i + off, off % 2
                    pe.wait_ge(xl_in[s], 16 * (i + off // 2) + 16)
                    for j in range(ND):
                        pe.wait_ge(g_out, n * ND + j + 1)
                        for y in range(YB):
                            for k in range(KC):
                                ins = nc.tensor.matmul(ps_d[:, j % 2, y * P:y * P + P], key_in[:, k, j * YB + y, :],
                                                       xl[:, s, k, :], start=k == 0, stop=k == KC - 1)
                        ins.then_inc(d_mm, 1)

                def scatter(i, off, part):
                    n = 2 * i + off
                    if part == 0:
                        pe.wait_ge(hot, n + 1)
                    for tb in range(2 * part, 2 * part + 2):
                        pe.wait_ge(w_out, n * NB + 2 * tb + 2)
                        for tok in range(TB):
                            for v in range(3):
                                for h in range(2):
                                    rows = slice(h * HT, h * HT + HT)
                                    ins = nc.tensor.matmul(ps_c[:, h, tb % 2, tok * YH:(tok + 1) * YH],
                                                           hot_m[rows, off % 2, :, tb * TB + tok],
                                                           hot_w[rows, off % 2, v, :, tb * TB + tok],
                                                           start=v == 0, stop=v == 2)
                                    if tok == TB - 1 and v == 2:
                                        ins.then_inc(c_mm, 1)

                def dense_out(i, off):
                    n = 2 * i + off
                    pe.wait_ge(w_out, (n + 1) * NB + 4)
                    pe.wait_ge(final, n + 1)
                    for y in range(YH):
                        ins = nc.tensor.matmul(ps_u[:, 0:D], g[:, off % 2, y, :], key_out[:, y, :],
                                               start=y == 0, stop=y == YH - 1)
                    ins.then_inc(u_mm, 1)

                def first():
                    for off in range(2):
                        for c in range(2):
                            half_scores(0, off, c)
                    turn_picks(0, 0, 1)
                    pe.wait_ge(w_in, 64)
                    dense_in(0, 0)

                def step(i, off, ahead):
                    for c in range(2):
                        if ahead == 2:
                            half_scores(i, off + 2, c)
                        scatter(i, off, c)
                    if ahead:
                        turn_picks(i, off + 1, min(ahead - 1, 1))
                        dense_in(i, off + 1)
                    dense_out(i, off)

                steps(pe, first, step)

            @block.scalar
            def _(act):
                act.sem_inc(g_out, 2)

                def scores_out(i, off):
                    n = 2 * i + off
                    for c in range(2):
                        act.wait_ge(sim_mm, 2 * n + c + 1)
                        if off:
                            act.wait_ge(picked, n)
                        nc.scalar.activation(sims[:, c * MH:(c + 1) * MH, :].rearrange("p h k -> p (h k)"), ps_sim,
                                             ACT.Copy).then_inc(sim_out, 1)

                def exps(i, off):
                    act.wait_ge(diff_ready, 2 * i + off + 1)
                    nc.scalar.activation(ew[:, :, :], diff[:, :, :], ACT.Exp).then_inc(weighed, 1)

                def gelus(i, off):
                    n = 2 * i + off
                    if off:
                        act.wait_ge(u_mm, n)
                    for j in range(ND):
                        act.wait_ge(d_mm, n * ND + j + 1)
                        nc.scalar.activation(g[:, off % 2, j * YB:(j + 1) * YB, :],
                                             ps_d[:, j % 2, :].rearrange("p (y n) -> p y n", n=P), ACT.Gelu).then_inc(g_out, 1)

                def first():
                    scores_out(0, 0)
                    exps(0, 0)
                    scores_out(0, 1)
                    gelus(0, 0)
                    exps(0, 1)

                def step(i, off, ahead):
                    if ahead == 2:
                        scores_out(i, off + 2)
                    if ahead:
                        gelus(i, off + 1)
                    if ahead == 2:
                        exps(i, off + 2)

                steps(act, first, step)

            @block.vector
            def _(dve):
                dve.sem_inc(w_out, 4)
                dve.sem_inc(final, 1)
                dve.wait_ge(w_in, 64)
                nc.vector.tensor_copy(identb[:, :], t["ident"][:, :])
                nc.vector.tensor_copy(iota_m[:, :, :], iota_f[:, :].unsqueeze(2).broadcast_to([P, P, TB])).then_inc(ready, 1)
                dve.wait_ge(ready, 1)

                def select(i, off):
                    n, s = 2 * i + off, off % 2
                    me = Own(dve, own_s, n, NSEL)
                    dve.wait_ge(sim_out, 2 * n + 2)
                    gate(dve, t["dve_gate"])
                    for h in range(2 * MH):
                        ins = nc.vector.max(s8[:, h, :], sims[:, h, :])
                    me.then(ins)
                    gate(dve, t["dve_gate"])
                    for h in range(2 * MH):
                        ins = nc.vector.max_index(i8[:, h, :], s8[:, h, :], sims[:, h, :])
                    ins.then_inc(picked, 1)
                    dve.wait_ge(picked, n + 1)
                    nc.vector.tensor_copy(i8f[:, :, :], i8[:, :, :])
                    me.then(nc.vector.tensor_tensor(pairs[:, :, :, :],
                                                    s8[:, 0:MH, :].unsqueeze(3).broadcast_to([P, MH, TOP, TOP]),
                                                    s8[:, MH:, :].unsqueeze(2).broadcast_to([P, MH, TOP, TOP]), ALU.add))
                    gate(dve, t["dve_gate"])
                    for h in range(MH):
                        ins = nc.vector.max(best[:, h, :], pairs[:, h, :, :].rearrange("p a b -> p (a b)"))
                    me.then(ins)
                    nc.vector.tensor_tensor(diff[:, :, :], best[:, :, :], best[:, :, 0:1].broadcast_to([P, MH, TOP]),
                                            ALU.subtract).then_inc(diff_ready, 1)
                    for h in range(MH):
                        ins = nc.vector.max_index(rank[:, h, :], best[:, h, :], pairs[:, h, :, :].rearrange("p a b -> p (a b)"))
                    me.then(ins)
                    flat = rank[:, :, :].rearrange("p h k -> p (h k)")
                    nc.vector.tensor_scalar(ab[:, 0, :], flat, 3, None, ALU.logical_shift_right)
                    me.then(nc.vector.tensor_scalar(ab[:, 1, :], flat, TOP - 1, None, ALU.bitwise_and))
                    me.then(nc.vector.tensor_copy(abf[:, :, :], ab[:, :, :]))
                    me.then(nc.vector.tensor_tensor(match[:, :, :, :].rearrange("p h k a -> p (h k) a"),
                                                    abf[:, :, :].rearrange("p c n -> p (c n)").unsqueeze(2).broadcast_to([P, 2 * SEL, TOP]),
                                                    iota8[:, :].unsqueeze(1).broadcast_to([P, 2 * SEL, TOP]), ALU.is_equal))
                    me.then(nc.vector.tensor_tensor(match[:, :, :, :], match[:, :, :, :],
                                                    i8f[:, :, :].unsqueeze(2).broadcast_to([P, 2 * MH, TOP, TOP]), ALU.mult))
                    me.then(nc.vector.tensor_reduce(xy[:, :, :], match[:, :, :, :].rearrange("p (c h) k a -> p c (h k) a", c=2),
                                                    AX.X, ALU.add))
                    me.then(nc.vector.tensor_scalar(ge[:, :], xy[:, 1, :], float(YH), None, ALU.is_ge))
                    nc.vector.scalar_tensor_tensor(picks[:, s, 0, :], ge[:, :], float(NK), xy[:, 0, :], ALU.mult, ALU.add)
                    nc.vector.scalar_tensor_tensor(picks[:, s, 1, :], ge[:, :], -float(YH), xy[:, 1, :], ALU.mult, ALU.add)
                    dve.wait_ge(weighed, n + 1)
                    me.then(nc.vector.tensor_reduce(den[:, 0, :], ew[:, :, :], AX.X, ALU.add))
                    me.then(nc.vector.reciprocal(den[:, 1, :], den[:, 0, :]))
                    me.then(nc.vector.tensor_tensor(w[:, :, :], ew[:, :, :], den[:, 1, :].unsqueeze(2).broadcast_to([P, MH, TOP]),
                                                    ALU.mult))
                    wf = w[:, :, :].rearrange("p h k -> p (h k)")
                    me.then(nc.vector.tensor_copy(picks[:, s, 2, :], wf))
                    me.then(nc.vector.tensor_tensor(wr[:, :], wf, picks[:, s, 2, :], ALU.subtract))
                    me.then(nc.vector.tensor_copy(picks[:, s, 3, :], wr[:, :]))
                    me.then(nc.vector.tensor_tensor(picks[:, s, 4, :], wr[:, :], picks[:, s, 3, :], ALU.subtract))
                    dve.sem_inc(sel_ready, 1)
                    assert me.n == NSEL, me.n

                def one_hots(i, off):
                    n, s = 2 * i + off, off % 2
                    me = Own(dve, own_h, n, NHOT)
                    dve.wait_ge(turned, n + 1)
                    nc.vector.tensor_copy(picksT[:, :, :].rearrange("p v n -> p (v n)"), ps_x[:, 0:QN * HT]).then_inc(turned_out, 1)
                    dve.wait_ge(turned_out, n + 1)

                    def is_at(dst, rows, v):
                        return nc.vector.tensor_tensor(
                            dst.rearrange("p m (b n) -> p m b n", n=TB),
                            iota_m[:, 0:rows, :].unsqueeze(2).broadcast_to([P, rows, HT // TB, TB]),
                            picksT[:, v, :].rearrange("p (b n) -> p b n", n=TB).unsqueeze(1).broadcast_to([P, rows, HT // TB, TB]),
                            ALU.is_equal)

                    me.then(is_at(hot_y[:, :, :], YH, 1))
                    is_at(hot_m[:, s, :, :], P, 0)
                    me.then(nc.vector.tensor_tensor(hot_w[:, s, :, :, :], hot_y[:, :, :].unsqueeze(1).broadcast_to([P, 3, YH, HT]),
                                                    picksT[:, 2:QN, :].unsqueeze(2).broadcast_to([P, 3, YH, HT]), ALU.mult))
                    dve.sem_inc(hot, 1)
                    assert me.n == NHOT, me.n

                def weigh(i, off):
                    n = 2 * i + off
                    dve.wait_ge(g_out, (n + 1) * ND + 2)
                    for tb in range(HT // TB):
                        for h in range(2):
                            dve.wait_ge(c_mm, n * NB + 2 * tb + h + 1)
                            a = h * HT + tb * TB
                            gv = g[:, off % 2, :, a:a + TB].rearrange("p y n -> p n y")
                            nc.vector.tensor_tensor(gv, ps_c[:, h, tb % 2, :].rearrange("p (n y) -> p n y", y=YH), gv,
                                                    ALU.mult).then_inc(w_out, 1)

                def finish(i, off):
                    n = 2 * i + off
                    dve.wait_ge(u_mm, n + 2)
                    dve.wait_ge(xr_in[off], 16 * i + 16)
                    dve.wait_ge(o_stored[off], 16 * i + 1)
                    nc.vector.scalar_tensor_tensor(o[:, off, :], ps_u[:, 0:D], t["gate_f"](1), xr[:, off, :],
                                                   ALU.mult, ALU.add).then_inc(final, 1)

                def first():
                    select(0, 0)
                    one_hots(0, 0)
                    select(0, 1)

                def step(i, off, ahead):
                    weigh(i, off)
                    if ahead:
                        one_hots(i, off + 1)
                    if ahead == 2:
                        select(i, off + 2)
                    finish(i, off)

                steps(dve, first, step)


def build(nc, ins, out, debug=None):
    with ExitStack() as ctx:
        def sem(name):
            return ctx.enter_context(nc.semaphore(name))

        memory_of = [ctx.enter_context(nc.sbuf_tensor(n, shape, F32)) for n, shape in (
            ("mk_sb", [P, KC, 2 * MH * NK]), ("scale_sb", [P, KC]), ("offset_sb", [P, KC]))]
        x_life = ctx.enter_context(ExitStack())
        ident = ctx.enter_context(nc.sbuf_tensor("ident_sb", [P, P], F32))
        gates = ctx.enter_context(nc.sbuf_tensor("gates_sb", [P, 4], F32))
        opened = ctx.enter_context(nc.sbuf_tensor("opened_sb", [P, 4], F32))
        x = x_life.enter_context(nc.sbuf_tensor("x_rows", [P, NT, D], F32))
        slots = x_life.enter_context(nc.sbuf_tensor("slots_sb", [P, NT], U32))
        xs_dram = nc.dram_tensor("xs_dram", (E, REGION, D), F32, kind="Internal").ap()
        ys_dram = nc.dram_tensor("ys_dram", (MAX_BLOCKS, TOK, D), F32, kind="Internal").ap()
        t = {
            "x": x[:, :, :], "x_in": ins["x"].rearrange("b (q p) d -> p (b q) d", p=P),
            "x_tile": lambda n: x[:, bass.ds(n, 1), :].rearrange("p a d -> p (a d)"),
            "ident": ident, "release_x": x_life.close, "memory": memory_of,
            "x_dram": nc.dram_tensor("x_dram", (NT, P, D), F32, kind="Internal").ap(),
            "xT_dram": nc.dram_tensor("xT_dram", (NT, P, KC, P), F32, kind="Internal").ap(),
            "out_tiles": out.rearrange("b (q p) d -> (b q) p d", p=P),
            "gate_x": lambda layer: opened[:, layer:layer + 1],
            "gate_f": lambda layer: opened[:, 2 + layer:3 + layer],
            "ctx_in": ins["ctx"],
            "ctxT_in": ins["ctxT"].rearrange("b (k p) n -> b p k n", p=P),
            "x_loaded": sem("x_loaded"), "consts": sem("consts"), "consts_n": 32,
            "dve_gate": sem("dve_gate"), "pool_gate": sem("pool_gate"),
            "pe_gate": sem("pe_gate"), "act_gate": sem("act_gate"),
            "k_dram": nc.dram_tensor("k_dram", (B, 3, D, KEYS), BF16, kind="Internal").ap(),
            "q_dram": nc.dram_tensor("q_dram", (B, 3, D, S), BF16, kind="Internal").ap(),
            "v_dram": nc.dram_tensor("v_dram", (B, G, P, KT * HG * DH), F32, kind="Internal").ap(),
            "xs_dram": xs_dram, "xs_rows": xs_dram.rearrange("e n d -> (e n) d"), "slots": slots,
            "ys_dram": ys_dram, "ys_rows": ys_dram.rearrange("e n d -> (e n) d"),
            "o_dram": nc.dram_tensor("o_dram", (B, D, S), F32, kind="Internal").ap(),
        }
        for n in ("wq", "wk", "wv", "wo", "wr", "l1_q", "l1_k", "l1_v", "l1_oT"):
            t[n + "_in"] = ins[n].rearrange("(k p) n -> p k n", p=P)
        for n in ("bo", "br", "iota_e", "base0", "before", "b1", "b2") + tuple(f"l1_{a}{b}" for a in "qkv" for b in ("a", "bT")):
            t[n + "_in"] = ins[n]
        for n in ("m_wq", "m_keys", "m_gamma", "m_beta", "m_iota", "m_out", "m_iota8"):
            t[n + "_in"] = ins[n]
        t["m_in_in"] = ins["m_in"].rearrange("(k p) y m -> p k y m", p=P)
        t["w1_in"] = ins["w1"].rearrange("e (k p) f -> p e k f", p=P)
        t["w2_in"] = ins["w2"].rearrange("e (c p) d -> p e c d", p=P)
        gates_opened = sem("gates_opened")
        with nc.Block() as block:
            @block.sync
            def _(sp):
                sp.dma_start(ident[:, :], ins["ident"]).then_inc(t["consts"], 16)
                sp.dma_start(gates[:, :], ins["gates"]).then_inc(t["consts"], 16)

            @block.scalar
            def _(act):
                act.wait_ge(t["consts"], 32)
                nc.scalar.activation(opened[:, :], gates[:, :], ACT.Tanh).then_inc(gates_opened, 1)
        project(nc, sem, t)
        attend_heads(nc, sem, t)
        experts(nc, sem, t)
        attend_wide(nc, sem, t)
        if debug is None or debug > 3:
            memory(nc, sem, t, out)
            return
        written = sem("written")
        with nc.Block() as block:
            @block.sync
            def _(sp):
                sp.dma_start(out.rearrange("b (q p) d -> p (b q) d", p=P), x[:, :, :]).then_inc(written, 16)
                sp.wait_ge(written, 16)
        t["release_x"]()


def laid_out(inputs):
    import numpy as np
    c = np.ascontiguousarray
    a = {k: np.asarray(v) for k, v in inputs.items()}

    def rows(v):
        return c(np.broadcast_to(v.reshape(1, -1), (P, v.size)))

    r = {
        "x": a["x"],
        "ctx": a["ctx_1024"],
        "ctxT": c(a["ctx_1024"].transpose(0, 2, 1)),
        "wq": c(a["L0_xattn_Wq"].T), "wk": c(a["L0_xattn_Wk"].T), "wv": c(a["L0_xattn_Wv"].T),
        "wo": c(a["L0_xattn_Wo"].T), "bo": c(a["L0_xattn_bo"].reshape(1, D)),
        "wr": a["L0_ffn_Wr"], "br": rows(a["L0_ffn_br"]),
        "w1": a["L0_ffn_We1"], "b1": c(a["L0_ffn_be1"].reshape(E * FC, P).T),
        "w2": a["L0_ffn_We2"], "b2": rows(a["L0_ffn_be2"]).reshape(P, E, D),
        "l1_q": a["L1_xattn_Q_weight"], "l1_k": a["L1_xattn_K_weight"], "l1_v": a["L1_xattn_V_weight"],
        "l1_oT": c(a["L1_xattn_O_weight"].T),
        "gates": rows(np.concatenate([a["g_xattn"], a["g_ffn"]])),
        "ident": np.eye(P, dtype=np.float32),
        "base0": c(np.broadcast_to(np.arange(E, dtype=np.float32) * REGION, (P, E))),
        "before": np.triu(np.ones((P, P), np.float32), 1),
        "iota_e": c(np.broadcast_to(np.arange(E, dtype=np.float32), (P, E))),
    }
    r |= {
        "m_wq": c(a["L1_ffn_w_q"].reshape(2 * MH, KD, D).transpose(1, 0, 2)),
        "m_keys": c(a["L1_ffn_keys"].transpose(3, 2, 0, 1).reshape(KD, 2 * MH, NK)),
        "m_gamma": c(a["L1_ffn_gamma"].reshape(KC, P).T), "m_beta": c(a["L1_ffn_beta"].reshape(KC, P).T),
        "m_in": c(a["L1_ffn_key_in"].reshape(NK, 2, YH, D).transpose(3, 2, 1, 0).reshape(D, YH, P)),
        "m_out": c(a["L1_ffn_key_out"].reshape(NK, 2, YH, D).transpose(1, 0, 2, 3).reshape(P, YH, D)),
        "m_iota": c(np.broadcast_to(np.arange(P, dtype=np.float32), (P, P))),
        "m_iota8": c(np.broadcast_to(np.arange(TOP, dtype=np.float32), (P, TOP))),
    }
    for n in "qkv":
        r[f"l1_{n}a"] = a[f"L1_xattn_{n.upper()}_A"]
        r[f"l1_{n}bT"] = c(a[f"L1_xattn_{n.upper()}_B"].T)
    return r


def kernel(**inputs):
    import concourse.bacc as bacc
    import numpy as np
    from concourse.bass_utils import run_bass_kernel_spmd

    nc = bacc.Bacc("TRN2", target_bir_lowering=False, num_devices=1)
    arrays = laid_out(inputs)
    ins = {n: nc.dram_tensor(n, a.shape, mybir.dt.from_np(a.dtype), kind="ExternalInput").ap() for n, a in arrays.items()}
    out = nc.dram_tensor("out", (B, S, D), F32, kind="ExternalOutput").ap()
    build(nc, ins, out)
    r = run_bass_kernel_spmd(nc, [arrays], core_ids=[0])
    return np.asarray(r.results[0]["out"])
```

```python
from contextlib import ExitStack

import concourse.bass as bass
from concourse import mybir

F32 = mybir.dt.float32
BF16 = mybir.dt.bfloat16
F16 = mybir.dt.float16
U32 = mybir.dt.uint32
I32 = mybir.dt.int32
ALU = mybir.AluOpType
ACT = mybir.ActivationFunctionType
AX = mybir.AxisListType

P = 128
B, S, D = 8, 512, 256
KEYS = 1601
KC = D // P
QT = S // P
NT = B * QT
KT = -(-KEYS // P)
H, DH = 16, 16
HG = 4
G = H // HG
LN_EPS = 1e-5


def key_rows(kt):
    return min(P, KEYS - kt * P)


def spans(total, width):
    return [(a, min(width, total - a)) for a in range(0, total, width)]


KEY_SPANS = spans(KEYS, 512)


class Own:

    def __init__(self, eng, sem, i=0, per=0):
        self.eng, self.sem, self.base, self.n = eng, sem, i * per, 0

    def then(self, ins):
        self.n += 1
        ins.then_inc(self.sem, 1)
        self.eng.wait_ge(self.sem, self.base + self.n)


def gate(eng, sem):
    eng.sem_inc(sem, 1)


class Stage:

    def __init__(self, nc, name):
        self.nc, self.name, self.ctx = nc, name, ExitStack()

    def __enter__(self):
        return self

    def __exit__(self, *exc):
        return self.ctx.__exit__(*exc)

    def sb(self, name, shape, dt=F32):
        return self.ctx.enter_context(self.nc.sbuf_tensor(f"{self.name}_{name}", shape, dt))

    def ps(self, name, shape, dt=F32):
        return self.ctx.enter_context(self.nc.psum_tensor(f"{self.name}_{name}", shape, dt))


def norm_tiles(nc, dve, own, x, out, stats, mv, ve, rstd, gates, var_ready, sd_ready, sd, done):
    gate(dve, gates)
    for q in range(QT):
        ins = nc.vector.bn_stats(stats[:, q, :], x(q))
    own.then(ins)
    gate(dve, gates)
    for q in range(QT):
        ins = nc.vector.bn_aggr(mv[:, q, :], stats[:, q, :])
    own.then(ins)
    nc.vector.tensor_scalar(ve[:, :], mv[:, :, 1], LN_EPS, None, ALU.add).then_inc(var_ready, 1)
    dve.wait_ge(*sd_ready)
    own.then(nc.vector.reciprocal(rstd[:, :], sd[:, :]))
    for q in range(QT):
        nc.vector.tensor_scalar(out(q), x(q), mv[:, q, 0:1], rstd[:, q:q + 1],
                                ALU.subtract, ALU.mult).then_inc(done, 1)


def project(nc, sem, t):
    PB = 2
    chunks = [("k", m, a, n) for m in range(KC) for a, n in KEY_SPANS] + [("q", m, 0, S) for m in range(KC)]
    NCH, RING = len(chunks), 4
    NKC = KC * len(KEY_SPANS)
    with Stage(nc, "pj") as st:
        ctx = st.sb("ctx", [P, PB, KC, KEYS])
        w = {n: st.sb(n, [P, KC, D]) for n in ("wq", "wk", "wv")}
        xn = st.sb("xn", [P, PB, QT, D])
        xnT = st.sb("xnT", [P, PB, KC, S])
        parts = {"k": st.sb("kp", [P, PB, 3, KC, KEYS], BF16), "q": st.sb("qp", [P, PB, 3, KC, S], BF16)}
        v = st.sb("v", [P, PB, G, KT, HG * DH])
        rest = st.sb("rest", [P, RING, 512])
        stats, mv = st.sb("stats", [P, QT, 6]), st.sb("mv", [P, QT, 2])
        ve, sd, rstd = st.sb("ve", [P, QT]), st.sb("sd", [P, QT]), st.sb("rstd", [P, QT])
        ps_t, ps_c, ps_v = st.ps("pst", [P, KC, 512]), st.ps("psc", [P, RING, 512]), st.ps("psv", [P, 2, 512])

        w_in = {n: sem("pj_" + n) for n in w}
        x_first, x_rest, ctx_in = sem("pj_x_first"), sem("pj_x_rest"), [sem("pj_ctx0"), sem("pj_ctx1")]
        own, normed, var, sdr = sem("pj_dve_own"), sem("pj_normed"), sem("pj_var"), sem("pj_sd")
        turned, xnT_ready = sem("pj_turned"), sem("pj_xnT")
        mm, first, left, second, third = (sem(f"pj_{n}") for n in ("mm", "part1", "rest", "part2", "part3"))
        v_mm, v_out, stored = sem("pj_v_mm"), sem("pj_v_out"), [sem("pj_stored0"), sem("pj_stored1")]
        v_clear = sem("pj_v_clear")
        NSTORE = 3 + 3 + 1

        def out_of(parts_of, s, part, m, a, n):
            return parts[parts_of][:, s, part, m, a:a + n]

        def steps(eng, step):
            with eng.Fori(0, B // PB - 1) as i:
                for s in range(PB):
                    step(i * PB + s, i, s, True)
            for s in range(PB):
                step(B - PB + s, B // PB - 1, s, s + 1 < PB)

        with nc.Block() as block:
            @block.sync
            def _(sp):
                sp.dma_start(w["wk"][:, :, :], t["wk_in"]).then_inc(w_in["wk"], 16)
                sp.dma_start(ctx[:, 0, :, :], t["ctxT_in"][0]).then_inc(ctx_in[0], 16)
                sp.dma_start(t["x"][:, 0:QT, :], t["x_in"][:, 0:QT]).then_inc(x_first, 16)
                for n in ("wv", "wq"):
                    sp.dma_start(w[n][:, :, :], t[n + "_in"]).then_inc(w_in[n], 16)
                sp.dma_start(t["x"][:, QT:NT, :], t["x_in"][:, QT:NT]).then_inc(x_rest, 16)
                sp.dma_start(ctx[:, 1, :, :], t["ctxT_in"][1]).then_inc(ctx_in[1], 16)
                for s in range(PB):
                    sp.sem_inc(stored[s], 1)

                def step(i, s, load):
                    b = i * PB + s
                    sp.wait_ge(third, (b + 1) * NCH)
                    sp.wait_ge(v_out, (b + 1) * KT + 2)
                    for part in range(3):
                        sp.dma_start(t["k_dram"][b, part].rearrange("(m p) n -> p m n", p=P),
                                     parts["k"][:, s, part, :, :]).then_inc(stored[s], 16)
                        sp.dma_start(t["q_dram"][b, part].rearrange("(m p) n -> p m n", p=P),
                                     parts["q"][:, s, part, :, :]).then_inc(stored[s], 16)
                    sp.dma_start(t["v_dram"][b].rearrange("g p n -> p g n"),
                                 v[:, s, :, :, :].rearrange("p g k c -> p g (k c)")).then_inc(stored[s], 16)
                    if load:
                        sp.wait_ge(v_mm, (b + 1) * KT)
                        sp.dma_start(ctx[:, s, :, :], t["ctxT_in"][b + PB]).then_inc(ctx_in[s], 16)

                with sp.Fori(0, B // PB - 1) as i:
                    for s in range(PB):
                        step(i, s, True)
                for s in range(PB):
                    step(B // PB - 1, s, False)
                for s in range(PB):
                    sp.wait_ge(stored[s], 1 + 16 * NSTORE * (B // PB))

            @block.tensor
            def _(pe):
                pe.wait_ge(t["consts"], t["consts_n"])
                for n in ("wk", "wv", "wq"):
                    pe.wait_ge(w_in[n], 16)

                def step(b, i, s, ahead):
                    pe.wait_ge(ctx_in[s], i * 16 + 16)
                    for c, (what, m, a, n) in enumerate(chunks[:NKC]):
                        pe.wait_ge(left, b * NCH + c + 1)
                        for k in range(KC):
                            ins = nc.tensor.matmul(ps_c[:, (NCH * s + c) % RING, 0:n], w["wk"][:, k, m * P:m * P + P],
                                                   ctx[:, s, k, a:a + n], start=k == 0, stop=k == KC - 1)
                        ins.then_inc(mm, 1)
                    pe.wait_ge(normed, (b + 1) * QT)
                    pe.wait_ge(xnT_ready, b + 1)
                    for q in range(QT):
                        for k in range(KC):
                            ins = nc.tensor.transpose(ps_t[:, k, q * P:q * P + P],
                                                      xn[:, s, q, k * P:k * P + P], t["ident"][:, :])
                    ins.then_inc(turned, 1)
                    for kt in range(KT):
                        r = key_rows(kt)
                        pe.wait_ge(v_out, b * KT + kt + 1)
                        for k in range(KC):
                            ins = nc.tensor.matmul(ps_v[0:r, (KT * s + kt) % 2, 0:D], ctx[:, s, k, kt * P:kt * P + r],
                                                   w["wv"][:, k, :], start=k == 0, stop=k == KC - 1)
                        ins.then_inc(v_mm, 1)
                    pe.wait_ge(xnT_ready, b + 2)
                    for c, (what, m, a, n) in list(enumerate(chunks))[NKC:]:
                        pe.wait_ge(left, b * NCH + c + 1)
                        for k in range(KC):
                            ins = nc.tensor.matmul(ps_c[:, (NCH * s + c) % RING, 0:n], w["wq"][:, k, m * P:m * P + P],
                                                   xnT[:, s, k, :], start=k == 0, stop=k == KC - 1)
                        ins.then_inc(mm, 1)

                steps(pe, step)

            @block.scalar
            def _(act):
                act.sem_inc(v_out, 2)
                act.wait_ge(v_clear, 1)

                def root(b):
                    act.wait_ge(var, b + 1)
                    nc.scalar.activation(sd[:, :], ve[:, :], ACT.Sqrt).then_inc(sdr, 1)

                def step(b, i, s, ahead):
                    def part1(c):
                        what, m, a, n = chunks[c]
                        act.wait_ge(mm, b * NCH + c + 1)
                        nc.scalar.activation(out_of(what, s, 0, m, a, n), ps_c[:, (NCH * s + c) % RING, 0:n],
                                             ACT.Copy).then_inc(first, 1)

                    def part2(c):
                        what, m, a, n = chunks[c]
                        act.wait_ge(left, b * NCH + c + 1 + RING)
                        nc.scalar.activation(out_of(what, s, 1, m, a, n), rest[:, (NCH * s + c) % RING, 0:n],
                                             ACT.Copy).then_inc(second, 1)

                    act.wait_ge(stored[s], i * 16 * NSTORE + 1)
                    for c in range(NKC):
                        part1(c)
                        if c:
                            part2(c - 1)
                    part2(NKC - 1)
                    for kt in range(KT):
                        r = key_rows(kt)
                        if kt == 6 and ahead:
                            root(b + 1)
                        act.wait_ge(v_mm, b * KT + kt + 1)
                        nc.scalar.activation(v[0:r, s, :, kt, :],
                                             ps_v[0:r, (KT * s + kt) % 2, 0:D].rearrange("p (g c) -> p g c", g=G),
                                             ACT.Copy).then_inc(v_out, 1)
                    for c in range(NKC, NCH):
                        part1(c)
                        if c > NKC:
                            part2(c - 1)
                    part2(NCH - 1)

                root(0)
                steps(act, step)

            @block.vector
            def _(dve):
                nc.vector.memset(v[:, :, :, KT - 1, :], 0.0).then_inc(v_clear, 1)
                dve.sem_inc(left, RING)
                dve.sem_inc(xnT_ready, 1)
                dve.wait_ge(x_first, 16)

                def norms(b, s):
                    norm_tiles(nc, dve, Own(dve, own, b, 3), lambda q: t["x_tile"](b * QT + q), lambda q: xn[:, s, q, :],
                               stats, mv, ve, rstd, t["dve_gate"], var, (sdr, b + 1), sd, normed)

                def step(b, i, s, ahead):
                    def subtract1(c):
                        what, m, a, n = chunks[c]
                        dve.wait_ge(first, b * NCH + c + 1)
                        nc.vector.tensor_tensor(rest[:, (NCH * s + c) % RING, 0:n], ps_c[:, (NCH * s + c) % RING, 0:n],
                                                out_of(what, s, 0, m, a, n), ALU.subtract).then_inc(left, 1)

                    def subtract2(c):
                        what, m, a, n = chunks[c]
                        dve.wait_ge(second, b * NCH + c + 1)
                        nc.vector.tensor_tensor(out_of(what, s, 2, m, a, n), rest[:, (NCH * s + c) % RING, 0:n],
                                                out_of(what, s, 1, m, a, n), ALU.subtract).then_inc(third, 1)

                    for c in range(NKC):
                        subtract1(c)
                        if c:
                            subtract2(c - 1)
                    subtract2(NKC - 1)
                    dve.wait_ge(turned, b + 1)
                    nc.vector.tensor_copy(xnT[:, s, :, :], ps_t[:, :, :]).then_inc(xnT_ready, 1)
                    if ahead:
                        norms(b + 1, 1 - s)
                    for c in range(NKC, NCH):
                        subtract1(c)
                        if c > NKC:
                            subtract2(c - 1)
                    subtract2(NCH - 1)

                norms(0, 0)
                dve.wait_ge(x_rest, 16)
                steps(dve, step)


Q_PART = [0, 1, 0, 2, 0, 1]
K_PART = [0, 0, 1, 0, 2, 1]
TERMS = DH * len(Q_PART)
STACK = TERMS + 3


def attend_heads(nc, sem, t):
    SLOTS = G
    PRING, SBANKS, MBANKS = 8, 3, 2
    NST = KT * HG
    max_jobs = [(j, q, h) for j in range(HG) for q in range(QT) for h in range(2)]
    HALF = 1024
    SCALE = 1.0 / float(D) ** 0.5
    UNITS = B * G
    NLOAD = 2 * len(Q_PART) + 1
    INVERT_IN, INVERT_AT = 4, 15
    EARLY, EARLY_AT = 10, 42
    MAX_SPREAD = 38
    TURN_AT = MAX_SPREAD // HG + 1
    with Stage(nc, "at") as st:
        ks, qs = st.sb("ks", [STACK, SLOTS, HG, KEYS], BF16), st.sb("qs", [STACK, SLOTS, HG, S], BF16)
        vd = st.sb("vd", [P, 2, KT * HG, DH])
        vw = st.sb("vw", [P, 2, KT * HG, 2 * DH])
        pr = st.sb("pr", [P, PRING, S])
        pmax, nmax = st.sb("pmax", [P, HG * QT, 2]), st.sb("nmax", [P, HG * QT])
        mrest, mpart = st.sb("mrest", [HG * QT, 2, P]), st.sb("mpart", [HG * QT, 3, P], BF16)
        acc, den, o = st.sb("acc", [P, S]), st.sb("den", [P, 2, S]), st.sb("o", [P, S])
        ps_s, ps_m, ps_o = st.ps("pss", [P, SBANKS, 512]), st.ps("psm", [P, MBANKS, HALF]), st.ps("pso", [P, 512])

        kq_in, v_in = [sem(f"at_kq{s}") for s in range(SLOTS)], [sem(f"at_v{s}") for s in range(2)]
        v_wide, v_dense_used, v_ones = sem("at_v_wide"), sem("at_v_dense_used"), sem("at_v_ones")
        s_mm, expd, pv = sem("at_scores"), sem("at_exp"), sem("at_pv")
        m_mm, m_red, m_all, m_turned, m_parts, m_in = (sem(f"at_max_{n}") for n in ("mm", "red", "all", "turned", "parts", "in"))
        own, acc_out, o_ready, o_stored, ones, inverted = (
            sem(f"at_{n}") for n in ("own", "acc_out", "o_ready", "o_stored", "ones", "inverted"))

        with nc.Block() as block:
            @block.sync
            def _(sp):
                def load(b, g, used=True):
                    u, v_slot = b * G + g, g % 2
                    if used:
                        sp.wait_ge(pv, (u + 1 - SLOTS) * NST + PRING)
                    for n, (kp, qp) in enumerate(zip(K_PART, Q_PART)):
                        rows = slice(g * HG * DH, (g + 1) * HG * DH)
                        sp.dma_start(ks[n * DH:(n + 1) * DH, g, :, :],
                                     t["k_dram"][b, kp, rows].rearrange("(j d) n -> d j n", d=DH)).then_inc(kq_in[g], 16)
                        sp.dma_start(qs[n * DH:(n + 1) * DH, g, :, :],
                                     t["q_dram"][b, qp, rows].rearrange("(j d) n -> d j n", d=DH)).then_inc(kq_in[g], 16)
                    sp.wait_ge(v_dense_used, u + 1)
                    sp.dma_start(vd[:, v_slot, :, :].rearrange("p a c -> p (a c)"), t["v_dram"][b, g]).then_inc(v_in[v_slot], 16)

                def rows_out(b, g):
                    u = b * G + g
                    sp.wait_ge(m_parts, u + 2)
                    for part in range(3):
                        sp.dma_start(qs[TERMS + part:TERMS + part + 1, g, :, :].rearrange("p j (q n) -> p (j q) n", n=P),
                                     mpart[:, part, :]).then_inc(m_in, 16)

                def heads_out(b, g):
                    sp.wait_ge(o_ready, b * G + g + 2)
                    for j in range(HG):
                        sp.dma_start(t["o_dram"][b, (g * HG + j) * DH:(g * HG + j + 1) * DH],
                                     o[j * 32:j * 32 + DH, :]).then_inc(o_stored, 16)

                sp.sem_inc(m_in, 1)
                sp.sem_inc(o_stored, 1)
                for g in range(G - 1):
                    load(0, g, False)
                rows_out(0, 0)
                load(0, G - 1, False)
                rows_out(0, 1)
                with sp.Fori(0, B - 1) as b:
                    for g in range(G):
                        load(b + 1, g)
                        rows_out(*((b, g + 2) if g + 2 < G else (b + 1, g + 2 - G)))
                        heads_out(b, g)
                for g in range(G):
                    if g + 2 < G:
                        rows_out(B - 1, g + 2)
                    heads_out(B - 1, g)
                sp.wait_ge(o_stored, 1 + UNITS * HG * 16)

            @block.tensor
            def _(pe):
                pe.sem_inc(pv, PRING)

                def max_product(b, g, u, n):
                    j, q, h = max_jobs[n]
                    if n == 0:
                        pe.wait_ge(kq_in[g], b * 16 * (NLOAD - 1) + 16 * (NLOAD - 1))
                        pe.wait_ge(m_parts, u + 1)
                    pe.wait_ge(m_red, u * len(max_jobs) + n + 1)
                    for a, w in spans(HALF if h == 0 else KEYS - HALF, 512):
                        ins = nc.tensor.matmul(ps_m[:, h, a:a + w], qs[0:TERMS, g, j, q * P:q * P + P],
                                               ks[0:TERMS, g, j, h * HALF + a:h * HALF + a + w], start=True, stop=True)
                    ins.then_inc(m_mm, 1)

                def turn_max(u):
                    pe.wait_ge(m_all, u + 1)
                    nc.tensor.transpose(ps_m[0:HG * QT, 0, 0:P], nmax[:, :], t["ident"][:, :]).then_inc(m_turned, 1)

                def scores(u, g, n):
                    kt, j = n // HG, n % HG
                    r = key_rows(kt)
                    pe.wait_ge(expd, u * NST + n + 1 + (SBANKS - 1 if g == n == 0 else 0))
                    nc.tensor.matmul(ps_s[0:r, (NST * g + n) % SBANKS, :], ks[:, g, j, kt * P:kt * P + r], qs[:, g, j, :],
                                     start=True, stop=True).then_inc(s_mm, 1)

                def values(u, g, n):
                    kt, j = n // HG, n % HG
                    r = key_rows(kt)
                    pe.wait_ge(expd, u * NST + n + 1 + SBANKS)
                    nc.tensor.matmul(ps_o[j * 32:(j + 1) * 32, :], vw[0:r, g % 2, kt * HG + j, :],
                                     pr[0:r, (NST * g + n) % PRING, :], start=kt == 0, stop=kt == KT - 1).then_inc(pv, 1)

                def first_scores(u, g):
                    pe.wait_ge(ones, g + 1)
                    pe.wait_ge(m_in, u * 48 + 49)
                    for j in range(HG):
                        scores(u, g, j)

                def unit(b, g):
                    u = b * G + g
                    nxt, over = ((b, x) if x < G else (b + 1, x - G) if b is not last else None for x in (g + 1, g + 2))
                    done, early = EARLY, 0
                    for kt in range(1, KT + 1):
                        if kt == KT and nxt is not None:
                            pe.wait_ge(ones, nxt[1] + 1)
                            pe.wait_ge(m_in, u * 48 + 97)
                        for j in range(HG):
                            tile = HG * (kt - 1) + j + 1
                            if kt < KT:
                                scores(u, g, kt * HG + j)
                            elif nxt is not None:
                                scores(u + 1, nxt[1], j)
                            todo = min(len(max_jobs), EARLY - (EARLY - len(max_jobs)) * tile // MAX_SPREAD)
                            while nxt is not None and done < todo:
                                max_product(nxt[0], nxt[1], u + 1, done)
                                done += 1
                            todo = max(0, EARLY * (tile - EARLY_AT) // (NST - EARLY_AT))
                            while over is not None and early < todo:
                                max_product(over[0], over[1], u + 2, early)
                                early += 1
                        if nxt is not None and kt == TURN_AT:
                            turn_max(u + 1)
                        if kt == 1:
                            pe.wait_ge(v_wide, u + 1)
                            pe.wait_ge(acc_out, u + 1)
                        for j in range(HG):
                            values(u, g, (kt - 1) * HG + j)

                last = B - 1
                for n in range(len(max_jobs)):
                    max_product(0, 0, 0, n)
                turn_max(0)
                for n in range(EARLY):
                    max_product(0, 1, 1, n)
                first_scores(0, 0)
                with pe.Fori(0, last) as b:
                    for g in range(G):
                        unit(b, g)
                for g in range(G):
                    unit(last, g)

            @block.scalar
            def _(act):
                act.sem_inc(expd, SBANKS)
                act.sem_inc(acc_out, 1)

                def exps(u, g, tiles):
                    for n in tiles:
                        r = key_rows(n // HG)
                        act.wait_ge(pv, u * NST + n + 1)
                        act.wait_ge(s_mm, u * NST + n + 1)
                        nc.scalar.activation(pr[0:r, (NST * g + n) % PRING, :], ps_s[0:r, (NST * g + n) % SBANKS, :],
                                             ACT.Exp, scale=SCALE).then_inc(expd, 1)

                def sums_out(u):
                    act.wait_ge(pv, (u + 1) * NST + PRING)
                    act.wait_ge(o_ready, u + 1)
                    nc.scalar.activation(acc[:, :], ps_o[:, :], ACT.Copy).then_inc(acc_out, 1)

                exps(0, 0, range(HG))
                with act.Fori(0, B - 1) as b:
                    for g in range(G):
                        exps(b * G + g, g, range(HG, NST))
                        exps(b * G + g + 1, (g + 1) % G, range(HG))
                        sums_out(b * G + g)
                for g in range(G):
                    exps((B - 1) * G + g, g, range(HG, NST))
                    if g + 1 < G:
                        exps((B - 1) * G + g + 1, g + 1, range(HG))
                    sums_out((B - 1) * G + g)

            @block.vector
            def _(dve):
                dve.sem_inc(m_red, MBANKS)
                dve.sem_inc(m_parts, 1)

                def invert(u, me, piece):
                    if piece == 0:
                        dve.wait_ge(acc_out, u + 2)
                        dve.wait_ge(o_ready, u + 1)
                        gate(dve, t["dve_gate"])
                        me.then(nc.vector.stream_shuffle(den[:, 0, :], acc[:, :], [DH + r % DH for r in range(32)]))
                    elif piece <= INVERT_IN:
                        cols = slice((piece - 1) * S // INVERT_IN, piece * S // INVERT_IN)
                        ins = nc.vector.reciprocal(den[:, 1, cols], den[:, 0, cols])
                        if piece == INVERT_IN:
                            ins.then_inc(inverted, 1)

                def maxima(u, me, behind=None):
                    for n, (j, q, h) in enumerate(max_jobs):
                        if behind is not None and n >= INVERT_AT and (n - INVERT_AT) % 4 == 0:
                            invert(behind, me, (n - INVERT_AT) // 4)
                        w = HALF if h == 0 else KEYS - HALF
                        dve.wait_ge(m_mm, u * len(max_jobs) + n + 1)
                        nc.vector.tensor_reduce(pmax[:, j * QT + q, h:h + 1], ps_m[:, h, 0:w], AX.X, ALU.max).then_inc(m_red, 1)
                    dve.wait_ge(m_red, (u + 1) * len(max_jobs) + MBANKS)
                    nc.vector.tensor_reduce(nmax[:, :], pmax[:, :, :], AX.X, ALU.max, negate=True).then_inc(m_all, 1)
                    dve.wait_ge(m_turned, u + 1)
                    dve.wait_ge(m_in, u * 48 + 1)
                    me.then(nc.vector.tensor_copy(mpart[:, 0, :], ps_m[0:HG * QT, 0, 0:P]))
                    me.then(nc.vector.tensor_tensor(mrest[:, 0, :], ps_m[0:HG * QT, 0, 0:P], mpart[:, 0, :], ALU.subtract))
                    me.then(nc.vector.tensor_copy(mpart[:, 1, :], mrest[:, 0, :]))
                    nc.vector.tensor_tensor(mpart[:, 2, :], mrest[:, 0, :], mpart[:, 1, :], ALU.subtract).then_inc(m_parts, 1)

                OWN_MAX, OWN = 3, 3 + 1
                for u in range(2):
                    maxima(u, Own(dve, own, u, OWN_MAX))
                with dve.Fori(1, UNITS - 1) as u:
                    me = Own(dve, own, u, OWN)
                    me.n = 2 * OWN_MAX - OWN
                    maxima(u + 1, me, u - 1)
                me = Own(dve, own, UNITS - 1, OWN)
                me.n = 2 * OWN_MAX - OWN
                for u in range(UNITS - 2, UNITS):
                    for piece in range(1 + INVERT_IN):
                        invert(u, me, piece)

            @block.gpsimd
            def _(pool):
                pool.sem_inc(v_dense_used, 2)
                pool.sem_inc(o_ready, 1)
                nc.gpsimd.memset(vw[:, :, :, :], 1.0).then_inc(v_ones, 1)
                pool.wait_ge(v_ones, 1)
                for s in range(SLOTS):
                    nc.gpsimd.memset(ks[TERMS:STACK, s, :, :], 1.0).then_inc(ones, 1)
                    pool.wait_ge(ones, s + 1)

                def spread(i, s, used=True):
                    u = 2 * i + s
                    pool.wait_ge(v_in[s], i * 16 + 16)
                    if used:
                        pool.wait_ge(pv, (u - 1) * NST + PRING)
                    gate(pool, t["pool_gate"])
                    nc.gpsimd.tensor_copy(vw[:, s, :, 0:DH], vd[:, s, :, :]).then_inc(v_wide, 1)
                    pool.wait_ge(v_wide, u + 1)
                    pool.sem_inc(v_dense_used, 1)

                def divide(u):
                    pool.wait_ge(inverted, u + 1)
                    pool.wait_ge(o_stored, u * 16 * HG + 1)
                    gate(pool, t["pool_gate"])
                    nc.gpsimd.tensor_tensor(o[:, :], acc[:, :], den[:, 1, :], ALU.mult).then_inc(o_ready, 1)

                spread(0, 0, False)
                spread(0, 1, False)
                with pool.Fori(1, UNITS // 2) as i:
                    for s in range(2):
                        spread(i, s)
                        divide(2 * i + s - 2)
                for u in range(UNITS - 2, UNITS):
                    divide(u)


E = 4
F = 4 * D
FC = F // P
TOK = 256
TQ = TOK // P
FULL_BLOCKS = B * S // TOK
MAX_BLOCKS = FULL_BLOCKS + E - 1
REGION = B * S + TOK


def route(nc, sem, t, st):
    NW = 7
    NOWN = 9
    with Stage(nc, "rt") as st_r:
        sb, ps = st_r.sb, st_r.ps
        oT = sb("oT", [P, 2, KC, S])
        wo, bo, one_row = sb("wo", [P, KC, D]), sb("bo", [1, D]), sb("one_row", [1, P])
        wr, br, iota = sb("wr", [P, KC, E]), sb("br", [P, E]), sb("iota", [P, E])
        base0, before_f = sb("base0", [P, E]), sb("before_f", [P, P])
        before, ones = sb("before", [P, P], BF16), sb("ones", [P, P], BF16)
        xn, xnT = sb("xn", [P, 2, QT, D]), sb("xnT", [P, KC, S])
        stats, mv = sb("stats", [P, QT, 6]), sb("mv", [P, QT, 2])
        ve, sd, rstd = sb("ve", [P, QT]), sb("sd", [P, QT]), sb("rstd", [P, QT])
        logit, top, at = sb("logit", [P, QT, 8]), sb("top", [P, QT, 8]), sb("at", [P, QT, 8], U32)
        atf, hot = sb("atf", [P, QT]), sb("hot", [P, QT + 1, E], BF16)
        place, slotf, slot = sb("place", [P, QT, E]), sb("slotf", [P, QT]), sb("slot", [P, 2, QT], U32)
        base, zeros = sb("base", [P, E]), sb("zeros", [P, TQ, D])
        rows, back = sb("rows", [P, 2, NT]), sb("back", [P, 2, NT])
        moved, step_ = sb("moved", [P, E]), sb("step", [P, E])
        count, blocks, blocks_u = sb("count", [P, E]), sb("blocks", [P, 1 + E]), sb("blocks_u", [P, E], U32)
        ps_o, ps_t = ps("pso", [P, 2, QT, D]), ps("pst", [P, KC, 512])
        ps_l, ps_r = ps("psl", [P, 512]), ps("psr", [P, 512])

        w_in, made, o_in = sem("rt_w"), sem("rt_made"), [sem("rt_o0"), sem("rt_o1")]
        projected, taken = sem("rt_projected"), sem("rt_taken")
        own_a, own_b, normed, var, sdr = sem("rt_own_a"), sem("rt_own_b"), sem("rt_normed"), sem("rt_var"), sem("rt_sd")
        turned, xnT_ready, routed, hot_ready = sem("rt_turned"), sem("rt_xnT"), sem("rt_routed"), sem("rt_hot")
        ranked, placed, scattered, xn_free = sem("rt_ranked"), sem("rt_placed"), sem("rt_scattered"), sem("rt_xn_free")
        counted, tailed = sem("rt_counted"), sem("rt_tailed")

        def steps(eng, first, step):
            first()
            with eng.Fori(0, B // 2 - 1) as i:
                for s in range(2):
                    step(i * 2 + s, s, 2)
            step(B - 2, 0, 1)
            step(B - 1, 1, 0)

        with nc.Block() as block:
            @block.sync
            def _(sp):
                sp.dma_start(oT[:, 0, :, :], t["o_dram"][0].rearrange("(k p) n -> p k n", p=P)).then_inc(o_in[0], 16)
                for dst, name in ((wo, "wo"), (bo, "bo"), (wr, "wr"), (br, "br"), (iota, "iota_e"), (base0, "base0"),
                                  (before_f, "before")):
                    sp.dma_start(dst.ap(), t[name + "_in"]).then_inc(w_in, 16)

                def heads_in(b, s):
                    sp.dma_start(oT[:, s, :, :], t["o_dram"][b].rearrange("(k p) n -> p k n", p=P)).then_inc(o_in[s], 16)

                heads_in(1, 1)
                for b in range(2, 4):
                    sp.wait_ge(projected, b - 1)
                    heads_in(b, b % 2)
                sp.wait_ge(counted, 1)
                for n in range(FULL_BLOCKS, MAX_BLOCKS):
                    sp.dma_start(t["ys_dram"][n].rearrange("(k p) d -> p k d", p=P), zeros[:, :, :]).then_inc(tailed, 16)
                for e in range(E):
                    sp.dma_start(st["w1"][:, e, :, :], t["w1_in"][:, e]).then_inc(st["w_in"], 16)
                    sp.dma_start(st["w2"][:, e, :, :], t["w2_in"][:, e]).then_inc(st["w_in"], 16)
                sp.dma_start(st["b1"][:, :], t["b1_in"]).then_inc(st["w_in"], 16)
                sp.dma_start(st["b2"][:, :, :], t["b2_in"]).then_inc(st["w_in"], 16)
                with sp.Fori(2, B // 2) as i:
                    for s in range(2):
                        sp.wait_ge(projected, i * 2 + s - 1)
                        heads_in(i * 2 + s, s)
                sp.wait_ge(counted, 2)
                for e in range(E):
                    n = sp.value_load(st["table"][0:1, 1 + E + e:2 + E + e], min_val=0, max_val=B * S)
                    sp.dma_start(t["xs_dram"][e, bass.ds(n, TOK)].rearrange("(k p) d -> p k d", p=P),
                                 zeros[:, :, :]).then_inc(tailed, 16)
                sp.wait_ge(tailed, 16 * (E + MAX_BLOCKS - FULL_BLOCKS))

            @block.tensor
            def _(pe):
                pe.wait_ge(w_in, 16 * NW)
                pe.wait_ge(made, 3)

                def project_heads(b, s):
                    pe.wait_ge(o_in[s], (b - s) * 8 + 16)
                    pe.wait_ge(taken, b + 1)
                    for q in range(QT):
                        for k in range(KC):
                            nc.tensor.matmul(ps_o[:, s, q, :], oT[:, s, k, q * P:q * P + P], wo[:, k, :],
                                             start=k == 0, stop=False)
                        ins = nc.tensor.matmul(ps_o[:, s, q, :], one_row[:, :], bo[:, :], start=False, stop=True)
                    ins.then_inc(projected, 1)

                def step(b, s, ahead):
                    pe.wait_ge(normed, (b + 1) * QT)
                    pe.wait_ge(xnT_ready, b + 1)
                    for q in range(QT):
                        for k in range(KC):
                            ins = nc.tensor.transpose(ps_t[:, k, q * P:q * P + P], xn[:, s, q, k * P:k * P + P],
                                                      t["ident"][:, :])
                    ins.then_inc(turned, 1)
                    pe.wait_ge(xnT_ready, b + 2)
                    for q in range(QT):
                        for k in range(KC):
                            ins = nc.tensor.matmul(ps_l[:, q * E:q * E + E], xnT[:, k, q * P:q * P + P], wr[:, k, :],
                                                   start=k == 0, stop=k == KC - 1)
                    ins.then_inc(routed, 1)
                    if ahead == 2:
                        project_heads(b + 2, s)
                    pe.wait_ge(hot_ready, b + 2)
                    pe.wait_ge(placed, b + 1)
                    nc.tensor.matmul(ps_r[:, 0:(QT + 1) * E], before[:, :], hot[:, :, :].rearrange("p q e -> p (q e)"),
                                     start=True, stop=False)
                    for q in range(QT):
                        ins = nc.tensor.matmul(ps_r[:, (q + 1) * E:(QT + 1) * E].rearrange("p (q e) -> p q e", e=E),
                                               ones[:, :], hot[:, q:q + 1, :].broadcast_to([P, QT - q, E]),
                                               start=False, stop=q == QT - 1)
                    ins.then_inc(ranked, 1)

                def first():
                    project_heads(0, 0)
                    project_heads(1, 1)

                steps(pe, first, step)

            @block.scalar
            def _(act):
                def root(b):
                    act.wait_ge(var, b + 1)
                    nc.scalar.activation(sd[:, :], ve[:, :], ACT.Sqrt).then_inc(sdr, 1)

                def step(b, s, ahead):
                    act.wait_ge(turned, b + 1)
                    act.wait_ge(routed, b + 1)
                    nc.scalar.activation(xnT[:, :, :], ps_t[:, :, :], ACT.Copy).then_inc(xnT_ready, 1)
                    if ahead:
                        root(b + 1)

                act.sem_inc(xnT_ready, 1)
                act.sem_inc(routed, 1)
                steps(act, lambda: root(0), step)

            @block.vector
            def _(dve):
                nc.vector.memset(logit[:, :, :], -3.0e38)
                nc.vector.memset(back[:, :, :], 0.0)
                nc.vector.memset(hot[:, :, :], 0.0).then_inc(hot_ready, 1)
                nc.vector.memset(one_row[:, :], 1.0).then_inc(made, 1)
                nc.vector.memset(ones[:, :], 1.0).then_inc(made, 1)
                dve.wait_ge(hot_ready, 1)
                dve.wait_ge(w_in, 16 * NW)
                nc.vector.tensor_copy(base[:, :], base0[:, :])
                nc.vector.tensor_copy(before[:, :], before_f[:, :]).then_inc(made, 1)
                dve.wait_ge(made, 3)
                dve.sem_inc(taken, 2)
                dve.sem_inc(placed, 1)

                def residual(b, s):
                    me = Own(dve, own_a, b, 4)
                    tiles = t["x"][:, bass.ds(b * QT, QT), :]
                    dve.wait_ge(projected, b + 1)
                    me.then(nc.vector.scalar_tensor_tensor(tiles, ps_o[:, s, :, :], t["gate_x"](0), tiles,
                                                           ALU.mult, ALU.add))
                    dve.sem_inc(taken, 1)
                    dve.wait_ge(xn_free, b + 1)
                    norm_tiles(nc, dve, me, lambda q: t["x_tile"](b * QT + q), lambda q: xn[:, s, q, :],
                               stats, mv, ve, rstd, t["dve_gate"], var, (sdr, b + 1), sd, normed)
                    assert me.n == 4, me.n

                def step(b, s, ahead):
                    if ahead:
                        residual(b + 1, 1 - s)
                    me = Own(dve, own_b, b, NOWN)
                    dve.wait_ge(routed, b + 2)
                    me.then(nc.vector.tensor_tensor(logit[:, :, 0:E], ps_l[:, 0:QT * E].rearrange("p (q e) -> p q e", e=E),
                                                    br[:, :].unsqueeze(1).broadcast_to([P, QT, E]), ALU.add))
                    gate(dve, t["dve_gate"])
                    for q in range(QT):
                        ins = nc.vector.max(top[:, q, :], logit[:, q, :])
                    me.then(ins)
                    gate(dve, t["dve_gate"])
                    for q in range(QT):
                        ins = nc.vector.max_index(at[:, q, :], top[:, q, :], logit[:, q, :])
                    me.then(ins)
                    me.then(nc.vector.tensor_copy(atf[:, :], at[:, :, 0]))
                    nc.vector.tensor_tensor(hot[:, 0:QT, :], iota[:, :].unsqueeze(1).broadcast_to([P, QT, E]),
                                            atf[:, :].unsqueeze(2).broadcast_to([P, QT, E]), ALU.is_equal).then_inc(hot_ready, 1)
                    dve.wait_ge(ranked, b + 1)
                    me.then(nc.vector.tensor_tensor(place[:, :, :], ps_r[:, 0:QT * E].rearrange("p (q e) -> p q e", e=E),
                                                    base[:, :].unsqueeze(1).broadcast_to([P, QT, E]), ALU.add))
                    me.then(nc.vector.tensor_tensor(place[:, :, :], place[:, :, :], hot[:, 0:QT, :], ALU.mult))
                    me.then(nc.vector.tensor_tensor(base[:, :], base[:, :], ps_r[:, QT * E:(QT + 1) * E], ALU.add))
                    me.then(nc.vector.tensor_reduce(slotf[:, :], place[:, :, :], AX.X, ALU.add))
                    nc.vector.tensor_copy(slot[:, s, :], slotf[:, :])
                    me.then(nc.vector.tensor_copy(rows[:, 0, bass.ds(b * QT, QT)], slotf[:, :]))
                    dve.sem_inc(placed, 1)

                steps(dve, lambda: residual(0, 0), step)
                me = Own(dve, own_b, B, NOWN)
                me.then(nc.vector.tensor_tensor(count[:, :], base[:, :], base0[:, :], ALU.subtract))
                me.then(nc.vector.tensor_scalar(blocks_u[:, :], count[:, :], float(TOK - 1), None, ALU.add))
                me.then(nc.vector.tensor_scalar(blocks_u[:, :], blocks_u[:, :], TOK.bit_length() - 1, None,
                                                ALU.logical_shift_right))
                me.then(nc.vector.memset(blocks[:, 0:1], 0.0))
                me.then(nc.vector.tensor_copy(blocks[:, 1:1 + E], blocks_u[:, :]))
                me.then(nc.vector.tensor_scalar(blocks[:, 1:1 + E], blocks[:, 1:1 + E], 1.0, None, ALU.max))
                for e in range(1, E):
                    me.then(nc.vector.tensor_tensor(blocks[:, 1 + e:2 + e], blocks[:, 1 + e:2 + e], blocks[:, e:e + 1], ALU.add))
                nc.vector.tensor_copy(st["table"][:, 0:1 + E], blocks[:, :])
                me.then(nc.vector.scalar_tensor_tensor(moved[:, :], blocks[:, 0:E], -float(TOK), base0[:, :], ALU.mult, ALU.add))
                me.then(nc.vector.tensor_tensor(step_[:, 1:E], moved[:, 1:E], moved[:, 0:E - 1], ALU.subtract))
                for e in range(1, E):
                    me.then(nc.vector.tensor_scalar(rows[:, 1, :], rows[:, 0, :], float(e * REGION), step_[:, e:e + 1],
                                                    ALU.is_ge, ALU.mult))
                    me.then(nc.vector.tensor_tensor(back[:, e % 2, :], rows[:, 1, :], back[:, 1 - e % 2, :], ALU.add))
                nc.vector.tensor_tensor(t["slots"][:, :], rows[:, 0, :], back[:, (E - 1) % 2, :], ALU.subtract)
                nc.vector.tensor_copy(st["table"][:, 1 + E:1 + 2 * E], count[:, :]).then_inc(counted, 1)

            @block.gpsimd
            def _(pool):
                nc.gpsimd.memset(zeros[:, :, :], 0.0).then_inc(counted, 1)
                pool.sem_inc(xn_free, 2)

                def step(b, s, ahead):
                    pool.wait_ge(placed, b + 2)
                    gate(pool, t["pool_gate"])
                    for q in range(QT):
                        nc.gpsimd.indirect_dma_start(
                            out=t["xs_rows"], out_offset=bass.IndirectOffsetOnAxis(ap=slot[:, s, q:q + 1], axis=0),
                            in_=xn[:, s, q, :], in_offset=None).then_inc(scattered, 16)
                    pool.wait_ge(scattered, b * 16 * QT + 16 * QT)
                    pool.sem_inc(xn_free, 1)

                steps(pool, lambda: None, step)


def experts(nc, sem, t):
    with Stage(nc, "ex") as stage:
        w1, b1 = stage.sb("w1", [P, E, KC, F]), stage.sb("b1", [P, E * FC])
        w2, b2 = stage.sb("w2", [P, E, FC, D]), stage.sb("b2", [P, E, D])
        table = stage.sb("table", [P, 1 + 2 * E], I32)
        w_in = sem("ex_w")
        route(nc, sem, t, {"w1": w1, "b1": b1, "w2": w2, "b2": b2, "table": table, "w_in": w_in})

        xs, xsT = stage.sb("xs", [P, TQ, D]), stage.sb("xsT", [P, KC, TOK])
        hid, y = stage.sb("hid", [P, FC, TOK]), stage.sb("y", [P, TQ, D])
        HB = 4
        ps_h, ps_o, ps_t = stage.ps("psh", [P, HB, 512]), stage.ps("pso", [P, TQ, 512]), stage.ps("pst", [P, KC, TOK])
        xs_in, turned, xsT_ready = sem("ex_xs"), sem("ex_turned"), sem("ex_xsT")
        up, relud, down, y_ready, y_stored = sem("ex_up"), sem("ex_relu"), sem("ex_down"), sem("ex_y"), sem("ex_stored")

        def starts(eng):
            return [eng.value_load(table[0:1, e:e + 1], min_val=0 if e == 0 else e, max_val=MAX_BLOCKS)
                    for e in range(E + 1)]

        def rows_of(dram, e, n, first):
            row = nc.s_assert_within((n - first) * TOK, 0, REGION - TOK, skip_runtime_bounds_check_because=
                                     "an expert has at most B * S tokens, so n - first <= B * S / TOK")
            return dram[e, bass.ds(row, TOK)].rearrange("(k p) d -> p k d", p=P)

        with nc.Block() as block:
            @block.sync
            def _(sp):
                sp.sem_inc(turned, 1)
                first = starts(sp)
                for e in range(E):
                    with sp.Fori(first[e], first[e + 1]) as n:
                        sp.wait_ge(turned, n + 1)
                        sp.dma_start(xs[:, :, :], rows_of(t["xs_dram"], e, n, first[e])).then_inc(xs_in, 16)
                sp.wait_ge(turned, first[E] + 1)
                sp.dma_start(xs[:, :, :], t["xs_dram"][0, 0:TOK].rearrange("(k p) d -> p k d", p=P)).then_inc(xs_in, 16)

            @block.tensor
            def _(pe):
                pe.wait_ge(w_in, 16 * (2 * E + 2))
                first = starts(pe)

                def turn(n):
                    pe.wait_ge(xs_in, n * 16 + 16)
                    pe.wait_ge(xsT_ready, n + 1)
                    for q in range(TQ):
                        for k in range(KC):
                            ins = nc.tensor.transpose(ps_t[:, k, q * P:q * P + P], xs[:, q, k * P:k * P + P],
                                                      t["ident"][:, :])
                    ins.then_inc(turned, 1)

                turn(0)
                for e in range(E):
                    with pe.Fori(first[e], first[e + 1]) as n:
                        def up_product(c):
                            pe.wait_ge(relud, n * FC + c + 1)
                            for k in range(KC):
                                ins = nc.tensor.matmul(ps_h[:, c % HB, 0:TOK], w1[:, e, k, c * P:c * P + P], xsT[:, k, :],
                                                       start=k == 0, stop=k == KC - 1)
                            ins.then_inc(up, 1)

                        def down_product(c):
                            pe.wait_ge(relud, n * FC + c + 1 + HB)
                            for q in range(TQ):
                                ins = nc.tensor.matmul(ps_o[:, q, 0:D], hid[:, c, q * P:q * P + P], w2[:, e, c, :],
                                                       start=c == 0, stop=c == FC - 1)
                            ins.then_inc(down, 1)

                        pe.wait_ge(xsT_ready, n + 2)
                        for c in range(FC + 2):
                            if c < FC:
                                up_product(c)
                            if c == FC // 2:
                                turn(n + 1)
                            if c == 2:
                                pe.wait_ge(y_ready, n + 1)
                            if c >= 2:
                                down_product(c - 2)

            @block.scalar
            def _(act):
                act.sem_inc(relud, HB)
                act.sem_inc(down, 1)
                act.wait_ge(w_in, 16 * (2 * E + 2))
                first = starts(act)
                for e in range(E):
                    with act.Fori(first[e], first[e + 1]) as n:
                        act.wait_ge(down, n * FC + 1)
                        for c in range(FC):
                            act.wait_ge(up, n * FC + c + 1)
                            nc.scalar.activation(hid[:, c, :], ps_h[:, c % HB, 0:TOK], ACT.Relu,
                                                 bias=b1[:, e * FC + c:e * FC + c + 1]).then_inc(relud, 1)
                        act.wait_ge(y_ready, n + 2)
                        act.dma_start(t["ys_dram"][bass.ds(n, 1)].rearrange("a (k p) d -> p (a k) d", p=P),
                                      y[:, :, :]).then_inc(y_stored, 16)
                act.wait_ge(y_stored, first[E] * 16 + 1)
                gate(act, t["act_gate"])

            @block.vector
            def _(dve):
                dve.sem_inc(xsT_ready, 1)
                dve.sem_inc(y_ready, 1)
                dve.sem_inc(y_stored, 1)
                dve.wait_ge(w_in, 16 * (2 * E + 2))
                first = starts(dve)
                dve.wait_ge(turned, 2)
                nc.vector.tensor_copy(xsT[:, :, :], ps_t[:, :, :]).then_inc(xsT_ready, 1)
                for e in range(E):
                    with dve.Fori(first[e], first[e + 1]) as n:
                        dve.wait_ge(turned, n + 3)
                        dve.wait_ge(up, n * FC + FC)
                        nc.vector.tensor_copy(xsT[:, :, :], ps_t[:, :, :]).then_inc(xsT_ready, 1)
                        dve.wait_ge(down, n * FC + FC + 1)
                        dve.wait_ge(y_stored, n * 16 + 1)
                        nc.vector.tensor_tensor(y[:, :, :], ps_o[:, :, 0:D],
                                                b2[:, e, :].unsqueeze(1).broadcast_to([P, TQ, D]), ALU.add).then_inc(y_ready, 1)


def attend_wide(nc, sem, t):
    R = 16
    SCALE = 1.0 / float(D) ** 0.5
    GR = [(a, min(4, KT - a)) for a in range(0, KT, 4)]
    NG = len(GR)
    with Stage(nc, "aw") as st:
        ctxT, ctx = st.sb("ctxT", [P, 2, KC, KEYS]), st.sb("ctx", [P, KT, D])
        wgt = {n: st.sb(n, [P, KC, D]) for n in ("q", "k", "v", "oT")}
        low = {n: (st.sb(n + "a", [R, D]), st.sb(n + "bT", [R, D])) for n in "qkv"}
        full = {n: st.sb(n + "f", [P, KC, D]) for n in "qkv"}
        amat, cmat = st.sb("amat", [P, KC, D]), st.sb("cmat", [P, KC, D])
        xn, xnT, gT = st.sb("xn", [P, QT, D]), st.sb("xnT", [P, KC, S]), st.sb("gT", [P, KC, S])
        prob, pT, uT = st.sb("prob", [P, KEYS]), st.sb("pT", [P, 2, KT, S]), st.sb("uT", [P, KC, S])
        peak, shift, den = st.sb("peak", [P, QT]), st.sb("shift", [P, QT]), st.sb("den", [P, QT])
        fac = st.sb("fac", [P, QT])
        stats, mv = st.sb("stats", [P, QT, 6]), st.sb("mv", [P, QT, 2])
        ve, sd, rstd = st.sb("ve", [P, QT]), st.sb("sd", [P, QT]), st.sb("rstd", [P, QT])
        y, slot = st.sb("y", [P, QT, D]), st.sb("slot", [P, QT], U32)
        xl, xlT = st.sb("xl", [P, QT, D]), st.sb("xlT", [P, KC, S])
        ve_l, sd_l, rstd_l = st.sb("ve_l", [P, QT]), st.sb("sd_l", [P, QT]), st.sb("rstd_l", [P, QT])
        ps_s, ps_p, ps_w = st.ps("pss", [P, 4, 512]), st.ps("psp", [P, 2, 4, P]), st.ps("psw", [P, KC, 512])

        y_in, y_used, slot_ready = sem("aw_y"), sem("aw_y_used"), sem("aw_slot")
        w_in, ctxT_in, ctx_in = sem("aw_w"), [sem("aw_ctxT0"), sem("aw_ctxT1")], sem("aw_ctx")
        mixed, mixed_out = sem("aw_mixed"), sem("aw_mixed_out")
        own_n, own_p, normed, var, sdr = sem("aw_own_n"), sem("aw_own_p"), sem("aw_normed"), sem("aw_var"), sem("aw_sd")
        s_mm, peaked, expd, p_turned, p_out = (sem(f"aw_{n}") for n in ("s_mm", "peaked", "exp", "p_turned", "p_out"))
        n_turned, xnT_out, a_mm, gT_out = (sem(f"aw_{n}") for n in ("n_turned", "xnT_out", "a_mm", "gT_out"))
        u_mm, uT_out, o_mm, o_out = (sem(f"aw_{n}") for n in ("u_mm", "uT_out", "o_mm", "o_out"))

        own_l, l_normed, l_var, l_sd = (sem(f"aw_last_{n}") for n in ("own", "normed", "var", "sd"))
        l_turned, l_out, l_counted, l_stored = (sem(f"aw_last_{n}") for n in ("turned", "out", "counted", "stored"))

        def steps(eng, step):
            step(0, 0, 0, True)
            step(1, 1, 1, True)
            with eng.Fori(1, B // 2 - 1) as i:
                for o in range(2):
                    step(i * 2 + o, o, 2, True)
            step(B - 2, 0, 2, True)
            step(B - 1, 1, 2, False)

        with nc.Block() as block:
            @block.sync
            def _(sp):
                for n in ("q", "k", "v", "oT"):
                    sp.dma_start(wgt[n][:, :, :], t["l1_" + n + "_in"]).then_inc(w_in, 16)
                for n in "qkv":
                    sp.dma_start(low[n][0][:, :], t["l1_" + n + "a_in"]).then_inc(w_in, 16)
                    sp.dma_start(low[n][1][:, :], t["l1_" + n + "bT_in"]).then_inc(w_in, 16)

                def turned_in(b, s):
                    sp.dma_start(ctxT[:, s, :, :], t["ctxT_in"][b]).then_inc(ctxT_in[s], 16)

                def rows_in(b):
                    sp.dma_start(ctx[:, 0:KT - 1, :], t["ctx_in"][b, 0:(KT - 1) * P].rearrange("(k p) d -> p k d", p=P))\
                        .then_inc(ctx_in, 16)
                    sp.dma_start(ctx[0:key_rows(KT - 1), KT - 1, :], t["ctx_in"][b, (KT - 1) * P:KEYS]).then_inc(ctx_in, 16)

                def step(b, s, ahead):
                    sp.wait_ge(u_mm, b)
                    rows_in(b)
                    if ahead:
                        sp.wait_ge(s_mm, (b + 1) * QT)
                        turned_in(b + 2, s)

                def last_out(b):
                    sp.wait_ge(l_out, b + 1)
                    sp.dma_start(t["x_dram"][bass.ds(b * QT, QT)].rearrange("q p d -> p q d"),
                                 t["x"][:, bass.ds(b * QT, QT), :]).then_inc(l_stored, 16)
                    for k in range(KC):
                        sp.dma_start(t["xT_dram"][bass.ds(b * QT, QT), :, k, :].rearrange("q p n -> p q n"),
                                     xlT[:, k, :].rearrange("p (q n) -> p q n", n=P)).then_inc(l_stored, 16)

                sp.sem_inc(l_stored, 1)
                turned_in(0, 0)
                turned_in(1, 1)
                rows_in(0)
                sp.wait_ge(s_mm, QT)
                turned_in(2, 0)
                step(1, 1, True)
                with sp.Fori(1, B // 2 - 1) as i:
                    for o in range(2):
                        step(i * 2 + o, o, True)
                        last_out(i * 2 + o - 2)
                for b in range(B - 2, B):
                    step(b, b % 2, False)
                    last_out(b - 2)
                for b in range(B - 2, B):
                    last_out(b)
                sp.wait_ge(l_stored, 16 * (1 + KC) * B + 1)

            @block.tensor
            def _(pe):
                pe.wait_ge(w_in, 160)
                for n, name in enumerate("qkv"):
                    if n:
                        pe.wait_ge(mixed_out, n)
                    for m in range(KC):
                        ins = nc.tensor.matmul(ps_w[:, m, 0:D], low[name][1][:, m * P:m * P + P], low[name][0][:, :],
                                               start=True, stop=True)
                    ins.then_inc(mixed, 1)
                for n, (left_, right) in enumerate(((full["q"], full["k"]), (full["v"], wgt["oT"]))):
                    pe.wait_ge(mixed_out, 3 + n)
                    for m in range(KC):
                        for k in range(KC):
                            ins = nc.tensor.matmul(ps_w[:, m, 0:D], left_[:, k, m * P:m * P + P], right[:, k, :],
                                                   start=k == 0, stop=k == KC - 1)
                    ins.then_inc(mixed, 1)
                pe.wait_ge(mixed_out, 5)

                def turn_norms(b):
                    pe.wait_ge(normed, (b + 1) * QT)
                    for k in range(KC):
                        for q in range(QT):
                            ins = nc.tensor.transpose(ps_p[:, k, q, :], xn[:, q, k * P:k * P + P], t["ident"][:, :])
                    ins.then_inc(n_turned, 1)

                def turn_last(b):
                    pe.wait_ge(l_normed, (b + 1) * QT)
                    for k in range(KC):
                        for q in range(QT):
                            ins = nc.tensor.transpose(ps_p[:, k, q, :], xl[:, q, k * P:k * P + P], t["ident"][:, :])
                    ins.then_inc(l_turned, 1)

                def a_product(b):
                    pe.wait_ge(xnT_out, b + 1)
                    for m in range(KC):
                        for k in range(KC):
                            ins = nc.tensor.matmul(ps_w[:, m, :], amat[:, k, m * P:m * P + P], xnT[:, k, :],
                                                   start=k == 0, stop=k == KC - 1)
                    ins.then_inc(a_mm, 1)

                def score_rows(b, s, q):
                    for n, (a, w) in enumerate(KEY_SPANS):
                        for k in range(KC):
                            ins = nc.tensor.matmul(ps_s[:, n, 0:w], gT[:, k, q * P:q * P + P], ctxT[:, s, k, a:a + w],
                                                   start=k == 0, stop=k == KC - 1)
                    ins.then_inc(s_mm, 1)

                def turn_probs(b, q):
                    pe.wait_ge(expd, b * QT + q + 1)
                    for n, (a, m) in enumerate(GR):
                        pe.wait_ge(p_out, (b * QT + q) * NG + n + 1)
                        for kt in range(a, a + m):
                            r = key_rows(kt)
                            ins = nc.tensor.transpose(ps_p[0:r, n % 2, kt - a, :], prob[:, kt * P:kt * P + r],
                                                      t["ident"][:, :])
                        ins.then_inc(p_turned, 1)

                def u_product(s, m, kts):
                    for kt in kts:
                        r = key_rows(kt)
                        ins = nc.tensor.matmul(ps_w[:, m, :], ctx[0:r, kt, m * P:m * P + P], pT[0:r, s, kt, :],
                                               start=kt == 0, stop=kt == KT - 1)
                    return ins

                def out_product(b):
                    pe.wait_ge(uT_out, b + 1)
                    for q in range(QT):
                        for k in range(KC):
                            ins = nc.tensor.matmul(ps_w[:, q // 2, (q % 2) * D:(q % 2) * D + D], uT[:, k, q * P:q * P + P],
                                                   cmat[:, k, :], start=k == 0, stop=k == KC - 1)
                    ins.then_inc(o_mm, 1)

                def step(b, s, back, ahead):
                    pe.wait_ge(gT_out, b + 1)
                    pe.wait_ge(ctxT_in[s], (b - s) * 8 + 16)
                    score_rows(b, s, 0)
                    if back:
                        pe.wait_ge(ctx_in, b * 32)
                        pe.wait_ge(p_out, b * QT * NG + 2)
                        u_product(1 - s, 0, range(KT))
                    turn_probs(b, 0)
                    score_rows(b, s, 1)
                    if back:
                        u_product(1 - s, 1, range(KT // 2))
                    turn_probs(b, 1)
                    score_rows(b, s, 2)
                    if ahead:
                        pe.wait_ge(p_out, (b * QT + 2) * NG + 2)
                        turn_norms(b + 1)
                    if back:
                        u_product(1 - s, 1, range(KT // 2, KT)).then_inc(u_mm, 1)
                    if ahead:
                        pe.wait_ge(xnT_out, b + 2)
                    turn_probs(b, 2)
                    score_rows(b, s, 3)
                    if back > 1:
                        pe.wait_ge(p_out, (b * QT + 3) * NG + 2)
                        turn_last(b - 2)
                    if back:
                        out_product(b - 1)
                    if back > 1:
                        pe.wait_ge(l_out, b - 1)
                    turn_probs(b, 3)
                    if ahead:
                        if back:
                            pe.wait_ge(o_out, b)
                        a_product(b + 1)

                turn_norms(0)
                a_product(0)
                steps(pe, step)
                pe.wait_ge(ctx_in, B * 32)
                pe.wait_ge(p_out, B * QT * NG + 2)
                pe.wait_ge(o_out, B - 1)
                for m in range(KC):
                    ins = u_product(1, m, range(KT))
                ins.then_inc(u_mm, 1)
                turn_last(B - 2)
                out_product(B - 1)
                pe.wait_ge(l_out, B - 1)
                turn_last(B - 1)

            @block.scalar
            def _(act):
                def root(b):
                    act.wait_ge(var, b + 1)
                    nc.scalar.activation(sd[:, :], ve[:, :], ACT.Sqrt).then_inc(sdr, 1)

                def copy(dst, src, ready, n, done):
                    act.wait_ge(ready, n)
                    nc.scalar.activation(dst, src, ACT.Copy).then_inc(done, 1)

                def norms_out(b):
                    copy(xnT[:, :, :].rearrange("p k (q n) -> p k q n", n=P), ps_p[:, :, :, :], n_turned, b + 1, xnT_out)

                def last_root(b):
                    act.wait_ge(l_var, b + 1)
                    nc.scalar.activation(sd_l[:, :], ve_l[:, :], ACT.Sqrt).then_inc(l_sd, 1)

                def last_out(b):
                    act.wait_ge(l_stored, b * 16 * (1 + KC) + 1)
                    act.wait_ge(l_counted, b + 1)
                    copy(xlT[:, :, :].rearrange("p k (q n) -> p k q n", n=P), ps_p[:, :, :, :], l_turned, b + 1, l_out)

                def step(b, s, back, ahead):
                    for q in range(QT):
                        if q == 2 and back > 1:
                            last_root(b - 2)
                        if q == 3 and back > 1:
                            last_out(b - 2)
                        act.wait_ge(peaked, b * QT + q + 1)
                        nc.scalar.activation(prob[:, :], ps_s[:, :, :].rearrange("p a n -> p (a n)")[:, 0:KEYS],
                                             ACT.Exp, bias=shift[:, q:q + 1], scale=SCALE,
                                             accum_out=den[:, q:q + 1]).then_inc(expd, 1)
                        if q == 0 and ahead:
                            root(b + 1)
                        if q == 2 and ahead:
                            norms_out(b + 1)
                        if q == 2 and back:
                            copy(uT[:, :, :], ps_w[:, :, :], u_mm, b, uT_out)
                    if ahead:
                        copy(gT[:, :, :], ps_w[:, :, :], a_mm, b + 2, gT_out)

                root(0)
                norms_out(0)
                copy(gT[:, :, :], ps_w[:, :, :], a_mm, 1, gT_out)
                steps(act, step)
                last_root(B - 2)
                copy(uT[:, :, :], ps_w[:, :, :], u_mm, B, uT_out)
                last_out(B - 2)
                last_root(B - 1)
                last_out(B - 1)

            @block.vector
            def _(dve):
                dve.sem_inc(p_out, 2)
                dve.sem_inc(y_used, 1)
                dve.wait_ge(w_in, 160)
                for n, name in enumerate("qkv"):
                    dve.wait_ge(mixed, n + 1)
                    nc.vector.tensor_tensor(full[name][:, :, :], ps_w[:, :, 0:D], wgt[name][:, :, :],
                                            ALU.add).then_inc(mixed_out, 1)
                for n, dst in enumerate((amat, cmat)):
                    dve.wait_ge(mixed, n + 4)
                    nc.vector.tensor_copy(dst[:, :, :], ps_w[:, :, 0:D]).then_inc(mixed_out, 1)

                def norms(b):
                    me = Own(dve, own_n, b, 4)
                    dve.wait_ge(y_in, b * 16 * QT + 16 * QT)
                    tiles = t["x"][:, bass.ds(b * QT, QT), :]
                    me.then(nc.vector.scalar_tensor_tensor(tiles, y[:, :, :], t["gate_f"](0), tiles, ALU.mult, ALU.add))
                    dve.sem_inc(y_used, 1)
                    norm_tiles(nc, dve, me, lambda q: t["x_tile"](b * QT + q), lambda q: xn[:, q, :],
                               stats, mv, ve, rstd, t["dve_gate"], var, (sdr, b + 1), sd, normed)

                def find_peak(me, b, q):
                    dve.wait_ge(s_mm, b * QT + q + 1)
                    me.then(nc.vector.tensor_reduce(peak[:, q:q + 1],
                                                    ps_s[:, :, :].rearrange("p a n -> p (a n)")[:, 0:KEYS],
                                                    AX.X, ALU.max))
                    nc.vector.tensor_scalar(shift[:, q:q + 1], peak[:, q:q + 1], -SCALE, None,
                                            ALU.mult).then_inc(peaked, 1)

                def probs_out(b, s, q):
                    for n, (a, m) in enumerate(GR):
                        r = key_rows(a + m - 1)
                        dve.wait_ge(p_turned, (b * QT + q) * NG + n + 1)
                        nc.vector.tensor_copy(pT[0:r, s, a:a + m, q * P:q * P + P], ps_p[0:r, n % 2, 0:m, :]).then_inc(p_out, 1)

                def add_out(b):
                    dve.wait_ge(o_mm, b + 1)
                    for q in range(QT):
                        ins = nc.vector.scalar_tensor_tensor(t["x_tile"](b * QT + q),
                                                             ps_w[:, q // 2, (q % 2) * D:(q % 2) * D + D],
                                                             fac[:, q:q + 1], t["x_tile"](b * QT + q), ALU.mult, ALU.add)
                    ins.then_inc(o_out, 1)

                def step(b, s, back, ahead):
                    me = Own(dve, own_p, b, QT + 2)
                    for q in range(QT):
                        find_peak(me, b, q)
                        if q == 0 and ahead:
                            norms(b + 1)
                        if q == QT - 1 and back:
                            add_out(b - 1)
                        probs_out(b, s, q)
                        if q == QT - 1 and back > 1:
                            last_stats(b - 2)
                        if q == 1 and back > 1:
                            last_norms(b - 2)
                    dve.wait_ge(expd, (b + 1) * QT)
                    if back:
                        dve.wait_ge(o_out, b)
                    me.then(nc.vector.reciprocal(fac[:, :], den[:, :]))
                    me.then(nc.vector.tensor_scalar(fac[:, :], fac[:, :], t["gate_x"](1), None, ALU.mult))

                def last_norms(b):
                    me = Own(dve, own_l, b, 3)
                    norm_tiles(nc, dve, me, lambda q: t["x_tile"](b * QT + q), lambda q: xl[:, q, :],
                               stats, mv, ve_l, rstd_l, t["dve_gate"], l_var, (l_sd, b + 1), sd_l, l_normed)

                def last_stats(b):
                    dve.wait_ge(l_out, b + 1)
                    gate(dve, t["dve_gate"])
                    for k in range(KC):
                        ins = nc.vector.bn_stats(t["bstats"][:, k, bass.ds(b, 1), :].rearrange("p a c -> p (a c)"), xlT[:, k, :])
                    ins.then_inc(l_counted, 1)

                dve.sem_inc(l_counted, 1)
                norms(0)
                steps(dve, step)
                last_norms(B - 2)
                last_stats(B - 2)
                add_out(B - 1)
                dve.wait_ge(o_out, B)
                last_norms(B - 1)
                last_stats(B - 1)

            @block.gpsimd
            def _(pool):
                with pool.Fori(0, B) as b:
                    pool.wait_ge(y_used, b + 1)
                    gate(pool, t["pool_gate"])
                    nc.gpsimd.tensor_copy(slot[:, :], t["slots"][:, bass.ds(b * QT, QT)]).then_inc(slot_ready, 1)
                    pool.wait_ge(slot_ready, b + 1)
                    gate(pool, t["pool_gate"])
                    for q in range(QT):
                        nc.gpsimd.indirect_dma_start(
                            out=y[:, q, :], out_offset=None, in_=t["ys_rows"],
                            in_offset=bass.IndirectOffsetOnAxis(ap=slot[:, q:q + 1], axis=0)).then_inc(y_in, 16)


MH, NK, KD = 8, 64, 128
TOP = 8
SEL = MH * TOP
YH = NK // 2
HT = P // 2


def memory(nc, sem, t, out):
    TB = 16
    NB = HT // TB * 2
    YB = 4
    ND = YH // YB
    WP = 2
    HALVES = [(m, c) for m in range(KC) for c in range(2)]
    QN = 2 + WP
    UP = 2.0 ** 15
    with Stage(nc, "mt") as st:
        key_in, key_out = st.sb("key_in", [P, KC, YH, P]), st.sb("key_out", [P, YH, D])
        iota_m, iota8 = st.sb("iota_m", [P, P, TB], F16), st.sb("iota8", [P, TOP])
        identb = st.sb("identb", [P, P], F16)
        iota_f, gate_down = st.sb("iota_f", [P, P]), st.sb("gate_down", [P, 1])
        xl, xb = st.sb("xl", [P, 2, KC, P]), st.sb("xb", [P, 2, KC, P])
        xr, o = st.sb("xr", [P, 2, D]), st.sb("o", [P, 2, D])
        sims = st.sb("sims", [P, 2 * MH, NK])
        s8, i8, i8f = st.sb("s8", [P, 2 * MH, TOP]), st.sb("i8", [P, 2 * MH, TOP], U32), st.sb("i8f", [P, 2 * MH, TOP])
        pairs = st.sb("pairs", [P, MH, TOP, TOP])
        best, rank = st.sb("best", [P, MH, TOP]), st.sb("rank", [P, MH, TOP], U32)
        ab, abf = st.sb("ab", [P, 2, SEL], U32), st.sb("abf", [P, 2, SEL])
        match = st.sb("match", [P, 2 * MH, TOP, TOP])
        xy, ge = st.sb("xy", [P, 2, SEL]), st.sb("ge", [P, SEL])
        diff, ew, den, w, wr = (st.sb("diff", [P, MH, TOP]), st.sb("ew", [P, MH, TOP]), st.sb("den", [P, 2, MH]),
                                st.sb("w", [P, MH, TOP]), st.sb("wrest", [P, SEL]))
        picks, picksT = st.sb("picks", [P, 2, QN, SEL], F16), st.sb("picksT", [P, QN, HT], F16)
        hot_m, hot_y = st.sb("hot_m", [P, 2, P, HT], F16), st.sb("hot_y", [P, YH, HT], F16)
        hot_w = st.sb("hot_w", [P, 2, WP, YH, HT], F16)
        g = st.sb("g", [P, 2, YH, P])
        ps_c, ps_d = st.ps("psc", [P, 2, 2, 512]), st.ps("psd", [P, 2, 512])
        ps_u, ps_x = st.ps("psu", [P, 512]), st.ps("psx", [P, 1024], F16)
        ps_sim = ps_x[:, :].bitcast(F32)
        mk, scale, offset = st.sb("mk", [P, KC, 2 * MH * NK]), st.sb("scale", [P, KC]), st.sb("offset", [P, KC])
        gamma, beta = st.sb("gamma", [P, KC]), st.sb("beta", [P, KC])
        bmv, bve, bsd = st.sb("bmv", [P, KC, 2]), st.sb("bve", [P, KC]), st.sb("bsd", [P, KC])
        wq = g[:, 0, :, :].rearrange("p (a b) n -> p a (b n)", b=2)
        keys = sims
        iota_in = sem("mt_iota_in")
        mk_in, k_mm, k_out = sem("mt_mk_in"), sem("mt_k_mm"), sem("mt_k_out")
        own_m, b_var, b_sd, normal = sem("mt_own_norm"), sem("mt_b_var"), sem("mt_b_sd"), sem("mt_normal")

        w_in, ready, xl_in, xr_in = sem("mt_w"), sem("mt_ready"), [sem("mt_xl0"), sem("mt_xl1")], [sem("mt_xr0"), sem("mt_xr1")]
        xb_ready, sim_mm, sim_out, picked = sem("mt_xb"), sem("mt_sim_mm"), sem("mt_sim_out"), sem("mt_picked")
        diff_ready, weighed, sel_ready = sem("mt_diff"), sem("mt_weighed"), sem("mt_sel")
        turned, turned_out, hot = sem("mt_turned"), sem("mt_turned_out"), sem("mt_hot")
        c_mm, w_out, d_mm, g_out = sem("mt_c_mm"), sem("mt_w_out"), sem("mt_d_mm"), sem("mt_g_out")
        u_mm, final, o_stored = sem("mt_u_mm"), sem("mt_final"), [sem("mt_o0"), sem("mt_o1")]
        own_s, own_h = sem("mt_own_select"), sem("mt_own_hot")
        NSEL, NHOT = 16, 2

        def steps(eng, first, step):
            first()
            with eng.Fori(0, NT // 2 - 1) as i:
                for off in range(2):
                    step(i, off, 2)
            for off in range(2):
                step(NT // 2 - 1, off, 1 - off)

        with nc.Block() as block:
            @block.sync
            def _(sp):
                for dst, name in ((keys[:, :, :], "m_keys"), (wq, "m_wq"), (gamma[:, :], "m_gamma"), (beta[:, :], "m_beta")):
                    sp.dma_start(dst, t[name + "_in"]).then_inc(mk_in, 16)
                for dst, name in ((iota_f, "m_iota"), (iota8, "m_iota8")):
                    sp.dma_start(dst.ap(), t[name + "_in"]).then_inc(iota_in, 16)
                for s in range(2):
                    sp.wait_ge(xl_in[s], 16)
                for dst, name in ((key_in, "m_in"), (key_out, "m_out")):
                    sp.dma_start(dst.ap(), t[name + "_in"]).then_inc(w_in, 16)

                for s in range(2):
                    sp.sem_inc(o_stored[s], 1)

                def load(i, off):
                    n = 2 * i + off
                    sp.dma_start(xr[:, off % 2, :], t["x_dram"][n]).then_inc(xr_in[off % 2], 16)

                def first():
                    load(0, 0)
                    load(0, 1)

                def step(i, off, ahead):
                    n = 2 * i + off
                    sp.wait_ge(final, n + 2)
                    sp.dma_start(t["out_tiles"][n], o[:, off, :]).then_inc(o_stored[off], 16)
                    if ahead == 2:
                        load(i, off + 2)

                steps(sp, first, step)
                for s in range(2):
                    sp.wait_ge(o_stored[s], 16 * (NT // 2) + 1)

            @block.gpsimd
            def _(pool):
                def token_rows(i, off):
                    n, s = 2 * i + off, off % 2
                    if off > 1:
                        pool.wait_ge(d_mm, (n - 1) * ND)
                        gate(pool, t["pool_gate"])
                    pool.dma_start(xl[:, s, :, :], t["xT_dram"][n]).then_inc(xl_in[s], 16)
                    if off > 1:
                        pool.wait_ge(sim_mm, (n - 1) * 2)
                    elif off == 0:
                        pool.wait_ge(normal, 1)
                    pool.wait_ge(xl_in[s], 16 * (i + off // 2) + 16)
                    gate(pool, t["pool_gate"])
                    for k in range(KC):
                        ins = nc.gpsimd.tensor_scalar(xb[:, s, k, :], xl[:, s, k, :], scale[:, k:k + 1], offset[:, k:k + 1],
                                                      ALU.mult, ALU.add)
                    ins.then_inc(xb_ready, 1)

                token_rows(0, 0)
                token_rows(0, 1)
                with pool.Fori(0, NT // 2 - 1) as i:
                    for off in range(2):
                        token_rows(i, off + 2)

            @block.tensor
            def _(pe):
                pe.sem_inc(u_mm, 1)
                pe.wait_ge(ready, 1)

                def half_scores(i, off, c):
                    n = 2 * i + off
                    if c == 0:
                        pe.wait_ge(xb_ready, n + 1)
                        if off > 1:
                            pe.wait_ge(turned_out, n - 1)
                    if off or c:
                        pe.wait_ge(sim_out, 2 * n + c)
                    for k in range(KC):
                        ins = nc.tensor.matmul(ps_sim, xb[:, off % 2, k, :], mk[:, k, c * 512:c * 512 + 512],
                                               start=k == 0, stop=k == KC - 1)
                    ins.then_inc(sim_mm, 1)

                def turn_picks(i, off, ahead):
                    n = 2 * i + off
                    pe.wait_ge(sel_ready, n + 1)
                    pe.wait_ge(sim_out, 2 * (n + 1 + ahead))
                    gate(pe, t["pe_gate"])
                    for h in range(2):
                        rows = slice(h * HT, h * HT + HT)
                        for v in range(QN):
                            ins = nc.tensor.transpose(ps_x[rows, v * HT:v * HT + HT], picks[rows, off % 2, v, :],
                                                      identb[rows, rows])
                    ins.then_inc(turned, 1)

                def dense_in(i, off):
                    n, s = 2 * i + off, off % 2
                    pe.wait_ge(xl_in[s], 16 * (i + off // 2) + 16)
                    for j in range(ND):
                        pe.wait_ge(g_out, n * ND + j + 1)
                        for y in range(YB):
                            for k in range(KC):
                                ins = nc.tensor.matmul(ps_d[:, j % 2, y * P:y * P + P], key_in[:, k, j * YB + y, :],
                                                       xl[:, s, k, :], start=k == 0, stop=k == KC - 1)
                        ins.then_inc(d_mm, 1)

                def scatter(i, off, part):
                    n = 2 * i + off
                    if part == 0:
                        pe.wait_ge(hot, n + 1)
                    for tb in range(2 * part, 2 * part + 2):
                        pe.wait_ge(w_out, n * NB + 2 * tb + 2)
                        for tok in range(TB):
                            for v in range(WP):
                                for h in range(2):
                                    rows = slice(h * HT, h * HT + HT)
                                    ins = nc.tensor.matmul(ps_c[:, h, tb % 2, tok * YH:(tok + 1) * YH],
                                                           hot_m[rows, off % 2, :, tb * TB + tok],
                                                           hot_w[rows, off % 2, v, :, tb * TB + tok],
                                                           start=v == 0, stop=v == WP - 1)
                                    if tok == TB - 1 and v == WP - 1:
                                        ins.then_inc(c_mm, 1)

                def dense_out(i, off):
                    n = 2 * i + off
                    pe.wait_ge(w_out, (n + 1) * NB + 4)
                    pe.wait_ge(final, n + 1)
                    for y in range(YH):
                        ins = nc.tensor.matmul(ps_u[:, 0:D], g[:, off % 2, y, :], key_out[:, y, :],
                                               start=y == 0, stop=y == YH - 1)
                    ins.then_inc(u_mm, 1)

                def first():
                    pe.wait_ge(mk_in, 64)
                    for n, (m, c) in enumerate(HALVES):
                        if n > 1:
                            pe.wait_ge(k_out, n - 1)
                        for h in range(MH):
                            ins = nc.tensor.matmul(ps_d[:, n % 2, h * NK:(h + 1) * NK], wq[:, c * MH + h, m * P:m * P + P],
                                                   keys[:, c * MH + h, :], start=True, stop=True)
                        ins.then_inc(k_mm, 1)
                    pe.wait_ge(k_out, len(HALVES))
                    for off in range(2):
                        for c in range(2):
                            half_scores(0, off, c)
                    turn_picks(0, 0, 1)
                    pe.wait_ge(w_in, 32)
                    dense_in(0, 0)

                def step(i, off, ahead):
                    for c in range(2):
                        if ahead == 2:
                            half_scores(i, off + 2, c)
                        scatter(i, off, c)
                    if ahead:
                        turn_picks(i, off + 1, min(ahead - 1, 1))
                        dense_in(i, off + 1)
                    dense_out(i, off)

                steps(pe, first, step)

            @block.scalar
            def _(act):
                act.sem_inc(g_out, 2)

                def scores_out(i, off):
                    n = 2 * i + off
                    for c in range(2):
                        act.wait_ge(sim_mm, 2 * n + c + 1)
                        if off:
                            act.wait_ge(picked, n)
                        nc.scalar.activation(sims[:, c * MH:(c + 1) * MH, :].rearrange("p h k -> p (h k)"), ps_sim,
                                             ACT.Copy).then_inc(sim_out, 1)

                def exps(i, off):
                    act.wait_ge(diff_ready, 2 * i + off + 1)
                    nc.scalar.activation(ew[:, :, :], diff[:, :, :], ACT.Exp).then_inc(weighed, 1)

                def gelus(i, off):
                    n = 2 * i + off
                    if off:
                        act.wait_ge(u_mm, n)
                    for j in range(ND):
                        act.wait_ge(d_mm, n * ND + j + 1)
                        nc.scalar.activation(g[:, off % 2, j * YB:(j + 1) * YB, :],
                                             ps_d[:, j % 2, :].rearrange("p (y n) -> p y n", n=P), ACT.Gelu).then_inc(g_out, 1)

                def first():
                    act.wait_ge(b_var, 1)
                    nc.scalar.activation(bsd[:, :], bve[:, :], ACT.Sqrt).then_inc(b_sd, 1)
                    for n, (m, c) in enumerate(HALVES):
                        act.wait_ge(k_mm, n + 1)
                        nc.scalar.activation(mk[:, m, c * 512:c * 512 + 512], ps_d[:, n % 2, :], ACT.Copy).then_inc(k_out, 1)
                    scores_out(0, 0)
                    exps(0, 0)
                    scores_out(0, 1)
                    gelus(0, 0)
                    exps(0, 1)

                def step(i, off, ahead):
                    if ahead == 2:
                        scores_out(i, off + 2)
                    if ahead:
                        gelus(i, off + 1)
                    if ahead == 2:
                        exps(i, off + 2)

                steps(act, first, step)

            @block.vector
            def _(dve):
                dve.sem_inc(w_out, 4)
                dve.sem_inc(final, 1)
                me = Own(dve, own_m)
                for k in range(KC):
                    ins = nc.vector.bn_aggr(bmv[:, k, :], t["bstats"][:, k, :, :].rearrange("p b c -> p (b c)"))
                me.then(ins)
                nc.vector.tensor_scalar(bve[:, :], bmv[:, :, 1], LN_EPS, None, ALU.add).then_inc(b_var, 1)
                dve.wait_ge(b_sd, 1)
                dve.wait_ge(mk_in, 64)
                me.then(nc.vector.reciprocal(bsd[:, :], bsd[:, :]))
                me.then(nc.vector.tensor_tensor(scale[:, :], bsd[:, :], gamma[:, :], ALU.mult))
                me.then(nc.vector.tensor_tensor(offset[:, :], bmv[:, :, 0], scale[:, :], ALU.mult))
                nc.vector.tensor_tensor(offset[:, :], beta[:, :], offset[:, :], ALU.subtract).then_inc(normal, 1)
                dve.wait_ge(iota_in, 32)
                nc.vector.tensor_copy(identb[:, :], t["ident"][:, :])
                nc.vector.tensor_scalar(gate_down[:, :], t["gate_f"](1), 1.0 / UP, None, ALU.mult)
                nc.vector.tensor_copy(iota_m[:, :, :], iota_f[:, :].unsqueeze(2).broadcast_to([P, P, TB])).then_inc(ready, 1)
                dve.wait_ge(ready, 1)

                def select(i, off):
                    n, s = 2 * i + off, off % 2
                    me = Own(dve, own_s, n, NSEL)
                    dve.wait_ge(sim_out, 2 * n + 2)
                    gate(dve, t["dve_gate"])
                    for h in range(2 * MH):
                        ins = nc.vector.max(s8[:, h, :], sims[:, h, :])
                    me.then(ins)
                    gate(dve, t["dve_gate"])
                    for h in range(2 * MH):
                        ins = nc.vector.max_index(i8[:, h, :], s8[:, h, :], sims[:, h, :])
                    ins.then_inc(picked, 1)
                    dve.wait_ge(picked, n + 1)
                    nc.vector.tensor_copy(i8f[:, :, :], i8[:, :, :])
                    me.then(nc.vector.tensor_tensor(pairs[:, :, :, :],
                                                    s8[:, 0:MH, :].unsqueeze(3).broadcast_to([P, MH, TOP, TOP]),
                                                    s8[:, MH:, :].unsqueeze(2).broadcast_to([P, MH, TOP, TOP]), ALU.add))
                    gate(dve, t["dve_gate"])
                    for h in range(MH):
                        ins = nc.vector.max(best[:, h, :], pairs[:, h, :, :].rearrange("p a b -> p (a b)"))
                    me.then(ins)
                    nc.vector.tensor_tensor(diff[:, :, :], best[:, :, :], best[:, :, 0:1].broadcast_to([P, MH, TOP]),
                                            ALU.subtract).then_inc(diff_ready, 1)
                    for h in range(MH):
                        ins = nc.vector.max_index(rank[:, h, :], best[:, h, :], pairs[:, h, :, :].rearrange("p a b -> p (a b)"))
                    me.then(ins)
                    flat = rank[:, :, :].rearrange("p h k -> p (h k)")
                    nc.vector.tensor_scalar(ab[:, 0, :], flat, 3, None, ALU.logical_shift_right)
                    me.then(nc.vector.tensor_scalar(ab[:, 1, :], flat, TOP - 1, None, ALU.bitwise_and))
                    me.then(nc.vector.tensor_copy(abf[:, :, :], ab[:, :, :]))
                    me.then(nc.vector.tensor_tensor(match[:, :, :, :].rearrange("p h k a -> p (h k) a"),
                                                    abf[:, :, :].rearrange("p c n -> p (c n)").unsqueeze(2).broadcast_to([P, 2 * SEL, TOP]),
                                                    iota8[:, :].unsqueeze(1).broadcast_to([P, 2 * SEL, TOP]), ALU.is_equal))
                    me.then(nc.vector.tensor_tensor(match[:, :, :, :], match[:, :, :, :],
                                                    i8f[:, :, :].unsqueeze(2).broadcast_to([P, 2 * MH, TOP, TOP]), ALU.mult))
                    me.then(nc.vector.tensor_reduce(xy[:, :, :], match[:, :, :, :].rearrange("p (c h) k a -> p c (h k) a", c=2),
                                                    AX.X, ALU.add))
                    me.then(nc.vector.tensor_scalar(ge[:, :], xy[:, 1, :], float(YH), None, ALU.is_ge))
                    nc.vector.scalar_tensor_tensor(picks[:, s, 0, :], ge[:, :], float(NK), xy[:, 0, :], ALU.mult, ALU.add)
                    nc.vector.scalar_tensor_tensor(picks[:, s, 1, :], ge[:, :], -float(YH), xy[:, 1, :], ALU.mult, ALU.add)
                    dve.wait_ge(weighed, n + 1)
                    me.then(nc.vector.tensor_reduce(den[:, 0, :], ew[:, :, :], AX.X, ALU.add))
                    me.then(nc.vector.reciprocal(den[:, 1, :], den[:, 0, :]))
                    me.then(nc.vector.scalar_tensor_tensor(w[:, :, :], ew[:, :, :], UP,
                                                           den[:, 1, :].unsqueeze(2).broadcast_to([P, MH, TOP]),
                                                           ALU.mult, ALU.mult))
                    wf = w[:, :, :].rearrange("p h k -> p (h k)")
                    me.then(nc.vector.tensor_copy(picks[:, s, 2, :], wf))
                    me.then(nc.vector.tensor_tensor(wr[:, :], wf, picks[:, s, 2, :], ALU.subtract))
                    me.then(nc.vector.tensor_copy(picks[:, s, 3, :], wr[:, :]))
                    dve.sem_inc(sel_ready, 1)
                    assert me.n == NSEL, me.n

                def one_hots(i, off):
                    n, s = 2 * i + off, off % 2
                    me = Own(dve, own_h, n, NHOT)
                    dve.wait_ge(turned, n + 1)
                    nc.vector.tensor_copy(picksT[:, :, :].rearrange("p v n -> p (v n)"), ps_x[:, 0:QN * HT]).then_inc(turned_out, 1)
                    dve.wait_ge(turned_out, n + 1)

                    def is_at(dst, rows, v):
                        return nc.vector.tensor_tensor(
                            dst.rearrange("p m (b n) -> p m b n", n=TB),
                            iota_m[:, 0:rows, :].unsqueeze(2).broadcast_to([P, rows, HT // TB, TB]),
                            picksT[:, v, :].rearrange("p (b n) -> p b n", n=TB).unsqueeze(1).broadcast_to([P, rows, HT // TB, TB]),
                            ALU.is_equal)

                    me.then(is_at(hot_y[:, :, :], YH, 1))
                    is_at(hot_m[:, s, :, :], P, 0)
                    me.then(nc.vector.tensor_tensor(hot_w[:, s, :, :, :], hot_y[:, :, :].unsqueeze(1).broadcast_to([P, WP, YH, HT]),
                                                    picksT[:, 2:QN, :].unsqueeze(2).broadcast_to([P, WP, YH, HT]), ALU.mult))
                    dve.sem_inc(hot, 1)
                    assert me.n == NHOT, me.n

                def weigh(i, off):
                    n = 2 * i + off
                    dve.wait_ge(g_out, (n + 1) * ND + 2)
                    for tb in range(HT // TB):
                        for h in range(2):
                            dve.wait_ge(c_mm, n * NB + 2 * tb + h + 1)
                            a = h * HT + tb * TB
                            gv = g[:, off % 2, :, a:a + TB].rearrange("p y n -> p n y")
                            nc.vector.tensor_tensor(gv, ps_c[:, h, tb % 2, :].rearrange("p (n y) -> p n y", y=YH), gv,
                                                    ALU.mult).then_inc(w_out, 1)

                def finish(i, off):
                    n = 2 * i + off
                    dve.wait_ge(u_mm, n + 2)
                    dve.wait_ge(xr_in[off], 16 * i + 16)
                    dve.wait_ge(o_stored[off], 16 * i + 1)
                    nc.vector.scalar_tensor_tensor(o[:, off, :], ps_u[:, 0:D], gate_down[:, :], xr[:, off, :],
                                                   ALU.mult, ALU.add).then_inc(final, 1)

                def first():
                    select(0, 0)
                    one_hots(0, 0)
                    select(0, 1)

                def step(i, off, ahead):
                    weigh(i, off)
                    if ahead:
                        one_hots(i, off + 1)
                    if ahead == 2:
                        select(i, off + 2)
                    finish(i, off)

                steps(dve, first, step)


def build(nc, ins, out, debug=None):
    with ExitStack() as ctx:
        def sem(name):
            return ctx.enter_context(nc.semaphore(name))

        bstats = ctx.enter_context(nc.sbuf_tensor("bstats_sb", [P, KC, B, 6], F32))
        x_life = ctx.enter_context(ExitStack())
        ident = ctx.enter_context(nc.sbuf_tensor("ident_sb", [P, P], F32))
        gates = ctx.enter_context(nc.sbuf_tensor("gates_sb", [P, 4], F32))
        opened = ctx.enter_context(nc.sbuf_tensor("opened_sb", [P, 4], F32))
        x = x_life.enter_context(nc.sbuf_tensor("x_rows", [P, NT, D], F32))
        slots = x_life.enter_context(nc.sbuf_tensor("slots_sb", [P, NT], U32))
        xs_dram = nc.dram_tensor("xs_dram", (E, REGION, D), F32, kind="Internal").ap()
        ys_dram = nc.dram_tensor("ys_dram", (MAX_BLOCKS, TOK, D), F32, kind="Internal").ap()
        t = {
            "x": x[:, :, :], "x_in": ins["x"].rearrange("b (q p) d -> p (b q) d", p=P),
            "x_tile": lambda n: x[:, bass.ds(n, 1), :].rearrange("p a d -> p (a d)"),
            "ident": ident, "release_x": x_life.close, "bstats": bstats,
            "x_dram": nc.dram_tensor("x_dram", (NT, P, D), F32, kind="Internal").ap(),
            "xT_dram": nc.dram_tensor("xT_dram", (NT, P, KC, P), F32, kind="Internal").ap(),
            "out_tiles": out.rearrange("b (q p) d -> (b q) p d", p=P),
            "gate_x": lambda layer: opened[:, layer:layer + 1],
            "gate_f": lambda layer: opened[:, 2 + layer:3 + layer],
            "ctx_in": ins["ctx"],
            "ctxT_in": ins["ctxT"].rearrange("b (k p) n -> b p k n", p=P),
            "consts": sem("consts"), "consts_n": 32,
            "dve_gate": sem("dve_gate"), "pool_gate": sem("pool_gate"),
            "pe_gate": sem("pe_gate"), "act_gate": sem("act_gate"),
            "k_dram": nc.dram_tensor("k_dram", (B, 3, D, KEYS), BF16, kind="Internal").ap(),
            "q_dram": nc.dram_tensor("q_dram", (B, 3, D, S), BF16, kind="Internal").ap(),
            "v_dram": nc.dram_tensor("v_dram", (B, G, P, KT * HG * DH), F32, kind="Internal").ap(),
            "xs_dram": xs_dram, "xs_rows": xs_dram.rearrange("e n d -> (e n) d"), "slots": slots,
            "ys_dram": ys_dram, "ys_rows": ys_dram.rearrange("e n d -> (e n) d"),
            "o_dram": nc.dram_tensor("o_dram", (B, D, S), F32, kind="Internal").ap(),
        }
        for n in ("wq", "wk", "wv", "wo", "wr", "l1_q", "l1_k", "l1_v", "l1_oT"):
            t[n + "_in"] = ins[n].rearrange("(k p) n -> p k n", p=P)
        for n in ("bo", "br", "iota_e", "base0", "before", "b1", "b2") + tuple(f"l1_{a}{b}" for a in "qkv" for b in ("a", "bT")):
            t[n + "_in"] = ins[n]
        for n in ("m_wq", "m_keys", "m_gamma", "m_beta", "m_iota", "m_out", "m_iota8"):
            t[n + "_in"] = ins[n]
        t["m_in_in"] = ins["m_in"].rearrange("(k p) y m -> p k y m", p=P)
        t["w1_in"] = ins["w1"].rearrange("e (k p) f -> p e k f", p=P)
        t["w2_in"] = ins["w2"].rearrange("e (c p) d -> p e c d", p=P)
        gates_opened = sem("gates_opened")
        with nc.Block() as block:
            @block.sync
            def _(sp):
                sp.dma_start(ident[:, :], ins["ident"]).then_inc(t["consts"], 16)
                sp.dma_start(gates[:, :], ins["gates"]).then_inc(t["consts"], 16)

            @block.scalar
            def _(act):
                act.wait_ge(t["consts"], 32)
                nc.scalar.activation(opened[:, :], gates[:, :], ACT.Tanh).then_inc(gates_opened, 1)
        project(nc, sem, t)
        attend_heads(nc, sem, t)
        experts(nc, sem, t)
        attend_wide(nc, sem, t)
        if debug is None or debug > 3:
            t["release_x"]()
            memory(nc, sem, t, out)
            return
        written = sem("written")
        with nc.Block() as block:
            @block.sync
            def _(sp):
                sp.dma_start(out.rearrange("b (q p) d -> p (b q) d", p=P), x[:, :, :]).then_inc(written, 16)
                sp.wait_ge(written, 16)
        t["release_x"]()


def laid_out(inputs):
    import numpy as np
    c = np.ascontiguousarray
    a = {k: np.asarray(v) for k, v in inputs.items()}

    def rows(v):
        return c(np.broadcast_to(v.reshape(1, -1), (P, v.size)))

    r = {
        "x": a["x"],
        "ctx": a["ctx_1024"],
        "ctxT": c(a["ctx_1024"].transpose(0, 2, 1)),
        "wq": c(a["L0_xattn_Wq"].T), "wk": c(a["L0_xattn_Wk"].T), "wv": c(a["L0_xattn_Wv"].T),
        "wo": c(a["L0_xattn_Wo"].T), "bo": c(a["L0_xattn_bo"].reshape(1, D)),
        "wr": a["L0_ffn_Wr"], "br": rows(a["L0_ffn_br"]),
        "w1": a["L0_ffn_We1"], "b1": c(a["L0_ffn_be1"].reshape(E * FC, P).T),
        "w2": a["L0_ffn_We2"], "b2": rows(a["L0_ffn_be2"]).reshape(P, E, D),
        "l1_q": a["L1_xattn_Q_weight"], "l1_k": a["L1_xattn_K_weight"], "l1_v": a["L1_xattn_V_weight"],
        "l1_oT": c(a["L1_xattn_O_weight"].T),
        "gates": rows(np.concatenate([a["g_xattn"], a["g_ffn"]])),
        "ident": np.eye(P, dtype=np.float32),
        "base0": c(np.broadcast_to(np.arange(E, dtype=np.float32) * REGION, (P, E))),
        "before": np.triu(np.ones((P, P), np.float32), 1),
        "iota_e": c(np.broadcast_to(np.arange(E, dtype=np.float32), (P, E))),
    }
    r |= {
        "m_wq": c(a["L1_ffn_w_q"].reshape(2 * MH, KD, D).transpose(1, 0, 2)),
        "m_keys": c(a["L1_ffn_keys"].transpose(3, 2, 0, 1).reshape(KD, 2 * MH, NK)),
        "m_gamma": c(a["L1_ffn_gamma"].reshape(KC, P).T), "m_beta": c(a["L1_ffn_beta"].reshape(KC, P).T),
        "m_in": c(a["L1_ffn_key_in"].reshape(NK, 2, YH, D).transpose(3, 2, 1, 0).reshape(D, YH, P)),
        "m_out": c(a["L1_ffn_key_out"].reshape(NK, 2, YH, D).transpose(1, 0, 2, 3).reshape(P, YH, D)),
        "m_iota": c(np.broadcast_to(np.arange(P, dtype=np.float32), (P, P))),
        "m_iota8": c(np.broadcast_to(np.arange(TOP, dtype=np.float32), (P, TOP))),
    }
    for n in "qkv":
        r[f"l1_{n}a"] = a[f"L1_xattn_{n.upper()}_A"]
        r[f"l1_{n}bT"] = c(a[f"L1_xattn_{n.upper()}_B"].T)
    return r


def kernel(**inputs):
    import concourse.bacc as bacc
    import numpy as np
    from concourse.bass_utils import run_bass_kernel_spmd

    nc = bacc.Bacc("TRN2", target_bir_lowering=False, num_devices=1)
    arrays = laid_out(inputs)
    ins = {n: nc.dram_tensor(n, a.shape, mybir.dt.from_np(a.dtype), kind="ExternalInput").ap() for n, a in arrays.items()}
    out = nc.dram_tensor("out", (B, S, D), F32, kind="ExternalOutput").ap()
    build(nc, ins, out)
    r = run_bass_kernel_spmd(nc, [arrays], core_ids=[0])
    return np.asarray(r.results[0]["out"])
```
